# Optimizing a Trainium2 kernel written in Bass

```python
import numpy as np
import jax
import jax.numpy as jnp

def _softmax(x, axis=-1):
    return jax.nn.softmax(x, axis=axis)

def _gelu(x):
    return jax.nn.gelu(x, approximate=True)

def _silu(x):
    return jax.nn.silu(x)

def _sigmoid(x):
    return jax.nn.sigmoid(x)

def _layernorm(x, axis=-1, eps=1e-05):
    m = jnp.mean(x, axis=axis, keepdims=True)
    v = jnp.var(x, axis=axis, keepdims=True)
    return (x - m) / jnp.sqrt(v + eps)

def _scatter_add(tgt, idx, src, axis=0):
    return tgt.at[idx].add(src)

def _segment_sum(src, seg, n):
    return jax.ops.segment_sum(src, seg, n)
kernel_name = 'mk_conv_attn_hybrid_d2_conv_nchw256_r2_80fec1'

def setup_inputs(seed: int=0):
    np.random.seed(seed)
    _w = jnp.asarray

    def _rec_inputs():
        import jax
        import jax.numpy as jnp
        _gk = jax.random.key(seed)
        x = 7.22e-05 + 1 * jax.random.normal(jax.random.fold_in(_gk, 1), (8, 128, 32, 32), jnp.float32)
        return x
    x = _rec_inputs()

    def _L0_conv_setup():
        import jax, jax.numpy as jnp
        import numpy as np
        DIM = 128
        DSTATE = 32
        DCONV = 3
        HEADDIM = 32
        CHUNK = 128
        NGROUPS = 1
        DINNER = int(2.0 * DIM)
        NHEADS = DINNER // HEADDIM
        CONVDIM = DINNER + 2 * NGROUPS * DSTATE
        DPROJ = 2 * DINNER + 2 * NGROUPS * DSTATE + NHEADS

        def _ssd(X, dA, Bm, Cm, chunk):
            b, l, h, p = X.shape
            n = Bm.shape[-1]
            c = l // chunk
            q = chunk
            Xc = X.reshape(b, c, q, h, p)
            Bc = Bm.reshape(b, c, q, h, n)
            Cc = Cm.reshape(b, c, q, h, n)
            Ac = dA.reshape(b, c, q, h).transpose(0, 3, 1, 2)
            Acs = jnp.cumsum(Ac, axis=-1)
            tri = jnp.tril(jnp.ones((q, q), bool))
            Ldec = jnp.where(tri, jnp.exp(Acs[..., :, None] - Acs[..., None, :]), 0.0)
            Y_diag = jnp.einsum('bcqhn,bcshn,bhcqs,bcshp->bcqhp', Cc, Bc, Ldec, Xc)
            decay_states = jnp.exp(Acs[..., -1:] - Acs)
            states = jnp.einsum('bcqhn,bhcq,bcqhp->bchpn', Bc, decay_states, Xc)
            A_last = jnp.pad(Acs[..., -1], ((0, 0), (0, 0), (1, 0)))
            ccs = jnp.cumsum(A_last, axis=-1)
            tric = jnp.tril(jnp.ones((c + 1, c + 1), bool))
            decay_chunk = jnp.where(tric, jnp.exp(ccs[..., :, None] - ccs[..., None, :]), 0.0)
            states0 = jnp.concatenate([jnp.zeros_like(states[:, :1]), states], axis=1)
            prev = jnp.einsum('bhzc,bchpn->bzhpn', decay_chunk, states0)[:, :-1]
            Y_off = jnp.einsum('bcqhn,bchpn,bhcq->bcqhp', Cc, prev, jnp.exp(Acs))
            return (Y_diag + Y_off).reshape(b, l, h, p)

        def _forward(x, ln_w, ln_b, in_proj_w, conv_w, conv_b, A_log, D, dt_bias, rms_w, out_proj_w):
            Bn, Cd, Hh, Ww = x.shape
            L = Hh * Ww
            mu = jnp.mean(x, axis=1, keepdims=True)
            var = jnp.mean((x - mu) ** 2, axis=1, keepdims=True)
            xn = (x - mu) * jax.lax.rsqrt(var + 1e-05)
            xn = xn * ln_w[None, :, None, None] + ln_b[None, :, None, None]
            zxbcdt = jnp.einsum('bchw,dc->bdhw', xn, in_proj_w)
            z = zxbcdt[:, :DINNER]
            xBC = zxbcdt[:, DINNER:DINNER + CONVDIM]
            dt = zxbcdt[:, DINNER + CONVDIM:]
            xBC = jax.lax.conv_general_dilated(xBC, conv_w, (1, 1), 'SAME', dimension_numbers=('NCHW', 'OIHW', 'NCHW'), feature_group_count=CONVDIM)
            xBC = jax.nn.silu(xBC + conv_b[None, :, None, None])

            def to_seq(t):
                return t.reshape(Bn, t.shape[1], L).transpose(0, 2, 1)
            xBC, dt, z = (to_seq(xBC), to_seq(dt), to_seq(z))
            xs = xBC[..., :DINNER].reshape(Bn, L, NHEADS, HEADDIM)
            Bg = xBC[..., DINNER:DINNER + NGROUPS * DSTATE].reshape(Bn, L, NGROUPS, DSTATE)
            Cg = xBC[..., DINNER + NGROUPS * DSTATE:].reshape(Bn, L, NGROUPS, DSTATE)
            hpg = NHEADS // NGROUPS
            Bm = jnp.repeat(Bg, hpg, axis=2)
            Cm = jnp.repeat(Cg, hpg, axis=2)
            dt = jax.nn.softplus(dt + dt_bias[None, None, :])
            A = -jnp.exp(A_log)
            y = _ssd(xs * dt[..., None], dt * A[None, None, :], Bm, Cm, CHUNK)
            y = y + D[None, None, :, None] * xs
            y = y.reshape(Bn, L, DINNER)
            y = y * jax.nn.silu(z)
            y = y * jax.lax.rsqrt(jnp.mean(y * y, axis=-1, keepdims=True) + 1e-05) * rms_w
            out = jnp.einsum('bld,cd->blc', y, out_proj_w)
            out = out.transpose(0, 2, 1).reshape(Bn, Cd, Hh, Ww)
            return x + out
        key = jax.random.key(seed)
        ks = jax.random.split(key, 8)
        B, H, W = (8, 32, 32)
        return dict(x=jax.random.normal(ks[0], (B, DIM, H, W), jnp.float32), ln_w=jnp.ones((DIM,), jnp.float32), ln_b=jnp.zeros((DIM,), jnp.float32), in_proj_w=jax.random.normal(ks[1], (DPROJ, DIM), jnp.float32) * 0.02, conv_w=jax.random.normal(ks[2], (CONVDIM, 1, DCONV, DCONV), jnp.float32) * 0.1, conv_b=jnp.zeros((CONVDIM,), jnp.float32), A_log=jnp.log(jax.random.uniform(ks[3], (NHEADS,), jnp.float32, 1.0, 16.0)), D=jnp.ones((NHEADS,), jnp.float32), dt_bias=jax.random.uniform(ks[4], (NHEADS,), jnp.float32, -2.0, 0.0), rms_w=jnp.ones((DINNER,), jnp.float32), out_proj_w=jax.random.normal(ks[5], (DIM, DINNER), jnp.float32) * 0.02)
    _L0_conv_all = _L0_conv_setup()
    _L0_conv_in = {k: v for k, v in _L0_conv_all.items() if k in ('ln_w', 'ln_b', 'in_proj_w', 'conv_w', 'conv_b', 'A_log', 'D', 'dt_bias', 'rms_w', 'out_proj_w')}
    del _L0_conv_all

    def _L1_attn_setup():
        import jax, jax.numpy as jnp
        import numpy as np
        B, T, E, H = (8, 512, 128, 8)
        key = jax.random.key(seed)
        ks = jax.random.split(key, 6)
        x = jax.random.normal(ks[0], (B, T, E), dtype=jnp.float32)
        sc = 1.0 / np.sqrt(E)
        Wk = jax.random.normal(ks[1], (E * H, E), dtype=jnp.float32) * sc
        Wq = jax.random.normal(ks[2], (E * H, E), dtype=jnp.float32) * sc
        Wv = jax.random.normal(ks[3], (E * H, E), dtype=jnp.float32) * sc
        Wu = jax.random.normal(ks[4], (E, H * E), dtype=jnp.float32) * (1.0 / np.sqrt(H * E))
        bu = jnp.zeros((E,), dtype=jnp.float32)
        return {'x': x, 'Wk': Wk, 'Wq': Wq, 'Wv': Wv, 'Wu': Wu, 'bu': bu}
    _L1_attn_all = _L1_attn_setup()
    _L1_attn_in = {k: v for k, v in _L1_attn_all.items() if k in ('Wk', 'Wq', 'Wv', 'Wu', 'bu')}
    del _L1_attn_all

    def _L1_ffn_setup():
        import jax, jax.numpy as jnp
        import numpy as np
        N_EXPERTS = 8
        TOP_K = 2
        key = jax.random.key(seed)
        ks = jax.random.split(key, 5)
        B, T, C, E, H = (8, 1024, 128, 8, 341)
        scale = 1.0 / np.sqrt(C)
        return {'x': jax.random.normal(ks[0], (B, T, C), dtype=jnp.float32), 'router_w': jax.random.normal(ks[1], (E, C), dtype=jnp.float32) * scale, 'w1': jax.random.normal(ks[2], (E, H, C), dtype=jnp.float32) * scale, 'w2': jax.random.normal(ks[3], (E, C, H), dtype=jnp.float32) * (1.0 / np.sqrt(H)), 'w3': jax.random.normal(ks[4], (E, H, C), dtype=jnp.float32) * scale}
    _L1_ffn_all = _L1_ffn_setup()
    _L1_ffn_in = {k: v for k, v in _L1_ffn_all.items() if k in ('router_w', 'w1', 'w2', 'w3')}
    del _L1_ffn_all
    return {'x': x, 'L0_conv_ln_w': _L0_conv_in['ln_w'], 'L0_conv_ln_b': _L0_conv_in['ln_b'], 'L0_conv_in_proj_w': _L0_conv_in['in_proj_w'], 'L0_conv_conv_w': _L0_conv_in['conv_w'], 'L0_conv_conv_b': _L0_conv_in['conv_b'], 'L0_conv_A_log': _L0_conv_in['A_log'], 'L0_conv_D': _L0_conv_in['D'], 'L0_conv_dt_bias': _L0_conv_in['dt_bias'], 'L0_conv_rms_w': _L0_conv_in['rms_w'], 'L0_conv_out_proj_w': _L0_conv_in['out_proj_w'], 'L1_attn_Wk': _L1_attn_in['Wk'], 'L1_attn_Wq': _L1_attn_in['Wq'], 'L1_attn_Wv': _L1_attn_in['Wv'], 'L1_attn_Wu': _L1_attn_in['Wu'], 'L1_attn_bu': _L1_attn_in['bu'], 'L1_ffn_router_w': _L1_ffn_in['router_w'], 'L1_ffn_w1': _L1_ffn_in['w1'], 'L1_ffn_w2': _L1_ffn_in['w2'], 'L1_ffn_w3': _L1_ffn_in['w3']}

def reference(x, L0_conv_ln_w, L0_conv_ln_b, L0_conv_in_proj_w, L0_conv_conv_w, L0_conv_conv_b, L0_conv_A_log, L0_conv_D, L0_conv_dt_bias, L0_conv_rms_w, L0_conv_out_proj_w, L1_attn_Wk, L1_attn_Wq, L1_attn_Wv, L1_attn_Wu, L1_attn_bu, L1_ffn_router_w, L1_ffn_w1, L1_ffn_w2, L1_ffn_w3):
    import jax
    import jax.numpy as jnp

    def _L0_conv_ref(x, ln_w, ln_b, in_proj_w, conv_w, conv_b, A_log, D, dt_bias, rms_w, out_proj_w):
        import jax, jax.numpy as jnp
        import numpy as np
        DIM = 128
        DSTATE = 32
        DCONV = 3
        HEADDIM = 32
        CHUNK = 128
        NGROUPS = 1
        DINNER = int(2.0 * DIM)
        NHEADS = DINNER // HEADDIM
        CONVDIM = DINNER + 2 * NGROUPS * DSTATE
        DPROJ = 2 * DINNER + 2 * NGROUPS * DSTATE + NHEADS

        def _ssd(X, dA, Bm, Cm, chunk):
            b, l, h, p = X.shape
            n = Bm.shape[-1]
            c = l // chunk
            q = chunk
            Xc = X.reshape(b, c, q, h, p)
            Bc = Bm.reshape(b, c, q, h, n)
            Cc = Cm.reshape(b, c, q, h, n)
            Ac = dA.reshape(b, c, q, h).transpose(0, 3, 1, 2)
            Acs = jnp.cumsum(Ac, axis=-1)
            tri = jnp.tril(jnp.ones((q, q), bool))
            Ldec = jnp.where(tri, jnp.exp(Acs[..., :, None] - Acs[..., None, :]), 0.0)
            Y_diag = jnp.einsum('bcqhn,bcshn,bhcqs,bcshp->bcqhp', Cc, Bc, Ldec, Xc)
            decay_states = jnp.exp(Acs[..., -1:] - Acs)
            states = jnp.einsum('bcqhn,bhcq,bcqhp->bchpn', Bc, decay_states, Xc)
            A_last = jnp.pad(Acs[..., -1], ((0, 0), (0, 0), (1, 0)))
            ccs = jnp.cumsum(A_last, axis=-1)
            tric = jnp.tril(jnp.ones((c + 1, c + 1), bool))
            decay_chunk = jnp.where(tric, jnp.exp(ccs[..., :, None] - ccs[..., None, :]), 0.0)
            states0 = jnp.concatenate([jnp.zeros_like(states[:, :1]), states], axis=1)
            prev = jnp.einsum('bhzc,bchpn->bzhpn', decay_chunk, states0)[:, :-1]
            Y_off = jnp.einsum('bcqhn,bchpn,bhcq->bcqhp', Cc, prev, jnp.exp(Acs))
            return (Y_diag + Y_off).reshape(b, l, h, p)

        def _forward(x, ln_w, ln_b, in_proj_w, conv_w, conv_b, A_log, D, dt_bias, rms_w, out_proj_w):
            Bn, Cd, Hh, Ww = x.shape
            L = Hh * Ww
            mu = jnp.mean(x, axis=1, keepdims=True)
            var = jnp.mean((x - mu) ** 2, axis=1, keepdims=True)
            xn = (x - mu) * jax.lax.rsqrt(var + 1e-05)
            xn = xn * ln_w[None, :, None, None] + ln_b[None, :, None, None]
            zxbcdt = jnp.einsum('bchw,dc->bdhw', xn, in_proj_w)
            z = zxbcdt[:, :DINNER]
            xBC = zxbcdt[:, DINNER:DINNER + CONVDIM]
            dt = zxbcdt[:, DINNER + CONVDIM:]
            xBC = jax.lax.conv_general_dilated(xBC, conv_w, (1, 1), 'SAME', dimension_numbers=('NCHW', 'OIHW', 'NCHW'), feature_group_count=CONVDIM)
            xBC = jax.nn.silu(xBC + conv_b[None, :, None, None])

            def to_seq(t):
                return t.reshape(Bn, t.shape[1], L).transpose(0, 2, 1)
            xBC, dt, z = (to_seq(xBC), to_seq(dt), to_seq(z))
            xs = xBC[..., :DINNER].reshape(Bn, L, NHEADS, HEADDIM)
            Bg = xBC[..., DINNER:DINNER + NGROUPS * DSTATE].reshape(Bn, L, NGROUPS, DSTATE)
            Cg = xBC[..., DINNER + NGROUPS * DSTATE:].reshape(Bn, L, NGROUPS, DSTATE)
            hpg = NHEADS // NGROUPS
            Bm = jnp.repeat(Bg, hpg, axis=2)
            Cm = jnp.repeat(Cg, hpg, axis=2)
            dt = jax.nn.softplus(dt + dt_bias[None, None, :])
            A = -jnp.exp(A_log)
            y = _ssd(xs * dt[..., None], dt * A[None, None, :], Bm, Cm, CHUNK)
            y = y + D[None, None, :, None] * xs
            y = y.reshape(Bn, L, DINNER)
            y = y * jax.nn.silu(z)
            y = y * jax.lax.rsqrt(jnp.mean(y * y, axis=-1, keepdims=True) + 1e-05) * rms_w
            out = jnp.einsum('bld,cd->blc', y, out_proj_w)
            out = out.transpose(0, 2, 1).reshape(Bn, Cd, Hh, Ww)
            return x + out
        return _forward(x, ln_w, ln_b, in_proj_w, conv_w, conv_b, A_log, D, dt_bias, rms_w, out_proj_w)

    def _L1_attn_ref(x, Wk, Wq, Wv, Wu, bu):
        import jax, jax.numpy as jnp
        import numpy as np
        B, T, E, H = (8, 512, 128, 8)
        b, t, e = x.shape
        h = Wk.shape[0] // e
        Wk3 = Wk.reshape(h, e, e)
        Wq3 = Wq.reshape(h, e, e)
        Wv3 = Wv.reshape(h, e, e)
        keys = jnp.einsum('btd,hod->bthо'.replace('о', 'o').replace('o', 'e'), x, Wk3) if False else jnp.einsum('btd,hod->bhto', x, Wk3)
        queries = jnp.einsum('btd,hod->bhto', x, Wq3)
        values = jnp.einsum('btd,hod->bhto', x, Wv3)
        dot = jnp.einsum('bhqe,bhke->bhqk', queries, keys) / jnp.sqrt(jnp.float32(e))
        causal = jnp.tril(jnp.ones((t, t), dtype=bool))
        dot = jnp.where(causal, dot, jnp.float32(-jnp.inf))
        attn = jax.nn.softmax(dot, axis=-1)
        out = jnp.einsum('bhqk,bhke->bqhe', attn, values).reshape(b, t, h * e)
        return out @ Wu.T + bu

    def _L1_ffn_ref(x, router_w, w1, w2, w3):
        import jax, jax.numpy as jnp
        import numpy as np
        N_EXPERTS = 8
        TOP_K = 2
        B, T, C = x.shape
        flat = x.reshape(-1, C)
        logits = flat @ router_w.T
        probs = jax.nn.softmax(logits, axis=-1)
        topk_probs, topk_idx = jax.lax.top_k(probs, TOP_K)
        topk_probs = topk_probs / (jnp.sum(topk_probs, axis=-1, keepdims=True) + 1e-09)
        onehot = jax.nn.one_hot(topk_idx, N_EXPERTS, dtype=flat.dtype)
        gates = jnp.einsum('nk,nke->ne', topk_probs, onehot)
        h1 = jnp.einsum('nc,ehc->neh', flat, w1)
        h3 = jnp.einsum('nc,ehc->neh', flat, w3)
        h = jax.nn.silu(h1) * h3
        y = jnp.einsum('neh,ech->nec', h, w2)
        out = jnp.einsum('ne,nec->nc', gates, y)
        return out.reshape(B, T, C)

    def _gn(v, G=32, eps=1e-05):
        B_, C_, H_, W_ = v.shape
        g = v.reshape(B_, G, C_ // G, H_, W_)
        m = jnp.mean(g, axis=(2, 3, 4), keepdims=True)
        s = jnp.var(g, axis=(2, 3, 4), keepdims=True)
        return ((g - m) / jnp.sqrt(s + eps)).reshape(v.shape)

    def _ln_c(v, eps=1e-06):
        m = jnp.mean(v, axis=1, keepdims=True)
        s = jnp.var(v, axis=1, keepdims=True)
        return (v - m) / jnp.sqrt(s + eps)

    def _ln_t(v, eps=1e-05):
        m = jnp.mean(v, axis=-1, keepdims=True)
        s = jnp.var(v, axis=-1, keepdims=True)
        return (v - m) / jnp.sqrt(s + eps)

    def _to_tokens(v):
        B_, C_, H_, W_ = v.shape
        return v.reshape(B_, C_, H_ * W_).transpose(0, 2, 1)

    def _from_tokens(t, like):
        B_, C_, H_, W_ = like.shape
        return t.transpose(0, 2, 1).reshape(B_, C_, H_, W_)
    x = _L0_conv_ref(x, L0_conv_ln_w, L0_conv_ln_b, L0_conv_in_proj_w, L0_conv_conv_w, L0_conv_conv_b, L0_conv_A_log, L0_conv_D, L0_conv_dt_bias, L0_conv_rms_w, L0_conv_out_proj_w)
    t = _to_tokens(x)
    t = t + _L1_attn_ref(_ln_t(t), L1_attn_Wk, L1_attn_Wq, L1_attn_Wv, L1_attn_Wu, L1_attn_bu)
    t = t + _L1_ffn_ref(_ln_t(t), L1_ffn_router_w, L1_ffn_w1, L1_ffn_w2, L1_ffn_w3)
    x = _from_tokens(t, x)
    return x

_drawn_inputs = setup_inputs


def setup_inputs(seed=0):
    import zlib

    import numpy as np

    out = dict(_drawn_inputs(seed))
    spreads = {'L0_conv_ln_w': (1.0, 0.2),
     'L0_conv_ln_b': (0.0, 0.1),
     'L0_conv_conv_b': (0.0, 0.1),
     'L0_conv_D': (1.0, 0.2),
     'L0_conv_rms_w': (1.0, 0.2),
     'L1_attn_bu': (0.0, 0.1)}
    factors = {}
    for name, (base, spread) in spreads.items():
        noise = np.random.default_rng([zlib.crc32(name.encode()), seed]).standard_normal(out[name].shape)
        drawn = base * np.exp(spread * noise) if base else spread * noise
        out[name] = jnp.asarray(drawn.astype(out[name].dtype))
    for name, factor in factors.items():
        out[name] = (out[name] * factor).astype(out[name].dtype)
    return out
```

```python
from contextlib import ExitStack

import concourse.bass as bass
from concourse import mybir

P = 128
HALF = 512
NH = 8
HD = 32
DI = NH * HD
NS = 32
TAPS = 3
NEG = -1.0e30
EPS = 1e-5

ALU = mybir.AluOpType
ACT = mybir.ActivationFunctionType
F32 = mybir.dt.float32
BF16 = mybir.dt.bfloat16
AX = mybir.AxisListType.X
DVE_STEPS = 49


def hybrid_kernel(nc, x, ln_w, ln_b, in_w, conv_w, conv_b, A_log, D, dt_bias, rms_w, out_w,
                  Wk, Wq, Wv, Wu, bu, router_w, w1, w2, w3, out):
    B, C, HH, WW = x.shape
    L = HH * WW
    NC = L // P
    NT = B * NC
    E, HF, _ = w1.shape
    RH = HH // 2
    CB = 2 * NS
    assert C == P and L == 2 * HALF and Wq.shape[0] == NH * P
    FCH = [(f, min(P, HF - f)) for f in range(0, HF, P)]
    NF = len(FCH)

    ctx = ExitStack()
    with ctx:
        def sb(name, shape, dt=F32):
            return ctx.enter_context(nc.sbuf_tensor(name, shape, dt))

        def sem(name):
            return ctx.enter_context(nc.semaphore(name))

        psum = ctx.enter_context(nc.psum_tensor("psum", [P, 8 * HALF], F32))
        bank = [psum[:, i * HALF:(i + 1) * HALF] for i in range(8)]

        def psum_pair(i, width):
            return psum[:, i * HALF:i * HALF + width]

        def at(n, per, k):
            return n * per + k + 1

        ident = sb("ident", [P, P])
        ident_bf = sb("ident_bf", [P, P], BF16)
        upto = sb("upto", [P, P])
        mask_after = sb("mask_after", [P, P], BF16)
        mask_ahead = sb("mask_ahead", [P, P], BF16)
        mean_w = sb("mean_w", [P, P])
        in_nat = sb("in_nat", [P, 5, P])
        inT = sb("inT", [P, 584])
        cw = sb("cw", [P, 3, TAPS * TAPS])
        cb = sb("cb", [P, 3])
        lnw = sb("lnw", [P, 1])
        lnb = sb("lnb", [P, 1])
        rmsw = sb("rmsw", [P, 2])
        out_nat = sb("out_nat", [P, DI])
        outT = sb("outT", [P, 2, P])
        dtb = sb("dtb", [P, NH])
        alog = sb("alog", [P, NH])
        aexp = sb("aexp", [P, NH])
        aneg = sb("aneg", [P, NH])
        dvec = sb("dvec", [P, NH])
        bub = sb("bub", [P, P])

        t_all = sb("t_all", [P, NT, P])
        xT_all = sb("xT_all", [P, NT, P])

        wq = sb("wq", [P, NH, P])
        wk = sb("wk", [P, NH, P])
        wv = sb("wv", [P, NH, P])
        wu = sb("wu", [P, NH * P])

        consts_in = sem("consts_in")
        attn_in = sem("attn_in")
        pool_made = sem("pool_made")
        setup_T = sem("setup_T")
        setup_copied = sem("setup_copied")
        a_exp = sem("a_exp")
        a_neg = sem("a_neg")

        N_CONST = 14

        def start_at_one(sems, but):
            with nc.Block() as block:
                @block.sync
                def _(sp):
                    for name in sems:
                        if name not in but:
                            sp.sem_inc(sems[name], 1)

        scan = ExitStack()
        with scan:
            def sb1(name, shape, dt=F32):
                return scan.enter_context(nc.sbuf_tensor(name, shape, dt))

            x_in_sb = sb1("x_in_sb", [P, L])
            x_st = sb1("x_st", [P, L])
            xc = sb1("xc", [P, L])
            sq = sb1("sq", [P, L])
            rstd = sb1("rstd", [P, NC])
            xn = sb1("xn", [P, L])
            pad = sb1("pad", [P, 3, HH + 2, WW + 2])
            acc = sb1("acc", [P, 3, L])
            xsC = sb1("xsC", [P, 2, L])
            BC = sb1("BC", [NS, 2, L])
            zs = sb1("zs", [P, NC, DI])
            dtr = sb1("dtr", [P, NC * NH])
            dta = sb1("dta", [P, NC * NH])
            dte = sb1("dte", [P, NC * NH])
            dtl = sb1("dtl", [P, NC * NH])
            dt = sb1("dt", [P, NC * NH])
            dA = sb1("dA", [P, NC * NH])
            nAcs = sb1("nAcs", [P, NC * NH])
            eAcs = sb1("eAcs", [P, NC * NH])
            tok = sb1("tok", [P, NC, DI + NS])
            Ldec = sb1("Ldec", [P, 2, NH, P])
            edec = sb1("edec", [NS, NC, NH])
            GL = sb1("GL", [P, 2, NH, P])
            xdt = sb1("xdt", [P, 2, DI])
            dx = sb1("dx", [P, 2, DI])
            Xd = sb1("Xd", [P, 2, DI])
            S = sb1("S", [NS, DI])
            y1 = sb1("y1", [P, 2, DI])
            ysq = sb1("ysq", [P, DI])
            ssq = sb1("ssq", [P, NC])
            rs = sb1("rs", [P, NC])
            yn = sb1("yn", [P, 2, DI])
            yT = sb1("yT", [P, 2, 2, P])
            st6 = sb1("st6", [P, 6])
            mv = sb1("mv", [P, 2, 2])
            rs2 = sb1("rs2", [P, 2])
            xnt = sb1("xnt", [P, 2, P])
            mhalf = sb1("mhalf", [P, 1])
            epst = sb1("epst", [P, 1])

            names = """x_in mean_ready xc_ready sq_ready var_ready xn_ready proj_ready pad_copied zproj_ready z_ready
                dtproj_ready dtabs_ready dte_ready dtln_ready dA_ready acs_ready nacs_ready eacs_ready conv_done
                xs_ready tok_ready tok_copied seg_ready decay_ready gl_ready xd_ready xdt_ready dx_ready st_ready
                state_ready y_ready y_drained yg_ready ssq_ready yn_ready yT_ready yT_copied t_ready t_drained
                lnx_ready xnT_ready xnT_copied xst_ready dve_step pool_step pad_zero var_drained rstd_ready rstd_rows ms_ready rs_ready mv_ready ve_ready rs2_ready""".split()
            s = {n: sem(n) for n in names}

            start_at_one(s, ("x_in", "dve_step", "pool_step", "pad_zero"))
            with nc.Block() as block:
                @block.sync
                def _(sp):
                    sp.dma_start(in_nat[:, 0:4, :], in_w[0:512, :].rearrange("(j p) c -> p j c", p=P)).then_inc(consts_in, 16)
                    sp.dma_start(in_nat[0:72, 4, :], in_w[512:584, :]).then_inc(consts_in, 16)
                    sp.dma_start(cw[:, 0:2, :], conv_w[0:256].rearrange("(j p) a h w -> p j (a h w)", p=P)).then_inc(consts_in, 16)
                    sp.dma_start(cw[0:CB, 2, :], conv_w[256:320].rearrange("p a h w -> p (a h w)")).then_inc(consts_in, 16)
                    with nc.allow_non_contiguous_dma("small vectors, one element a partition"):
                        sp.dma_start(cb[:, 0:2], conv_b[0:256].rearrange("(j p) -> p j", p=P)).then_inc(consts_in, 16)
                        sp.dma_start(cb[0:CB, 2:3], conv_b[256:320].rearrange("(p a) -> p a", a=1)).then_inc(consts_in, 16)
                        sp.dma_start(lnw[:, :], ln_w.rearrange("(p a) -> p a", a=1)).then_inc(consts_in, 16)
                        sp.dma_start(lnb[:, :], ln_b.rearrange("(p a) -> p a", a=1)).then_inc(consts_in, 16)
                        sp.dma_start(rmsw[:, :], rms_w.rearrange("(j p) -> p j", p=P)).then_inc(consts_in, 16)
                    sp.dma_start(out_nat[:, :], out_w).then_inc(consts_in, 16)
                    sp.dma_start(dtb[:, :], dt_bias.partition_broadcast(P)).then_inc(consts_in, 16)
                    sp.dma_start(alog[:, :], A_log.partition_broadcast(P)).then_inc(consts_in, 16)
                    sp.dma_start(dvec[:, :], D.partition_broadcast(P)).then_inc(consts_in, 16)
                    sp.dma_start(bub[:, :], bu.partition_broadcast(P)).then_inc(consts_in, 16)
                    sp.dma_start(x_in_sb[:, :], x[0].rearrange("c h w -> c (h w)")).then_inc(s["x_in"], 16)
                    for w, src in ((wq, Wq), (wk, Wk), (wv, Wv)):
                        sp.dma_start(w[:, :, :], src.rearrange("(h o) d -> o h d", o=P)).then_inc(attn_in, 16)
                    sp.dma_start(wu[:, :], Wu).then_inc(attn_in, 16)
                    with sp.Fori(1, B) as b:
                        sp.wait_ge(s["xst_ready"], at(b, 1, 0))
                        sp.wait_ge(s["xc_ready"], at(b, 2, 0))
                        sp.dma_start(x_in_sb[:, :], x[bass.ds(b, 1)].rearrange("b c h w -> c (b h w)")).then_inc(s["x_in"], 16)

                @block.gpsimd
                def _(pool):
                    g = nc.gpsimd
                    g.memset(ident[:, :], 1.0).then_inc(s["pool_step"], 1)
                    g.memset(ident_bf[:, :], 1.0).then_inc(s["pool_step"], 1)
                    g.memset(upto[:, :], 1.0).then_inc(s["pool_step"], 1)
                    g.memset(mask_after[:, :], 0.0).then_inc(s["pool_step"], 1)
                    g.memset(mask_ahead[:, :], 0.0).then_inc(s["pool_step"], 1)
                    g.memset(mean_w[:, :], 1.0 / C).then_inc(s["pool_step"], 1)
                    g.memset(mhalf[:, :], -0.5).then_inc(s["pool_step"], 1)
                    g.memset(epst[:, :], EPS).then_inc(s["pool_step"], 1)
                    g.memset(pad[:, :, :, :], 0.0).then_inc(s["pad_zero"], 1)
                    pool.wait_ge(s["pool_step"], 8)
                    for m in (ident, ident_bf):
                        g.affine_select(out=m[:, :], in_=m[:, :], compare_op=ALU.is_equal, fill=0.0, base=0,
                                        pattern=[[-1, P]], channel_multiplier=1).then_inc(pool_made, 1)
                    g.affine_select(out=upto[:, :], in_=upto[:, :], compare_op=ALU.is_ge, fill=0.0, base=0,
                                    pattern=[[1, P]], channel_multiplier=-1).then_inc(pool_made, 1)
                    g.affine_select(out=mask_after[:, :], in_=mask_after[:, :], compare_op=ALU.is_ge, fill=NEG, base=0,
                                    pattern=[[1, P]], channel_multiplier=-1).then_inc(pool_made, 1)
                    g.affine_select(out=mask_ahead[:, :], in_=mask_ahead[:, :], compare_op=ALU.is_ge, fill=NEG, base=0,
                                    pattern=[[-1, P]], channel_multiplier=1).then_inc(pool_made, 1)
                    pool.wait_ge(consts_in, 16 * N_CONST)
                    def power(t, ready):
                        return g.tensor_tensor(t, t, mhalf[:, 0:1].to_broadcast([P, t.shape[1]]), ALU.pow).then_inc(ready, 1)

                    with pool.Fori(0, B) as b:
                        pool.wait_ge(s["var_drained"], at(b, 1, 1))
                        power(rstd[:, :], s["rstd_ready"])

                        def chunk_in(c):
                            pool.wait_ge(s["tok_copied"], at(b, NC, c + 1))
                            pool.wait_ge(s["y_ready"], at(b, NC, max(c - 1, 0)))
                            pool.wait_ge(s["xd_ready"], at(b, NC, max(c - 1, 0)))
                            xs3 = tok[:, c, 0:DI].rearrange("p (h d) -> p h d", d=HD)
                            g.tensor_tensor(xdt[:, c % 2, :].rearrange("p (h d) -> p h d", d=HD), xs3,
                                            dt[:, c * NH:(c + 1) * NH].unsqueeze(2).to_broadcast([P, NH, HD]), ALU.mult
                                            ).then_inc(s["xdt_ready"], 1)
                            pool.wait_ge(s["yg_ready"], at(b, NC, max(c - 1, 0)))
                            g.tensor_tensor(dx[:, c % 2, :].rearrange("p (h d) -> p h d", d=HD), xs3,
                                            dvec[:, :].unsqueeze(2).to_broadcast([P, NH, HD]), ALU.mult
                                            ).then_inc(s["dx_ready"], 1)

                        def chunk_rs(c):
                            pool.wait_ge(s["ssq_ready"], at(b, NC, c + 1))
                            if c == 0:
                                pool.wait_ge(s["yn_ready"], at(b, NC, 0))
                            g.tensor_tensor(rs[:, c:c + 1], ssq[:, c:c + 1], epst[:, :], ALU.add
                                            ).then_inc(s["ms_ready"], 1)
                            pool.wait_ge(s["ms_ready"], at(b, NC, c + 1))
                            power(rs[:, c:c + 1], s["rs_ready"])

                        def chunk_rs2(c):
                            pool.wait_ge(s["mv_ready"], at(b, NC, c + 1))
                            pool.wait_ge(s["lnx_ready"], at(b, NC, max(c - 1, 0)))
                            g.tensor_tensor(rs2[:, c % 2:c % 2 + 1], mv[:, c % 2, 1:2], epst[:, :], ALU.add
                                            ).then_inc(s["ve_ready"], 1)
                            pool.wait_ge(s["ve_ready"], at(b, NC, c + 1))
                            power(rs2[:, c % 2:c % 2 + 1], s["rs2_ready"])

                        for step in range(NC + 3):
                            for f, lag in ((chunk_in, 0), (chunk_rs, 1), (chunk_rs2, 3)):
                                if 0 <= step - lag < NC:
                                    f(step - lag)

                @block.tensor
                def _(pe):
                    t = nc.tensor
                    pe.wait_ge(pool_made, 5)
                    pe.wait_ge(consts_in, 16 * N_CONST)
                    for j in range(5):
                        n = P if j < 4 else 72
                        if j >= 2:
                            pe.wait_ge(setup_copied, j - 1)
                        t.transpose(bank[j % 2][:, 0:n], in_nat[0:n, j, :], ident[0:n, 0:n]).then_inc(setup_T, 1)
                    for j in range(2):
                        pe.wait_ge(setup_copied, 4 + j)
                        t.transpose(bank[(5 + j) % 2][:, 0:P], out_nat[:, j * P:(j + 1) * P], ident[:, :]).then_inc(setup_T, 1)
                    pe.wait_ge(setup_copied, 7)
                    with pe.Fori(0, B) as b:
                        pe.wait_ge(s["x_in"], b * 16 + 16)
                        pe.wait_ge(s["gl_ready"], at(b, NC, 0))
                        for hf in range(2):
                            t.matmul(bank[hf][:, :], mean_w[:, :],
                                     x_in_sb[:, hf * HALF:(hf + 1) * HALF],
                                     start=True, stop=True).then_inc(s["mean_ready"], 1)
                        pe.wait_ge(s["sq_ready"], at(b, 2, 2))
                        for c in range(NC):
                            last = t.matmul(bank[0][:, c:c + 1], sq[:, c * P:(c + 1) * P], mean_w[:, 0:1], start=True, stop=True)
                        last.then_inc(s["var_ready"], 1)
                        pe.wait_ge(s["rstd_ready"], at(b, 1, 1))
                        for c in range(NC):
                            last = t.matmul(bank[c // 4][:, (c % 4) * P:(c % 4 + 1) * P], rstd[:, c:c + 1].to_broadcast([P, P]),
                                            ident[:, :], start=True, stop=True)
                            if c % 4 == 3:
                                last.then_inc(s["rstd_rows"], 1)
                        pe.wait_ge(s["decay_ready"], at(b, NC, 0))
                        for u in range(6):
                            hf, m = u // 3, u % 3
                            n = P if m < 2 else CB
                            pe.wait_ge(s["xn_ready"], at(b, 2, hf + 1))
                            if u >= 2:
                                pe.wait_ge(s["pad_copied"], at(b, 6, u - 1))
                            t.matmul(bank[2 + u % 2][0:n, :], inT[:, DI + m * P:DI + m * P + n],
                                     xn[:, hf * HALF:(hf + 1) * HALF], start=True, stop=True).then_inc(s["proj_ready"], 1)
                        pe.wait_ge(s["yT_copied"], at(b, NC, 0))
                        pe.wait_ge(s["xnT_copied"], at(b, NC, 0))
                        for c in range(NC):
                            last = t.matmul(bank[6][:, c * NH:(c + 1) * NH], xn[:, c * P:(c + 1) * P], inT[:, 576:584],
                                            start=True, stop=True)
                        last.then_inc(s["dtproj_ready"], 1)
                        pe.wait_ge(s["y_drained"], at(b, NC, 0))
                        pe.wait_ge(s["state_ready"], at(b, NC, 0))
                        for c in range(NC):
                            if c >= 2:
                                pe.wait_ge(s["z_ready"], at(b, NC, c - 1))
                            t.matmul(bank[4 + c % 2][:, 0:DI], xn[:, c * P:(c + 1) * P], inT[:, 0:DI],
                                     start=True, stop=True).then_inc(s["zproj_ready"], 1)
                        pe.wait_ge(s["dA_ready"], at(b, 1, 1))
                        t.matmul(bank[6][:, 64:128], upto[:, :], dA[:, :], start=True, stop=True).then_inc(s["acs_ready"], 1)

                        def chunk_in(c):
                            sl = slice(c * P, (c + 1) * P)
                            pb = bank[c % 2]
                            if c == 0:
                                pe.wait_ge(s["xs_ready"], at(b, 4, 4))
                            if c >= 2:
                                pe.wait_ge(s["gl_ready"], at(b, NC, c - 1))
                            for m in range(2):
                                t.transpose(pb[:, m * P:(m + 1) * P], xsC[:, m, sl], ident[:, :])
                            t.transpose(pb[:, DI:DI + NS], BC[:, 0, sl], ident[0:NS, 0:NS])
                            t.matmul(pb[:, 384:512], BC[:, 0, sl], BC[:, 1, sl], start=True, stop=True).then_inc(s["tok_ready"], 1)
                            if c == 0:
                                pe.wait_ge(s["pad_copied"], at(b, 6, 6))
                            else:
                                pe.wait_ge(s["decay_ready"], at(b, NC, c))
                            for j in range(2):
                                seg = bank[2 + j]
                                t.matmul(seg[:, :].rearrange("p (h q) -> p h q", q=P), ident_bf[:, :],
                                         mask_after[:, :].unsqueeze(1).to_broadcast([P, 4, P]), start=True, stop=False)
                                for h in range(4):
                                    col = c * NH + 4 * j + h
                                    last = t.matmul(seg[:, h * P:(h + 1) * P], dA[:, col:col + 1].to_broadcast([P, P]),
                                                    upto[:, :], start=False, stop=(h == 3))
                            last.then_inc(s["seg_ready"], 1)

                        def chunk_y(c):
                            sl = slice(c * P, (c + 1) * P)
                            pe.wait_ge(s["xd_ready"], at(b, NC, c + 1))
                            if c == 0:
                                pe.wait_ge(s["z_ready"], at(b, NC, NC))
                            else:
                                pe.wait_ge(s["state_ready"], at(b, NC, c))
                            t.matmul(bank[5][0:NS, 0:DI], tok[:, c, DI:DI + NS], Xd[:, c % 2, :], start=True,
                                     stop=True).then_inc(s["st_ready"], 1)
                            pe.wait_ge(s["y_drained"], at(b, NC, c))
                            pe.wait_ge(s["gl_ready"], at(b, NC, c + 1))
                            pe.wait_ge(s["xdt_ready"], at(b, NC, c + 1))
                            for h in range(NH):
                                last = t.matmul(bank[4][:, DI + h * HD:DI + (h + 1) * HD], GL[:, c % 2, h, :],
                                                xdt[:, c % 2, h * HD:(h + 1) * HD], start=True, stop=True)
                            if c:
                                last = t.matmul(bank[4][:, 0:DI], BC[:, 1, sl], S[:, :], start=True, stop=True)
                            last.then_inc(s["y_ready"], 1)

                        def chunk_yT(c):
                            pe.wait_ge(s["yn_ready"], at(b, NC, c + 1))
                            if c == 0:
                                pe.wait_ge(s["nacs_ready"], at(b, 1, 1))
                            if c >= 4:
                                pe.wait_ge(s["xnT_copied"], at(b, NC, c - 3))
                            pe.wait_ge(s["yT_copied"], at(b, NC, c))
                            for j in range(2):
                                last = t.transpose(bank[6][:, j * P:(j + 1) * P], yn[:, c % 2, j * P:(j + 1) * P], ident[:, :])
                            last.then_inc(s["yT_ready"], 1)

                        def chunk_out(c):
                            if c == 0:
                                pe.wait_ge(s["xst_ready"], at(b, 1, 1))
                            pe.wait_ge(s["t_drained"], at(b, NC, c))
                            pe.wait_ge(s["yT_copied"], at(b, NC, c + 1))
                            t.matmul(bank[7][:, 0:P], x_st[:, c * P:(c + 1) * P], ident[:, :], start=True, stop=False)
                            t.matmul(bank[7][:, 0:P], yT[:, c % 2, 0, :], outT[:, 0, :], start=False, stop=False)
                            t.matmul(bank[7][:, 0:P], yT[:, c % 2, 1, :], outT[:, 1, :], start=False,
                                     stop=True).then_inc(s["t_ready"], 1)

                        def chunk_xnT(c):
                            pe.wait_ge(s["lnx_ready"], at(b, NC, c + 1))
                            pe.wait_ge(s["yT_copied"], at(b, NC, min(c + 4, NC)))
                            pe.wait_ge(s["xnT_copied"], at(b, NC, c))
                            t.transpose(bank[6][:, 256:384], xnt[:, c % 2, :], ident[:, :]).then_inc(s["xnT_ready"], 1)

                        for step in range(NC + 5):
                            for f, lag in ((chunk_in, 0), (chunk_y, 1), (chunk_yT, 2), (chunk_out, 3), (chunk_xnT, 5)):
                                if 0 <= step - lag < NC:
                                    f(step - lag)
                    pe.wait_ge(s["xnT_copied"], B * NC + 1)

                @block.scalar
                def _(act):
                    a = nc.scalar
                    act.wait_ge(consts_in, 16 * N_CONST)
                    a.activation(aexp[:, :], alog[:, :], ACT.Exp).then_inc(a_exp, 1)
                    act.wait_ge(s["pad_zero"], 1)
                    with act.Fori(0, B) as b:
                        for hf in range(2):
                            act.wait_ge(s["xc_ready"], at(b, 2, hf + 1))
                            a.activation(sq[:, hf * HALF:(hf + 1) * HALF], xc[:, hf * HALF:(hf + 1) * HALF],
                                         ACT.Square).then_inc(s["sq_ready"], 1)
                        act.wait_ge(s["conv_done"], at(b, 3, 0))
                        for u in range(6):
                            hf, m = u // 3, u % 3
                            n = P if m < 2 else CB
                            act.wait_ge(s["proj_ready"], at(b, 6, u + 1))
                            a.activation(pad[0:n, m, 1 + hf * RH:1 + (hf + 1) * RH, 1:1 + WW],
                                         bank[2 + u % 2][0:n, :].rearrange("p (h w) -> p h w", w=WW),
                                         ACT.Copy).then_inc(s["pad_copied"], 1)
                        act.wait_ge(s["t_ready"], at(b, NC, 0))
                        a.activation(x_st[:, :], x_in_sb[:, :], ACT.Copy).then_inc(s["xst_ready"], 1)
                        act.wait_ge(s["yg_ready"], at(b, NC, 0))
                        for c in range(NC):
                            act.wait_ge(s["zproj_ready"], at(b, NC, c + 1))
                            a.activation(zs[:, c, :], bank[4 + c % 2][:, 0:DI], ACT.Silu).then_inc(s["z_ready"], 1)
                        act.wait_ge(s["dtabs_ready"], at(b, 1, 1))
                        a.activation(dte[:, :], dta[:, :], ACT.Exp, scale=-1.0).then_inc(s["dte_ready"], 1)
                        act.wait_ge(s["dte_ready"], at(b, 1, 1))
                        a.activation(dtl[:, :], dte[:, :], ACT.Ln, bias=1.0).then_inc(s["dtln_ready"], 1)
                        act.wait_ge(s["tok_ready"], at(b, NC, 0))
                        act.wait_ge(s["y_ready"], at(b, NC, 0))
                        for m in range(2):
                            act.wait_ge(s["conv_done"], at(b, 3, m + 1))
                            a.activation(xsC[:, m, :], acc[:, m, :], ACT.Silu, bias=cb[:, m:m + 1]).then_inc(s["xs_ready"], 1)
                        act.wait_ge(s["conv_done"], at(b, 3, 3))
                        for j in range(2):
                            a.activation(BC[:, j, :], acc[j * NS:(j + 1) * NS, 2, :], ACT.Silu,
                                         bias=cb[j * NS:(j + 1) * NS, 2:3]).then_inc(s["xs_ready"], 1)
                        act.wait_ge(s["nacs_ready"], at(b, 1, 1))
                        a.activation(eAcs[:, :], nAcs[:, :], ACT.Exp, scale=-1.0).then_inc(s["eacs_ready"], 1)

                        def chunk_in(c):
                            if c == 0:
                                act.wait_ge(s["st_ready"], at(b, NC, 0))
                                act.wait_ge(s["dx_ready"], at(b, NC, 0))
                            act.wait_ge(s["tok_ready"], at(b, NC, c + 1))
                            a.activation(tok[:, c, :], bank[c % 2][:, 0:DI + NS], ACT.Copy).then_inc(s["tok_copied"], 1)
                            act.wait_ge(s["seg_ready"], at(b, NC, c + 1))
                            act.wait_ge(s["xd_ready"], at(b, NC, max(c - 1, 0)))
                            act.wait_ge(s["gl_ready"], at(b, NC, max(c - 1, 0)))
                            for h in range(NH):
                                a.activation(Ldec[:, c % 2, h, :], bank[2 + h // 4][:, (h % 4) * P:(h % 4 + 1) * P], ACT.Exp,
                                             bias=nAcs[:, c * NH + h:c * NH + h + 1])
                            if c == 0:
                                act.wait_ge(s["state_ready"], at(b, NC, 0))
                            for j in range(2):
                                last = a.activation(edec[:, c, 4 * j:4 * j + 4],
                                                    bank[2 + j][0:NS, :].rearrange("p (h q) -> p h q", q=P)[:, :, P - 1],
                                                    ACT.Exp)
                            last.then_inc(s["decay_ready"], 1)

                        def chunk_sq(c):
                            act.wait_ge(s["yg_ready"], at(b, NC, c + 1))
                            if c == 0:
                                act.wait_ge(s["yn_ready"], at(b, NC, 0))
                            act.wait_ge(s["ssq_ready"], at(b, NC, c))
                            a.activation(ysq[:, :], y1[:, c % 2, :], ACT.Square, scale=DI ** -0.5,
                                         accum_out=ssq[:, c:c + 1]).then_inc(s["ssq_ready"], 1)

                        def chunk_yT(c):
                            act.wait_ge(s["yT_ready"], at(b, NC, c + 1))
                            act.wait_ge(s["t_ready"], at(b, NC, max(c - 1, 0)))
                            a.activation(yT[:, c % 2, :, :], bank[6][:, 0:256].rearrange("p (j q) -> p j q", q=P),
                                         ACT.Copy).then_inc(s["yT_copied"], 1)

                        def chunk_xnT(c):
                            act.wait_ge(s["xnT_ready"], at(b, NC, c + 1))
                            a.activation(xT_all[:, bass.ds(b * NC + c, 1), :].rearrange("p a q -> p (a q)"),
                                         bank[6][:, 256:384], ACT.Copy).then_inc(s["xnT_copied"], 1)

                        for step in range(NC + 5):
                            for f, lag in ((chunk_in, 0), (chunk_sq, 1), (chunk_yT, 2), (chunk_xnT, 5)):
                                if 0 <= step - lag < NC:
                                    f(step - lag)

                @block.vector
                def _(dve):
                    v = nc.vector
                    for j in range(5):
                        n = P if j < 4 else 72
                        dve.wait_ge(setup_T, j + 1)
                        v.tensor_copy(inT[:, j * P:j * P + n], bank[j % 2][:, 0:n]).then_inc(setup_copied, 1)
                    for j in range(2):
                        dve.wait_ge(setup_T, 6 + j)
                        v.tensor_scalar(outT[:, j, :], bank[(5 + j) % 2][:, 0:P], rmsw[:, j:j + 1], None,
                                        ALU.mult).then_inc(setup_copied, 1)
                    dve.wait_ge(a_exp, 1)
                    v.tensor_scalar(aneg[:, :], aexp[:, :], -1.0, None, ALU.mult).then_inc(a_neg, 1)
                    dve.wait_ge(a_neg, 1)
                    dve.wait_ge(s["x_in"], 16)
                    PER = DVE_STEPS
                    with dve.Fori(0, B) as b:
                        k = [0]

                        def link(ins):
                            k[0] += 1
                            ins.then_inc(s["dve_step"], 1)
                            dve.wait_ge(s["dve_step"], b * PER + k[0])

                        for hf in range(2):
                            sl = slice(hf * HALF, (hf + 1) * HALF)
                            dve.wait_ge(s["mean_ready"], at(b, 2, hf + 1))
                            v.tensor_tensor(xc[:, sl], x_in_sb[:, sl],
                                            bank[hf][:, :], ALU.subtract).then_inc(s["xc_ready"], 1)
                        dve.wait_ge(s["zproj_ready"], at(b, NC, 0))
                        dve.wait_ge(s["xc_ready"], at(b, 2, 2))
                        dve.wait_ge(s["var_ready"], at(b, 1, 1))
                        v.tensor_scalar(rstd[:, :], bank[0][:, 0:NC], EPS, None, ALU.add).then_inc(s["var_drained"], 1)
                        for hf in range(2):
                            sl = slice(hf * HALF, (hf + 1) * HALF)
                            dve.wait_ge(s["rstd_rows"], at(b, 2, hf + 1))
                            link(v.tensor_tensor(xn[:, sl], xc[:, sl], bank[hf][:, :], ALU.mult))
                            v.tensor_scalar(xn[:, sl], xn[:, sl], lnw[:, :], lnb[:, :], ALU.mult, ALU.add
                                            ).then_inc(s["xn_ready"], 1)
                        dve.wait_ge(s["dtproj_ready"], at(b, 1, 1))
                        link(v.tensor_tensor(dtr[:, :].rearrange("p (c h) -> p c h", h=NH),
                                             bank[6][:, 0:NC * NH].rearrange("p (c h) -> p c h", h=NH),
                                             dtb[:, :].unsqueeze(1).to_broadcast([P, NC, NH]), ALU.add))
                        v.scalar_tensor_tensor(dta[:, :], dtr[:, :], -1.0, dtr[:, :], ALU.mult, ALU.max
                                               ).then_inc(s["dtabs_ready"], 1)

                        def conv(m):
                            n = P if m < 2 else CB
                            dst = acc[0:n, m, :].rearrange("p (h w) -> p h w", w=WW)
                            for tap in range(TAPS * TAPS):
                                r, c0 = tap // TAPS, tap % TAPS
                                win = pad[0:n, m, r:r + HH, c0:c0 + WW]
                                if tap == 0:
                                    ins = v.tensor_scalar(dst, win, cw[0:n, m, 0:1], None, ALU.mult)
                                else:
                                    ins = v.scalar_tensor_tensor(dst, win, cw[0:n, m, tap:tap + 1], dst, ALU.mult, ALU.add)
                                if tap < TAPS * TAPS - 1:
                                    link(ins)
                            ins.then_inc(s["conv_done"], 1)

                        dve.wait_ge(s["pad_copied"], at(b, 6, 6))
                        dve.wait_ge(s["xs_ready"], at(b, 4, 0))
                        conv(0)
                        dve.wait_ge(s["dtln_ready"], at(b, 1, 1))
                        dve.wait_ge(s["xdt_ready"], at(b, NC, 0))
                        link(v.scalar_tensor_tensor(dt[:, :], dtr[:, :], 0.0, dtl[:, :], ALU.max, ALU.add))
                        dve.wait_ge(s["seg_ready"], at(b, NC, 0))
                        v.tensor_tensor(dA[:, :].rearrange("p (c h) -> p c h", h=NH),
                                        dt[:, :].rearrange("p (c h) -> p c h", h=NH),
                                        aneg[:, :].unsqueeze(1).to_broadcast([P, NC, NH]), ALU.mult).then_inc(s["dA_ready"], 1)
                        conv(1)
                        conv(2)
                        dve.wait_ge(s["acs_ready"], at(b, 1, 1))
                        dve.wait_ge(s["decay_ready"], at(b, NC, 0))
                        v.tensor_scalar(nAcs[:, :], bank[6][:, 64:128], -1.0, None, ALU.mult).then_inc(s["nacs_ready"], 1)

                        def chunk_norm(c):
                            dve.wait_ge(s["rs_ready"], at(b, NC, c + 1))
                            dve.wait_ge(s["yT_ready"], at(b, NC, max(c - 1, 0)))
                            v.tensor_scalar(yn[:, c % 2, :], y1[:, c % 2, :], rs[:, c:c + 1], None, ALU.mult
                                            ).then_inc(s["yn_ready"], 1)

                        def chunk_in(c):
                            dve.wait_ge(s["decay_ready"], at(b, NC, c + 1))
                            dve.wait_ge(s["tok_copied"], at(b, NC, c + 1))
                            dve.wait_ge(s["y_ready"], at(b, NC, max(c - 1, 0)))
                            v.tensor_tensor(GL[:, c % 2, :, :], Ldec[:, c % 2, :, :],
                                            bank[c % 2][:, 384:512].unsqueeze(1).to_broadcast([P, NH, P]), ALU.mult
                                            ).then_inc(s["gl_ready"], 1)
                            dve.wait_ge(s["xdt_ready"], at(b, NC, c + 1))
                            dve.wait_ge(s["st_ready"], at(b, NC, max(c - 1, 0)))
                            v.tensor_tensor(Xd[:, c % 2, :].rearrange("p (h d) -> p h d", d=HD),
                                            xdt[:, c % 2, :].rearrange("p (h d) -> p h d", d=HD),
                                            Ldec[:, c % 2, :, P - 1:P].to_broadcast([P, NH, HD]), ALU.mult
                                            ).then_inc(s["xd_ready"], 1)

                        def chunk_y(c):
                            dve.wait_ge(s["st_ready"], at(b, NC, c + 1))
                            dve.wait_ge(s["y_ready"], at(b, NC, c + 1))
                            if c == 0:
                                v.tensor_copy(S[:, :], bank[5][0:NS, 0:DI]).then_inc(s["state_ready"], 1)
                                dve.wait_ge(s["dx_ready"], at(b, NC, c + 1))
                                ins = v.tensor_tensor(y1[:, c % 2, :], bank[4][:, DI:2 * DI], dx[:, c % 2, :], ALU.add)
                                ins.then_inc(s["y_drained"], 1)
                                dve.wait_ge(s["y_drained"], at(b, NC, c + 1))
                            else:
                                link(v.tensor_tensor(S[:, :].rearrange("p (h d) -> p h d", d=HD),
                                                     S[:, :].rearrange("p (h d) -> p h d", d=HD),
                                                     edec[:, c, :].unsqueeze(2).to_broadcast([NS, NH, HD]), ALU.mult))
                                v.tensor_tensor(S[:, :], S[:, :], bank[5][0:NS, 0:DI], ALU.add).then_inc(s["state_ready"], 1)
                                if c == 1:
                                    dve.wait_ge(s["eacs_ready"], at(b, 1, 1))
                                link(v.tensor_tensor(y1[:, c % 2, :].rearrange("p (h d) -> p h d", d=HD),
                                                     bank[4][:, 0:DI].rearrange("p (h d) -> p h d", d=HD),
                                                     eAcs[:, c * NH:(c + 1) * NH].unsqueeze(2).to_broadcast([P, NH, HD]), ALU.mult))
                                ins = v.tensor_tensor(y1[:, c % 2, :], y1[:, c % 2, :], bank[4][:, DI:2 * DI], ALU.add)
                                ins.then_inc(s["y_drained"], 1)
                                dve.wait_ge(s["y_drained"], at(b, NC, c + 1))
                                dve.wait_ge(s["dx_ready"], at(b, NC, c + 1))
                                link(v.tensor_tensor(y1[:, c % 2, :], y1[:, c % 2, :], dx[:, c % 2, :], ALU.add))
                            if c == 0:
                                dve.wait_ge(s["z_ready"], at(b, NC, NC))
                            v.tensor_tensor(y1[:, c % 2, :], y1[:, c % 2, :], zs[:, c, :], ALU.mult).then_inc(s["yg_ready"], 1)

                        def chunk_ln(c):
                            tile = t_all[:, bass.ds(b * NC + c, 1), :].rearrange("p a q -> p (a q)")
                            dve.wait_ge(s["ve_ready"], at(b, NC, max(c - 1, 0)))
                            dve.wait_ge(s["t_ready"], at(b, NC, c + 1))
                            v.tensor_copy(tile, bank[7][:, 0:P]).then_inc(s["t_drained"], 1)
                            dve.drain()
                            v.bn_stats(st6[:, :], tile)
                            dve.drain()
                            v.bn_aggr(mv[:, c % 2, :], st6[:, :]).then_inc(s["mv_ready"], 1)

                        def chunk_lnx(c):
                            tile = t_all[:, bass.ds(b * NC + c, 1), :].rearrange("p a q -> p (a q)")
                            dve.wait_ge(s["rs2_ready"], at(b, NC, c + 1))
                            dve.wait_ge(s["xnT_ready"], at(b, NC, max(c - 1, 0)))
                            v.tensor_scalar(xnt[:, c % 2, :], tile, mv[:, c % 2, 0:1], rs2[:, c % 2:c % 2 + 1], ALU.subtract, ALU.mult
                                            ).then_inc(s["lnx_ready"], 1)

                        for step in range(NC + 4):
                            for f, lag in ((chunk_norm, 2), (chunk_in, 0), (chunk_y, 1), (chunk_ln, 3), (chunk_lnx, 4)):
                                if 0 <= step - lag < NC:
                                    f(step - lag)
                        assert k[0] == PER, k[0]


        with ExitStack() as attn:
            def sb2(name, shape, dt=F32):
                return attn.enter_context(nc.sbuf_tensor(name, shape, dt))

            wuT = sb2("wuT", [P, NH, P])
            qk_w = sb2("qk_w", [P, NH, P])
            vu_w = sb2("vu_w", [P, NH, P])
            qk_st = sb2("qk_st", [P, P])
            x_at = sb2("x_at", [P, L])
            vals = sb2("vals", [P, NC, NH * P])
            qT = sb2("qT", [P, L])
            prob = sb2("prob", [P, 2, L])
            probT = sb2("probT", [P, 2, NC, P])
            nmax = sb2("nmax", [P, NC])
            rsum = sb2("rsum", [P, NC])
            rinv = sb2("rinv", [P, NC])

            a = {n: sem(n) for n in """w_filled w_copied x_at_ready qk_st_ready bank4_filled bank5_filled bank4_drained
                bank5_drained scores_ready nmax_ready prob_ready att_ready att_drained rinv_ready bias_added""".split()}
            start_at_one(a, ("w_filled", "w_copied"))
            filled = [a["bank4_filled"], a["bank5_filled"]]
            emptied = [a["bank4_drained"], a["bank5_drained"]]
            PER_HEAD = 7
            FIRST = NC + 1
            PER_IMAGE = FIRST + NH * PER_HEAD - 1
            groups = [(i, g) for i in range(NC) for g in range(0, i + 1, 4)]
            with nc.Block() as block:
                @block.tensor
                def _(pe):
                    t = nc.tensor
                    pe.wait_ge(attn_in, 16 * 4)
                    for h in range(NH):
                        if h >= 2:
                            pe.wait_ge(a["w_copied"], h - 1)
                        t.transpose(bank[h % 2][:, 0:P], wu[:, h * P:(h + 1) * P], ident[:, :]).then_inc(a["w_filled"], 1)
                    for h in range(NH):
                        pe.wait_ge(a["w_copied"], NH + h - 1)
                        if h == 0:
                            pe.wait_ge(a["w_copied"], NH)
                        t.matmul(bank[h % 2][:, 0:P], wq[:, h, :], wk[:, h, :], start=True, stop=True)
                        t.matmul(bank[h % 2][:, P:2 * P], wv[:, h, :], wuT[:, h, :], start=True,
                                 stop=True).then_inc(a["w_filled"], 1)

                    def project(b, use, w):
                        for hf in range(2):
                            pe.wait_ge(emptied[hf], at(b, PER_IMAGE, use))
                            t.matmul(bank[4 + hf][:, :], w, x_at[:, hf * HALF:(hf + 1) * HALF], start=True,
                                     stop=True).then_inc(filled[hf], 1)

                    with pe.Fori(0, B) as b:
                        pe.wait_ge(a["x_at_ready"], at(b, 1, 1))
                        for i in range(NC):
                            for hf in range(2):
                                pe.wait_ge(emptied[hf], at(b, PER_IMAGE, i))
                                t.matmul(bank[4 + hf][:, :], x_at[:, i * P:(i + 1) * P],
                                         vu_w[:, 4 * hf:4 * hf + 4, :].rearrange("p h c -> p (h c)"), start=True,
                                         stop=True).then_inc(filled[hf], 1)
                        pe.wait_ge(a["qk_st_ready"], at(b, NH, 1))
                        project(b, NC, qk_st[:, :])

                        def head(h, more):
                            hh = b * NH + h
                            use0 = FIRST + h * PER_HEAD
                            uses = [0]

                            def scores(i):
                                w = (i + 1) * P
                                if i == 0:
                                    for hf in range(2):
                                        pe.wait_ge(emptied[hf], at(b, PER_IMAGE, use0))
                                pe.wait_ge(a["prob_ready"], at(hh, NC, max(i - 1, 0)))
                                for j in range((w + HALF - 1) // HALF):
                                    n = min(HALF, w - j * HALF)
                                    diag = i * P - j * HALF
                                    last_j = w <= (j + 1) * HALF
                                    last = t.matmul(bank[2 * (i % 2) + j][:, 0:n], qT[:, i * P:(i + 1) * P],
                                                    x_at[:, j * HALF:j * HALF + n], start=True, stop=not last_j)
                                    if last_j:
                                        last = t.matmul(bank[2 * (i % 2) + j][:, diag:diag + P], ident_bf[:, :],
                                                        mask_ahead[:, :], start=False, stop=True)
                                last.then_inc(a["scores_ready"], 1)

                            def turn(i):
                                pe.wait_ge(a["prob_ready"], at(hh, NC, i + 1))
                                for g in range(0, i + 1, 4):
                                    u = uses[0]
                                    pe.wait_ge(emptied[u % 2], at(b, PER_IMAGE, use0 + u // 2))
                                    for kt in range(g, min(g + 4, i + 1)):
                                        last = t.transpose(bank[4 + u % 2][:, (kt - g) * P:(kt - g + 1) * P],
                                                           prob[:, i % 2, kt * P:(kt + 1) * P], ident[:, :])
                                    last.then_inc(filled[u % 2], 1)
                                    uses[0] += 1

                            def attend(i):
                                done = (sum(1 for x in groups if x[0] <= i) + (2 if proj_at <= i else 0))
                                for hf in range(2):
                                    pe.wait_ge(emptied[hf], at(b, PER_IMAGE, use0 + (done + 1 - hf) // 2))
                                pe.wait_ge(a["att_drained"], at(hh, NC, max(i - 1, 0)))
                                for kt in range(i + 1):
                                    last = t.matmul(bank[6 + i % 2][:, 0:P], probT[:, i % 2, kt, :],
                                                    vals[:, kt, bass.ds(h * P, P)], start=(kt == 0), stop=(kt == i))
                                last.then_inc(a["att_ready"], 1)

                            proj_at = NC - 1 if more else NC
                            for step in range(NC + 2):
                                if step < NC:
                                    scores(step)
                                if step == NC - 1 and more:
                                    pe.wait_ge(a["qk_st_ready"], at(hh, 1, 2))
                                    assert uses[0] % 2 == 0
                                if 1 <= step <= NC:
                                    if step - 1 == NC - 1 and more:
                                        project(b, use0 + uses[0] // 2, qk_st[:, :])
                                        uses[0] += 2
                                    turn(step - 1)
                                if step >= 2:
                                    attend(step - 2)

                        with pe.Fori(0, NH - 1) as h:
                            head(h, True)
                        head(NH - 1, False)

                @block.scalar
                def _(act):
                    s_ = nc.scalar
                    with act.Fori(0, B) as b:
                        for i in range(NC):
                            act.wait_ge(filled[0], at(b, PER_IMAGE, i + 1))
                            if i == 0:
                                act.wait_ge(a["att_ready"], at(b, NH * NC, 0))
                            s_.activation(vals[:, i, 0:HALF], bank[4][:, :], ACT.Copy).then_inc(emptied[0], 1)

                        def queries(use):
                            for hf in range(2):
                                act.wait_ge(filled[hf], at(b, PER_IMAGE, use + 1))
                                s_.activation(qT[:, hf * HALF:(hf + 1) * HALF], bank[4 + hf][:, :], ACT.Copy).then_inc(emptied[hf], 1)

                        queries(NC)

                        def head(h, more):
                            hh = b * NH + h
                            use0 = FIRST + h * PER_HEAD
                            uses = [0]
                            for step in range(NC + 1):
                                if step < NC:
                                    i = step
                                    act.wait_ge(a["nmax_ready"], at(hh, NC, i + 1))
                                    for hf in range(2):
                                        act.wait_ge(filled[hf], at(b, PER_IMAGE, use0 + (sum(1 for x in groups if x[0] <= i - 2) + 1 - hf) // 2))
                                    if i == 0:
                                        act.wait_ge(a["rinv_ready"], at(hh, NC, 0))
                                    w = (i + 1) * P
                                    src = psum_pair(2 * (i % 2), w)
                                    s_.activation(prob[:, i % 2, 0:w], src, ACT.Exp, bias=nmax[:, i:i + 1],
                                                  accum_out=rsum[:, i:i + 1]).then_inc(a["prob_ready"], 1)
                                if step >= 1:
                                    i = step - 1
                                    if i == NC - 1 and more:
                                        queries(use0 + uses[0] // 2)
                                        uses[0] += 2
                                    for g in range(0, i + 1, 4):
                                        u = uses[0]
                                        n = min(4, i + 1 - g)
                                        act.wait_ge(filled[u % 2], at(b, PER_IMAGE, use0 + u // 2 + 1))
                                        act.wait_ge(a["att_ready"], at(hh, NC, max(i - 1, 0)))
                                        s_.activation(probT[:, i % 2, g:g + n, :],
                                                      bank[4 + u % 2][:, 0:n * P].rearrange("p (k q) -> p k q", q=P),
                                                      ACT.Copy).then_inc(emptied[u % 2], 1)
                                        uses[0] += 1

                        with act.Fori(0, NH - 1) as h:
                            head(h, True)
                        head(NH - 1, False)

                @block.vector
                def _(dve):
                    v = nc.vector
                    for h in range(NH):
                        dve.wait_ge(a["w_filled"], h + 1)
                        v.tensor_copy(wuT[:, h, :], bank[h % 2][:, 0:P]).then_inc(a["w_copied"], 1)
                    for h in range(NH):
                        dve.wait_ge(a["w_filled"], NH + h + 1)
                        v.tensor_scalar(qk_w[:, h, :], bank[h % 2][:, 0:P], P ** -0.5, None, ALU.mult)
                        v.tensor_copy(vu_w[:, h, :], bank[h % 2][:, P:2 * P]).then_inc(a["w_copied"], 1)
                    dve.wait_ge(a["w_copied"], 2 * NH)
                    with dve.Fori(0, B) as b:
                        dve.wait_ge(a["att_ready"], at(b, NH * NC, 0))
                        v.tensor_copy(x_at[:, :].rearrange("p (i q) -> p i q", q=P), xT_all[:, bass.ds(b * NC, NC), :]
                                      ).then_inc(a["x_at_ready"], 1)
                        v.tensor_copy(qk_st[:, :], qk_w[:, 0, :]).then_inc(a["qk_st_ready"], 1)
                        tiles = t_all[:, bass.ds(b * NC, NC), :]
                        v.tensor_tensor(tiles, tiles, bub[:, :].unsqueeze(1).to_broadcast([P, NC, P]), ALU.add
                                        ).then_inc(a["bias_added"], 1)
                        for i in range(NC):
                            dve.wait_ge(filled[1], at(b, PER_IMAGE, i + 1))
                            if i == 0:
                                dve.wait_ge(a["bias_added"], at(b, 1, 1))
                            v.tensor_copy(vals[:, i, HALF:2 * HALF], bank[5][:, :]).then_inc(emptied[1], 1)

                        def head(h, more):
                            hh = b * NH + h
                            for step in range(NC + 2):
                                if step < NC:
                                    i = step
                                    dve.wait_ge(a["scores_ready"], at(hh, NC, i + 1))
                                    w = (i + 1) * P
                                    if i == 0:
                                        dve.wait_ge(a["prob_ready"], at(hh, NC, 0))
                                    v.reduce_max(nmax[:, i:i + 1], psum_pair(2 * (i % 2), w), AX, negate=True
                                                 ).then_inc(a["nmax_ready"], 1)
                                if step == 1 and more:
                                    v.tensor_copy(qk_st[:, :], qk_w[:, bass.ds(h + 1, 1), :].rearrange("p a q -> p (a q)")
                                                  ).then_inc(a["qk_st_ready"], 1)
                                if step >= 2:
                                    i = step - 2
                                    tile = t_all[:, bass.ds(b * NC + i, 1), :].rearrange("p a q -> p (a q)")
                                    dve.wait_ge(a["prob_ready"], at(hh, NC, i + 1))
                                    if i == 0:
                                        dve.wait_ge(a["att_drained"], at(hh, NC, 0))
                                    v.reciprocal(rinv[:, i:i + 1], rsum[:, i:i + 1]).then_inc(a["rinv_ready"], 1)
                                    dve.wait_ge(a["rinv_ready"], at(hh, NC, i + 1))
                                    dve.wait_ge(a["att_ready"], at(hh, NC, i + 1))
                                    v.scalar_tensor_tensor(tile, bank[6 + i % 2][:, 0:P], rinv[:, i:i + 1], tile,
                                                           ALU.mult, ALU.add).then_inc(a["att_drained"], 1)

                        with dve.Fori(0, NH - 1) as h:
                            head(h, True)
                        head(NH - 1, False)

        gates = sb("gates", [P, NT, E])
        with ExitStack() as rout:
            def sb3(name, shape, dt=F32):
                return rout.enter_context(nc.sbuf_tensor(name, shape, dt))

            router_nat = sb3("router_nat", [E, P])
            routerT = sb3("routerT", [P, E])
            st6b = sb3("st6b", [P, 6])
            mvb = sb3("mvb", [P, 2, 2])
            rsb = sb3("rsb", [P, 2])
            x2t = sb3("x2t", [P, 2, P])
            x2s = sb3("x2s", [P, 2, P])
            logits = sb3("logits", [P, NT, E])
            expo = sb3("expo", [P, NT, E])
            probs = sb3("probs", [P, NT, E])
            first = sb3("first", [P, NT, E])
            second = sb3("second", [P, NT, E])
            cand = sb3("cand", [P, NT, E])
            number = sb3("number", [P, E])
            best = sb3("best", [P, NT])
            best2 = sb3("best2", [P, NT])
            pick = sb3("pick", [P, NT])
            den = sb3("den", [P, NT])
            mhalf2 = sb3("mhalf2", [P, 1])
            epst2 = sb3("epst2", [P, 1])
            r = {n: sem(n) for n in """mvb_ready veb_ready rsb_ready x2_ready x2T_ready x2s_ready x2T_copied logits_ready
                logits_drained router_in routerT_ready routerT_copied consts2_made peak_off expo_ready gate_step""".split()}
            start_at_one(r, ("router_in", "routerT_ready", "routerT_copied", "consts2_made", "peak_off", "expo_ready", "gate_step"))
            with nc.Block() as block:
                @block.sync
                def _(sp):
                    sp.dma_start(router_nat[:, :], router_w).then_inc(r["router_in"], 16)

                @block.gpsimd
                def _(pool):
                    g = nc.gpsimd
                    g.memset(mhalf2[:, :], -0.5).then_inc(r["consts2_made"], 1)
                    g.memset(epst2[:, :], EPS).then_inc(r["consts2_made"], 1)
                    for e in range(E):
                        g.memset(number[:, e:e + 1], float(e)).then_inc(r["consts2_made"], 1)
                    pool.wait_ge(r["consts2_made"], 2 + E)
                    with pool.Fori(0, B) as b:
                        for c in range(NC):
                            pool.wait_ge(r["mvb_ready"], at(b, NC, c + 1))
                            pool.wait_ge(r["x2_ready"], at(b, NC, max(c - 1, 0)))
                            g.tensor_tensor(rsb[:, c % 2:c % 2 + 1], mvb[:, c % 2, 1:2], epst2[:, :], ALU.add
                                            ).then_inc(r["veb_ready"], 1)
                            pool.wait_ge(r["veb_ready"], at(b, NC, c + 1))
                            g.tensor_tensor(rsb[:, c % 2:c % 2 + 1], rsb[:, c % 2:c % 2 + 1], mhalf2[:, :], ALU.pow
                                            ).then_inc(r["rsb_ready"], 1)

                @block.vector
                def _(dve):
                    v = nc.vector
                    dve.wait_ge(r["routerT_ready"], 1)
                    v.tensor_copy(routerT[:, :], bank[0][:, 0:E]).then_inc(r["routerT_copied"], 1)
                    with dve.Fori(0, B) as b:
                        def stats(c):
                            tile = t_all[:, bass.ds(b * NC + c, 1), :].rearrange("p a q -> p (a q)")
                            dve.drain()
                            v.bn_stats(st6b[:, :], tile)
                            dve.drain()
                            v.bn_aggr(mvb[:, c % 2, :], st6b[:, :]).then_inc(r["mvb_ready"], 1)

                        def norm(c):
                            tile = t_all[:, bass.ds(b * NC + c, 1), :].rearrange("p a q -> p (a q)")
                            dve.wait_ge(r["rsb_ready"], at(b, NC, c + 1))
                            dve.wait_ge(r["x2T_ready"], at(b, NC, max(c - 1, 0)))
                            v.tensor_scalar(x2t[:, c % 2, :], tile, mvb[:, c % 2, 0:1], rsb[:, c % 2:c % 2 + 1],
                                            ALU.subtract, ALU.mult).then_inc(r["x2_ready"], 1)

                        for c in range(NC + 1):
                            if c < NC:
                                stats(c)
                            if c:
                                norm(c - 1)
                        dve.wait_ge(r["logits_ready"], at(b, 1, 1))
                        v.tensor_copy(logits[:, bass.ds(b * NC, NC), :],
                                      bank[2][:, 0:NC * E].rearrange("p (c e) -> p c e", e=E)).then_inc(r["logits_drained"], 1)

                    k = [0]

                    def step(ins):
                        k[0] += 1
                        ins.then_inc(r["gate_step"], 1)
                        dve.wait_ge(r["gate_step"], k[0])

                    def wide(t):
                        return t[:, :].unsqueeze(2).to_broadcast([P, NT, E])

                    numbers = number[:, :].unsqueeze(1).to_broadcast([P, NT, E])
                    dve.wait_ge(r["logits_drained"], B + 1)
                    step(v.reduce_max(best[:, :], logits[:, :, :], AX))
                    v.tensor_tensor(logits[:, :, :], logits[:, :, :], wide(best), ALU.subtract).then_inc(r["peak_off"], 1)
                    dve.wait_ge(r["expo_ready"], 1)
                    step(v.tensor_reduce(den[:, :], expo[:, :, :], AX, ALU.add))
                    step(v.reciprocal(den[:, :], den[:, :]))
                    step(v.tensor_tensor(probs[:, :, :], expo[:, :, :], wide(den), ALU.mult))

                    def top(hot, value):
                        step(v.reduce_max(value[:, :], probs[:, :, :], AX))
                        step(v.tensor_tensor(cand[:, :, :], probs[:, :, :], wide(value), ALU.is_lt))
                        step(v.tensor_scalar(cand[:, :, :], cand[:, :, :], float(E), None, ALU.mult))
                        step(v.tensor_tensor(cand[:, :, :], cand[:, :, :], numbers, ALU.add))
                        step(v.tensor_reduce(pick[:, :], cand[:, :, :], AX, ALU.min))
                        step(v.tensor_tensor(hot[:, :, :], wide(pick), numbers, ALU.is_equal))

                    dve.wait_ge(r["consts2_made"], 2 + E)
                    top(first, best)
                    step(v.scalar_tensor_tensor(probs[:, :, :].rearrange("p t e -> p (t e)"), first[:, :, :].rearrange("p t e -> p (t e)"),
                                                -2.0, probs[:, :, :].rearrange("p t e -> p (t e)"), ALU.mult, ALU.add))
                    top(second, best2)
                    step(v.tensor_tensor(den[:, :], best[:, :], best2[:, :], ALU.add))
                    step(v.tensor_scalar(den[:, :], den[:, :], 1e-9, None, ALU.add))
                    step(v.reciprocal(den[:, :], den[:, :]))
                    step(v.tensor_tensor(best[:, :], best[:, :], den[:, :], ALU.mult))
                    step(v.tensor_tensor(best2[:, :], best2[:, :], den[:, :], ALU.mult))
                    step(v.tensor_tensor(first[:, :, :], first[:, :, :], wide(best), ALU.mult))
                    step(v.tensor_tensor(second[:, :, :], second[:, :, :], wide(best2), ALU.mult))
                    step(v.tensor_tensor(gates[:, :, :], first[:, :, :], second[:, :, :], ALU.add))

                @block.tensor
                def _(pe):
                    t = nc.tensor
                    pe.wait_ge(r["router_in"], 16)
                    t.transpose(bank[0][:, 0:E], router_nat[:, :], ident[0:E, 0:E]).then_inc(r["routerT_ready"], 1)
                    pe.wait_ge(r["routerT_copied"], 1)
                    with pe.Fori(0, B) as b:
                        def turn(c):
                            pe.wait_ge(r["x2_ready"], at(b, NC, c + 1))
                            pe.wait_ge(r["x2T_copied"], at(b, NC, max(c - 1, 0)))
                            t.transpose(bank[c % 2][:, 0:P], x2t[:, c % 2, :], ident[:, :]).then_inc(r["x2T_ready"], 1)

                        def route(c):
                            if c == 0:
                                pe.wait_ge(r["logits_drained"], at(b, 1, 0))
                            pe.wait_ge(r["x2s_ready"], at(b, NC, c + 1))
                            return t.matmul(bank[2][:, c * E:(c + 1) * E], x2s[:, c % 2, :], routerT[:, :], start=True, stop=True)

                        for c in range(NC + 1):
                            if c < NC:
                                turn(c)
                            if c:
                                last = route(c - 1)
                                if c == NC:
                                    last.then_inc(r["logits_ready"], 1)

                @block.scalar
                def _(act):
                    a_ = nc.scalar
                    with act.Fori(0, B) as b:
                        for c in range(NC):
                            act.wait_ge(r["x2T_ready"], at(b, NC, c + 1))
                            a_.activation(x2s[:, c % 2, :], bank[c % 2][:, 0:P], ACT.Copy).then_inc(r["x2s_ready"], 1)
                            a_.activation(xT_all[:, bass.ds(b * NC + c, 1), :].rearrange("p a q -> p (a q)"),
                                          bank[c % 2][:, 0:P], ACT.Copy).then_inc(r["x2T_copied"], 1)
                    act.wait_ge(r["peak_off"], 1)
                    a_.activation(expo[:, :, :], logits[:, :, :], ACT.Exp).then_inc(r["expo_ready"], 1)

        with ExitStack() as moe:
            def sb4(name, shape, dt=F32):
                return moe.enter_context(nc.sbuf_tensor(name, shape, dt))

            SUP = NT // 4
            w1n = sb4("w1n", [P, NF, P])
            w3n = sb4("w3n", [P, NF, P])
            w2n = sb4("w2n", [P, HF])
            w1T = sb4("w1T", [P, HF])
            w3T = sb4("w3T", [P, HF])
            w2T = sb4("w2T", [P, NF, P])
            act1 = sb4("act1", [P, 2, HALF])
            hT = sb4("hT", [P, 2, NF, HALF])
            m = {n: sem(n) for n in """w_in wT_made w13_copied w2_copied up_ready silu_ready hid_ready down_ready
                down_drained""".split()}
            start_at_one(m, ("w_in",))
            LASTF = FCH[-1][1]
            with nc.Block() as block:
                @block.sync
                def _(sp):
                    with sp.Fori(0, E) as e:
                        sp.wait_ge(m["wT_made"], at(e, 1, 0))
                        for w, src in ((w1n, w1), (w3n, w3)):
                            sp.dma_start(w[:, 0:NF - 1, :], src[bass.ds(e, 1), 0:(NF - 1) * P, :].rearrange("a (j p) c -> p (a j) c", p=P)
                                         ).then_inc(m["w_in"], 16)
                            sp.dma_start(w[0:LASTF, NF - 1, :], src[bass.ds(e, 1), (NF - 1) * P:HF, :].rearrange("a p c -> p (a c)")
                                         ).then_inc(m["w_in"], 16)
                        sp.dma_start(w2n[:, :], w2[bass.ds(e, 1), :, :].rearrange("a p c -> p (a c)")).then_inc(m["w_in"], 16)

                @block.tensor
                def _(pe):
                    t = nc.tensor
                    with pe.Fori(0, E) as e:
                        pe.wait_ge(m["w_in"], e * 80 + 80)
                        pe.wait_ge(m["down_drained"], at(e, SUP, 0))
                        pe.wait_ge(m["w13_copied"], at(e, 1, 0))
                        for f, n in enumerate(x[1] for x in FCH):
                            t.transpose(bank[6][:, f * P:f * P + n], w1n[0:n, f, :], ident[0:n, 0:n])
                            t.transpose(bank[7][:, f * P:f * P + n], w3n[0:n, f, :], ident[0:n, 0:n])
                            last = t.transpose(bank[4][0:n, f * P:(f + 1) * P], w2n[:, f * P:f * P + n], ident[:, :])
                        last.then_inc(m["wT_made"], 1)
                        with pe.Fori(0, SUP // 2) as s2:
                            es = e * SUP + s2 * 2

                            def up(s):
                                x_ = xT_all[:, bass.ds(s2 * 8 + 4 * s, 4), :].rearrange("p j q -> p (j q)")
                                for f, (f0, n) in enumerate(FCH):
                                    u = 3 * s + f
                                    pe.wait_ge(m["hid_ready"], at(es, NF, max(u - 1, 0)))
                                    t.matmul(bank[u % 2][0:n, :], w1T[:, f0:f0 + n], x_, start=True, stop=True)
                                    t.matmul(bank[2 + u % 2][0:n, :], w3T[:, f0:f0 + n], x_, start=True,
                                             stop=True).then_inc(m["up_ready"], 1)

                            def down(s):
                                pe.wait_ge(m["hid_ready"], at(es, NF, NF * (s + 1)))
                                pe.wait_ge(m["down_drained"], at(es, 1, max(s - 1, 0)))
                                for j in range(4):
                                    for f, (f0, n) in enumerate(FCH):
                                        last = t.matmul(bank[4 + s][:, j * P:(j + 1) * P], hT[0:n, s, f, j * P:(j + 1) * P],
                                                        w2T[0:n, f, :], start=(f == 0), stop=(f == NF - 1))
                                last.then_inc(m["down_ready"], 1)

                            pe.wait_ge(m["w13_copied"], at(e, 1, 1))
                            pe.wait_ge(m["w2_copied"], at(e, 1, 1))
                            up(0)
                            up(1)
                            down(0)
                            down(1)

                @block.scalar
                def _(act):
                    a_ = nc.scalar
                    with act.Fori(0, E) as e:
                        act.wait_ge(m["wT_made"], at(e, 1, 1))
                        act.wait_ge(m["down_ready"], at(e, SUP, 0))
                        a_.activation(w1T[:, :], bank[6][:, 0:HF], ACT.Copy)
                        a_.activation(w3T[:, :], bank[7][:, 0:HF], ACT.Copy).then_inc(m["w13_copied"], 1)
                        with act.Fori(0, SUP // 2) as s2:
                            es = e * SUP + s2 * 2
                            for u in range(2 * NF):
                                n = FCH[u % NF][1]
                                act.wait_ge(m["up_ready"], at(es, NF, u + 1))
                                act.wait_ge(m["hid_ready"], at(es, NF, max(u - 1, 0)))
                                a_.activation(act1[0:n, u % 2, :], bank[u % 2][0:n, :], ACT.Silu).then_inc(m["silu_ready"], 1)

                @block.vector
                def _(dve):
                    v = nc.vector
                    with dve.Fori(0, E) as e:
                        dve.wait_ge(m["wT_made"], at(e, 1, 1))
                        dve.wait_ge(m["down_ready"], at(e, SUP, 0))
                        v.tensor_copy(w2T[:, 0:NF - 1, :], bank[4][:, 0:(NF - 1) * P].rearrange("p (f c) -> p f c", c=P))
                        v.tensor_copy(w2T[0:LASTF, NF - 1, :], bank[4][0:LASTF, (NF - 1) * P:NF * P]).then_inc(m["w2_copied"], 1)
                        with dve.Fori(0, SUP // 2) as s2:
                            es = e * SUP + s2 * 2

                            def hidden(s):
                                for f, (f0, n) in enumerate(FCH):
                                    u = 3 * s + f
                                    dve.wait_ge(m["silu_ready"], at(es, NF, u + 1))
                                    dve.wait_ge(m["down_ready"], at(es, 1, 0))
                                    v.tensor_tensor(hT[0:n, s, f, :], act1[0:n, u % 2, :], bank[2 + u % 2][0:n, :], ALU.mult
                                                    ).then_inc(m["hid_ready"], 1)

                            def weigh(s):
                                dve.wait_ge(m["down_ready"], at(es, 1, s + 1))
                                for j in range(4):
                                    tile = t_all[:, bass.ds(s2 * 8 + 4 * s + j, 1), :].rearrange("p a q -> p (a q)")
                                    gate = gates[:, bass.ds(s2 * 8 + 4 * s + j, 1), bass.ds(e, 1)].rearrange("p a q -> p (a q)")
                                    last = v.scalar_tensor_tensor(tile, bank[4 + s][:, j * P:(j + 1) * P], gate, tile,
                                                                  ALU.mult, ALU.add)
                                last.then_inc(m["down_drained"], 1)

                            hidden(0)
                            hidden(1)
                            weigh(0)
                            weigh(1)

        with ExitStack() as fin:
            t_st = fin.enter_context(nc.sbuf_tensor("t_st", [P, NC, P], F32))
            f = {n: sem(n) for n in ("staged", "turned", "drained_scalar", "drained_vector")}
            start_at_one(f, ())
            staged, turned = f["staged"], f["turned"]
            drained = [f["drained_scalar"], f["drained_vector"]]
            stored = sem("stored")
            with nc.Block() as block:
                @block.gpsimd
                def _(pool):
                    with pool.Fori(0, B) as b:
                        pool.wait_ge(turned, at(b, 2, 0))
                        nc.gpsimd.tensor_copy(t_st[:, :, :], t_all[:, bass.ds(b * NC, NC), :]).then_inc(staged, 1)

                @block.tensor
                def _(pe):
                    with pe.Fori(0, B) as b:
                        pe.wait_ge(staged, at(b, 1, 1))
                        for hf in range(2):
                            pe.wait_ge(drained[hf], at(b, 1, 0))
                            for j in range(4):
                                last = nc.tensor.transpose(bank[hf][:, j * P:(j + 1) * P], t_st[:, 4 * hf + j, :], ident[:, :])
                            last.then_inc(turned, 1)

                @block.scalar
                def _(act):
                    with act.Fori(0, B) as b:
                        act.wait_ge(turned, at(b, 2, 1))
                        nc.scalar.activation(xT_all[:, bass.ds(b * NC, 4), :],
                                             bank[0][:, :].rearrange("p (j q) -> p j q", q=P), ACT.Copy).then_inc(drained[0], 1)

                @block.vector
                def _(dve):
                    with dve.Fori(0, B) as b:
                        dve.wait_ge(turned, at(b, 2, 2))
                        nc.vector.tensor_copy(xT_all[:, bass.ds(b * NC + 4, 4), :],
                                              bank[1][:, :].rearrange("p (j q) -> p j q", q=P)).then_inc(drained[1], 1)

                @block.sync
                def _(sp):
                    with sp.Fori(0, B) as b:
                        sp.wait_ge(drained[0], at(b, 1, 1))
                        sp.wait_ge(drained[1], at(b, 1, 1))
                        sp.dma_start(out[bass.ds(b, 1)].rearrange("b c h w -> c b (h w)"),
                                     xT_all[:, bass.ds(b * NC, NC), :].rearrange("p (a j) q -> p a (j q)", a=1)).then_inc(stored, 16)
                    sp.wait_ge(stored, B * 16)


_INS = ["x", "L0_conv_ln_w", "L0_conv_ln_b", "L0_conv_in_proj_w", "L0_conv_conv_w", "L0_conv_conv_b", "L0_conv_A_log",
        "L0_conv_D", "L0_conv_dt_bias", "L0_conv_rms_w", "L0_conv_out_proj_w", "L1_attn_Wk", "L1_attn_Wq", "L1_attn_Wv",
        "L1_attn_Wu", "L1_attn_bu", "L1_ffn_router_w", "L1_ffn_w1", "L1_ffn_w2", "L1_ffn_w3"]


def kernel(**inputs):
    import numpy as _np
    import concourse.bacc as _bacc
    from concourse import mybir as _mybir
    from concourse.bass_utils import run_bass_kernel_spmd as _run

    nc = _bacc.Bacc("TRN2", target_bir_lowering=False, num_devices=1)
    arrays, args = {}, []
    for name in _INS:
        a = _np.ascontiguousarray(inputs[name])
        arrays[f"in_{name}"] = a
        args.append(nc.dram_tensor(f"in_{name}", a.shape, _mybir.dt.from_np(a.dtype), kind="ExternalInput").ap())
    shape = inputs["x"].shape
    args.append(nc.dram_tensor("out_0", shape, _mybir.dt.float32, kind="ExternalOutput").ap())
    hybrid_kernel(nc, *args)
    r = _run(nc, [arrays], core_ids=[0])
    return r.results[0]["out_0"]
```

```python
from contextlib import ExitStack

import concourse.bass as bass
from concourse import mybir

P = 128
HALF = 512
NH = 8
HD = 32
DI = NH * HD
NS = 32
TAPS = 3
NEG = -1.0e30
EPS = 1e-5

ALU = mybir.AluOpType
ACT = mybir.ActivationFunctionType
F32 = mybir.dt.float32
F32R = mybir.dt.float32r
BF16 = mybir.dt.bfloat16
AX = mybir.AxisListType.X
DVE_STEPS = 49


def hybrid_kernel(nc, x, ln_w, ln_b, in_w, conv_w, conv_b, A_log, D, dt_bias, rms_w, out_w,
                  Wk, Wq, Wv, Wu, bu, router_w, w1, w2, w3, out):
    B, C, HH, WW = x.shape
    L = HH * WW
    NC = L // P
    NT = B * NC
    E, HF, _ = w1.shape
    RH = HH // 2
    CB = 2 * NS
    assert C == P and L == 2 * HALF and Wq.shape[0] == NH * P
    FCH = [(f, min(P, HF - f)) for f in range(0, HF, P)]
    NF = len(FCH)

    ctx = ExitStack()
    with ctx:
        def sb(name, shape, dt=F32):
            return ctx.enter_context(nc.sbuf_tensor(name, shape, dt))

        def sem(name):
            return ctx.enter_context(nc.semaphore(name))

        psum = ctx.enter_context(nc.psum_tensor("psum", [P, 8 * HALF], F32))
        bank = [psum[:, i * HALF:(i + 1) * HALF] for i in range(8)]

        def psum_pair(i, width):
            return psum[:, i * HALF:i * HALF + width]

        def at(n, per, k):
            return n * per + k + 1

        ident = sb("ident", [P, P])
        ident_bf = sb("ident_bf", [P, P], BF16)
        upto = sb("upto", [P, P])
        mask_after = sb("mask_after", [P, P], BF16)
        mask_ahead = sb("mask_ahead", [P, P], BF16)

        until_experts = ExitStack()

        def sb0(name, shape, dt=F32):
            return until_experts.enter_context(nc.sbuf_tensor(name, shape, dt))

        t_all = sb("t_all", [P, NT, P])
        xT_all = sb0("xT_all", [P, NT, P])

        wq = sb0("wq", [P, NH, P])
        wk = sb0("wk", [P, NH, P])
        wv = sb0("wv", [P, NH, P])
        wu = sb0("wu", [P, NH * P])

        consts_in = sem("consts_in")
        attn_in = sem("attn_in")
        pool_made = sem("pool_made")
        setup_T = sem("setup_T")
        setup_copied = sem("setup_copied")
        a_exp = sem("a_exp")
        a_neg = sem("a_neg")

        N_CONST = 13

        def start_at_one(sems, but):
            with nc.Block() as block:
                @block.sync
                def _(sp):
                    for name in sems:
                        if name not in but:
                            sp.sem_inc(sems[name], 1)

        scan = ExitStack()
        with scan:
            def sb1(name, shape, dt=F32):
                return scan.enter_context(nc.sbuf_tensor(name, shape, dt))

            mean_w = sb1("mean_w", [P, P])
            in_nat = sb1("in_nat", [P, 5, P])
            inT = sb1("inT", [P, 584])
            cw = sb1("cw", [P, 3, TAPS * TAPS])
            cb = sb1("cb", [P, 3])
            lnw = sb1("lnw", [P, 1])
            lnb = sb1("lnb", [P, 1])
            rmsw = sb1("rmsw", [P, 2])
            out_nat = sb1("out_nat", [P, DI])
            outT = sb1("outT", [P, 2, P])
            dtb = sb1("dtb", [P, NH])
            alog = sb1("alog", [P, NH])
            aexp = sb1("aexp", [P, NH])
            aneg = sb1("aneg", [P, NH])
            dvec = sb1("dvec", [P, NH])
            x_in_sb = sb1("x_in_sb", [P, L])
            x_st = sb1("x_st", [P, L])
            xc = sb1("xc", [P, L])
            sq = sb1("sq", [P, L])
            rstd = sb1("rstd", [P, NC])
            xn = sb1("xn", [P, L])
            pad = sb1("pad", [P, 3, HH + 2, WW + 2])
            acc = sb1("acc", [P, 3, L])
            xsC = sb1("xsC", [P, 2, L])
            BC = sb1("BC", [NS, 2, L])
            zs = sb1("zs", [P, NC, DI])
            dtr = sb1("dtr", [P, NC * NH])
            dta = sb1("dta", [P, NC * NH])
            dte = sb1("dte", [P, NC * NH])
            dtl = sb1("dtl", [P, NC * NH])
            dt = sb1("dt", [P, NC * NH])
            dA = sb1("dA", [P, NC * NH])
            nAcs = sb1("nAcs", [P, NC * NH])
            eAcs = sb1("eAcs", [P, NC * NH])
            tok = sb1("tok", [P, NC, DI + NS])
            Ldec = sb1("Ldec", [P, 2, NH, P])
            edec = sb1("edec", [NS, NC, NH])
            GL = sb1("GL", [P, 2, NH, P])
            xdt = sb1("xdt", [P, 2, DI])
            dx = sb1("dx", [P, 2, DI])
            Xd = sb1("Xd", [P, 2, DI])
            S = sb1("S", [NS, DI])
            y1 = sb1("y1", [P, 2, DI])
            ysq = sb1("ysq", [P, DI])
            ssq = sb1("ssq", [P, NC])
            rs = sb1("rs", [P, NC])
            yn = sb1("yn", [P, 2, DI])
            yT = sb1("yT", [P, 2, 2, P])
            st6 = sb1("st6", [P, 6])
            mv = sb1("mv", [P, 2, 2])
            rs2 = sb1("rs2", [P, 2])
            xnt = sb1("xnt", [P, 2, P])
            mhalf = sb1("mhalf", [P, 1])
            epst = sb1("epst", [P, 1])

            names = """x_in mean_ready xc_ready sq_ready var_ready xn_ready proj_ready pad_copied zproj_ready z_ready
                dtproj_ready dtabs_ready dte_ready dtln_ready dA_ready acs_ready nacs_ready eacs_ready conv_done
                xs_ready tok_ready tok_copied seg_ready decay_ready gl_ready xd_ready xdt_ready dx_ready st_ready
                state_ready y_ready y_drained yg_ready ssq_ready yn_ready yT_ready yT_copied t_ready t_drained
                lnx_ready xnT_ready xnT_copied xst_ready dve_step pool_step pad_zero var_drained rstd_ready rstd_rows ms_ready rs_ready mv_ready ve_ready rs2_ready""".split()
            s = {n: sem(n) for n in names}

            start_at_one(s, ("x_in", "dve_step", "pool_step", "pad_zero"))
            with nc.Block() as block:
                @block.sync
                def _(sp):
                    sp.dma_start(in_nat[:, 0:4, :], in_w[0:512, :].rearrange("(j p) c -> p j c", p=P)).then_inc(consts_in, 16)
                    sp.dma_start(in_nat[0:72, 4, :], in_w[512:584, :]).then_inc(consts_in, 16)
                    sp.dma_start(cw[:, 0:2, :], conv_w[0:256].rearrange("(j p) a h w -> p j (a h w)", p=P)).then_inc(consts_in, 16)
                    sp.dma_start(cw[0:CB, 2, :], conv_w[256:320].rearrange("p a h w -> p (a h w)")).then_inc(consts_in, 16)
                    with nc.allow_non_contiguous_dma("small vectors, one element a partition"):
                        sp.dma_start(cb[:, 0:2], conv_b[0:256].rearrange("(j p) -> p j", p=P)).then_inc(consts_in, 16)
                        sp.dma_start(cb[0:CB, 2:3], conv_b[256:320].rearrange("(p a) -> p a", a=1)).then_inc(consts_in, 16)
                        sp.dma_start(lnw[:, :], ln_w.rearrange("(p a) -> p a", a=1)).then_inc(consts_in, 16)
                        sp.dma_start(lnb[:, :], ln_b.rearrange("(p a) -> p a", a=1)).then_inc(consts_in, 16)
                        sp.dma_start(rmsw[:, :], rms_w.rearrange("(j p) -> p j", p=P)).then_inc(consts_in, 16)
                    sp.dma_start(out_nat[:, :], out_w).then_inc(consts_in, 16)
                    sp.dma_start(dtb[:, :], dt_bias.partition_broadcast(P)).then_inc(consts_in, 16)
                    sp.dma_start(alog[:, :], A_log.partition_broadcast(P)).then_inc(consts_in, 16)
                    sp.dma_start(dvec[:, :], D.partition_broadcast(P)).then_inc(consts_in, 16)
                    sp.dma_start(x_in_sb[:, :], x[0].rearrange("c h w -> c (h w)")).then_inc(s["x_in"], 16)
                    for w, src in ((wq, Wq), (wk, Wk), (wv, Wv)):
                        sp.dma_start(w[:, :, :], src.rearrange("(h o) d -> o h d", o=P)).then_inc(attn_in, 16)
                    sp.dma_start(wu[:, :], Wu).then_inc(attn_in, 16)
                    with sp.Fori(1, B) as b:
                        sp.wait_ge(s["xst_ready"], at(b, 1, 0))
                        sp.wait_ge(s["xc_ready"], at(b, 2, 0))
                        sp.dma_start(x_in_sb[:, :], x[bass.ds(b, 1)].rearrange("b c h w -> c (b h w)")).then_inc(s["x_in"], 16)

                @block.gpsimd
                def _(pool):
                    g = nc.gpsimd
                    g.memset(ident[:, :], 1.0).then_inc(s["pool_step"], 1)
                    g.memset(ident_bf[:, :], 1.0).then_inc(s["pool_step"], 1)
                    g.memset(upto[:, :], 1.0).then_inc(s["pool_step"], 1)
                    g.memset(mask_after[:, :], 0.0).then_inc(s["pool_step"], 1)
                    g.memset(mask_ahead[:, :], 0.0).then_inc(s["pool_step"], 1)
                    g.memset(mean_w[:, :], 1.0 / C).then_inc(s["pool_step"], 1)
                    g.memset(mhalf[:, :], -0.5).then_inc(s["pool_step"], 1)
                    g.memset(epst[:, :], EPS).then_inc(s["pool_step"], 1)
                    g.memset(pad[:, :, :, :], 0.0).then_inc(s["pad_zero"], 1)
                    pool.wait_ge(s["pool_step"], 8)
                    for m in (ident, ident_bf):
                        g.affine_select(out=m[:, :], in_=m[:, :], compare_op=ALU.is_equal, fill=0.0, base=0,
                                        pattern=[[-1, P]], channel_multiplier=1).then_inc(pool_made, 1)
                    g.affine_select(out=upto[:, :], in_=upto[:, :], compare_op=ALU.is_ge, fill=0.0, base=0,
                                    pattern=[[1, P]], channel_multiplier=-1).then_inc(pool_made, 1)
                    g.affine_select(out=mask_after[:, :], in_=mask_after[:, :], compare_op=ALU.is_ge, fill=NEG, base=0,
                                    pattern=[[1, P]], channel_multiplier=-1).then_inc(pool_made, 1)
                    g.affine_select(out=mask_ahead[:, :], in_=mask_ahead[:, :], compare_op=ALU.is_ge, fill=NEG, base=0,
                                    pattern=[[-1, P]], channel_multiplier=1).then_inc(pool_made, 1)
                    pool.wait_ge(consts_in, 16 * N_CONST)
                    def power(t, ready):
                        return g.tensor_tensor(t, t, mhalf[:, 0:1].to_broadcast([P, t.shape[1]]), ALU.pow).then_inc(ready, 1)

                    with pool.Fori(0, B) as b:
                        pool.wait_ge(s["var_drained"], at(b, 1, 1))
                        power(rstd[:, :], s["rstd_ready"])

                        def chunk_in(c):
                            pool.wait_ge(s["tok_copied"], at(b, NC, c + 1))
                            pool.wait_ge(s["y_ready"], at(b, NC, max(c - 1, 0)))
                            pool.wait_ge(s["xd_ready"], at(b, NC, max(c - 1, 0)))
                            xs3 = tok[:, c, 0:DI].rearrange("p (h d) -> p h d", d=HD)
                            g.tensor_tensor(xdt[:, c % 2, :].rearrange("p (h d) -> p h d", d=HD), xs3,
                                            dt[:, c * NH:(c + 1) * NH].unsqueeze(2).to_broadcast([P, NH, HD]), ALU.mult
                                            ).then_inc(s["xdt_ready"], 1)
                            pool.wait_ge(s["yg_ready"], at(b, NC, max(c - 1, 0)))
                            g.tensor_tensor(dx[:, c % 2, :].rearrange("p (h d) -> p h d", d=HD), xs3,
                                            dvec[:, :].unsqueeze(2).to_broadcast([P, NH, HD]), ALU.mult
                                            ).then_inc(s["dx_ready"], 1)

                        def chunk_rs(c):
                            pool.wait_ge(s["ssq_ready"], at(b, NC, c + 1))
                            if c == 0:
                                pool.wait_ge(s["yn_ready"], at(b, NC, 0))
                            g.tensor_tensor(rs[:, c:c + 1], ssq[:, c:c + 1], epst[:, :], ALU.add
                                            ).then_inc(s["ms_ready"], 1)
                            pool.wait_ge(s["ms_ready"], at(b, NC, c + 1))
                            power(rs[:, c:c + 1], s["rs_ready"])

                        def chunk_rs2(c):
                            pool.wait_ge(s["mv_ready"], at(b, NC, c + 1))
                            pool.wait_ge(s["lnx_ready"], at(b, NC, max(c - 1, 0)))
                            g.tensor_tensor(rs2[:, c % 2:c % 2 + 1], mv[:, c % 2, 1:2], epst[:, :], ALU.add
                                            ).then_inc(s["ve_ready"], 1)
                            pool.wait_ge(s["ve_ready"], at(b, NC, c + 1))
                            power(rs2[:, c % 2:c % 2 + 1], s["rs2_ready"])

                        for step in range(NC + 4):
                            for f, lag in ((chunk_in, 0), (chunk_rs, 2), (chunk_rs2, 4)):
                                if 0 <= step - lag < NC:
                                    f(step - lag)

                @block.tensor
                def _(pe):
                    t = nc.tensor
                    pe.wait_ge(pool_made, 5)
                    pe.wait_ge(consts_in, 16 * N_CONST)
                    for j in range(5):
                        n = P if j < 4 else 72
                        if j >= 2:
                            pe.wait_ge(setup_copied, j - 1)
                        t.transpose(bank[j % 2][:, 0:n], in_nat[0:n, j, :], ident[0:n, 0:n]).then_inc(setup_T, 1)
                    for j in range(2):
                        pe.wait_ge(setup_copied, 4 + j)
                        t.transpose(bank[(5 + j) % 2][:, 0:P], out_nat[:, j * P:(j + 1) * P], ident[:, :]).then_inc(setup_T, 1)
                    pe.wait_ge(setup_copied, 7)
                    with pe.Fori(0, B) as b:
                        pe.wait_ge(s["x_in"], b * 16 + 16)
                        pe.wait_ge(s["gl_ready"], at(b, NC, 0))
                        for hf in range(2):
                            t.matmul(bank[hf][:, :], mean_w[:, :],
                                     x_in_sb[:, hf * HALF:(hf + 1) * HALF],
                                     start=True, stop=True).then_inc(s["mean_ready"], 1)
                        pe.wait_ge(s["sq_ready"], at(b, 2, 2))
                        for c in range(NC):
                            last = t.matmul(bank[0][:, c:c + 1], sq[:, c * P:(c + 1) * P], mean_w[:, 0:1], start=True, stop=True)
                        last.then_inc(s["var_ready"], 1)
                        pe.wait_ge(s["rstd_ready"], at(b, 1, 1))
                        for c in range(NC):
                            last = t.matmul(bank[c // 4][:, (c % 4) * P:(c % 4 + 1) * P], rstd[:, c:c + 1].to_broadcast([P, P]),
                                            ident[:, :], start=True, stop=True)
                            if c % 4 == 3:
                                last.then_inc(s["rstd_rows"], 1)
                        pe.wait_ge(s["decay_ready"], at(b, NC, 0))
                        for u in range(6):
                            hf, m = u // 3, u % 3
                            n = P if m < 2 else CB
                            pe.wait_ge(s["xn_ready"], at(b, 2, hf + 1))
                            if u >= 2:
                                pe.wait_ge(s["pad_copied"], at(b, 6, u - 1))
                            t.matmul(bank[2 + u % 2][0:n, :], inT[:, DI + m * P:DI + m * P + n],
                                     xn[:, hf * HALF:(hf + 1) * HALF], start=True, stop=True).then_inc(s["proj_ready"], 1)
                        pe.wait_ge(s["yT_copied"], at(b, NC, 0))
                        pe.wait_ge(s["xnT_copied"], at(b, NC, 0))
                        for c in range(NC):
                            last = t.matmul(bank[6][:, c * NH:(c + 1) * NH], xn[:, c * P:(c + 1) * P], inT[:, 576:584],
                                            start=True, stop=True)
                        last.then_inc(s["dtproj_ready"], 1)
                        pe.wait_ge(s["y_drained"], at(b, NC, 0))
                        pe.wait_ge(s["state_ready"], at(b, NC, 0))
                        for c in range(NC):
                            if c >= 2:
                                pe.wait_ge(s["z_ready"], at(b, NC, c - 1))
                            t.matmul(bank[4 + c % 2][:, 0:DI], xn[:, c * P:(c + 1) * P], inT[:, 0:DI],
                                     start=True, stop=True).then_inc(s["zproj_ready"], 1)
                        pe.wait_ge(s["dA_ready"], at(b, 1, 1))
                        t.matmul(bank[6][:, 64:128], upto[:, :], dA[:, :], start=True, stop=True).then_inc(s["acs_ready"], 1)

                        def chunk_in(c):
                            sl = slice(c * P, (c + 1) * P)
                            pb = bank[c % 2]
                            if c == 0:
                                pe.wait_ge(s["xs_ready"], at(b, 4, 4))
                            if c >= 2:
                                pe.wait_ge(s["gl_ready"], at(b, NC, c - 1))
                            for m in range(2):
                                t.transpose(pb[:, m * P:(m + 1) * P], xsC[:, m, sl], ident[:, :])
                            t.transpose(pb[:, DI:DI + NS], BC[:, 0, sl], ident[0:NS, 0:NS])
                            t.matmul(pb[:, 384:512], BC[:, 0, sl], BC[:, 1, sl], start=True, stop=True).then_inc(s["tok_ready"], 1)
                            if c == 0:
                                pe.wait_ge(s["pad_copied"], at(b, 6, 6))
                            else:
                                pe.wait_ge(s["decay_ready"], at(b, NC, c))
                            for j in range(2):
                                seg = bank[2 + j]
                                t.matmul(seg[:, :].rearrange("p (h q) -> p h q", q=P), ident_bf[:, :],
                                         mask_after[:, :].unsqueeze(1).to_broadcast([P, 4, P]), start=True, stop=False)
                                for h in range(4):
                                    col = c * NH + 4 * j + h
                                    last = t.matmul(seg[:, h * P:(h + 1) * P], dA[:, col:col + 1].to_broadcast([P, P]),
                                                    upto[:, :], start=False, stop=(h == 3))
                            last.then_inc(s["seg_ready"], 1)

                        def chunk_y(c):
                            sl = slice(c * P, (c + 1) * P)
                            pe.wait_ge(s["xd_ready"], at(b, NC, c + 1))
                            if c == 0:
                                pe.wait_ge(s["z_ready"], at(b, NC, NC))
                            else:
                                pe.wait_ge(s["state_ready"], at(b, NC, c))
                            t.matmul(bank[5][0:NS, 0:DI], tok[:, c, DI:DI + NS], Xd[:, c % 2, :], start=True,
                                     stop=True).then_inc(s["st_ready"], 1)
                            pe.wait_ge(s["y_drained"], at(b, NC, c))
                            pe.wait_ge(s["gl_ready"], at(b, NC, c + 1))
                            pe.wait_ge(s["xdt_ready"], at(b, NC, c + 1))
                            for h in range(NH):
                                last = t.matmul(bank[4][:, DI + h * HD:DI + (h + 1) * HD], GL[:, c % 2, h, :],
                                                xdt[:, c % 2, h * HD:(h + 1) * HD], start=True, stop=True)
                            if c:
                                last = t.matmul(bank[4][:, 0:DI], BC[:, 1, sl], S[:, :], start=True, stop=True)
                            last.then_inc(s["y_ready"], 1)

                        def chunk_yT(c):
                            pe.wait_ge(s["yn_ready"], at(b, NC, c + 1))
                            if c == 0:
                                pe.wait_ge(s["nacs_ready"], at(b, 1, 1))
                            if c >= 4:
                                pe.wait_ge(s["xnT_copied"], at(b, NC, c - 3))
                            pe.wait_ge(s["yT_copied"], at(b, NC, c))
                            for j in range(2):
                                last = t.transpose(bank[6][:, j * P:(j + 1) * P], yn[:, c % 2, j * P:(j + 1) * P], ident[:, :])
                            last.then_inc(s["yT_ready"], 1)

                        def chunk_out(c):
                            if c == 0:
                                pe.wait_ge(s["xst_ready"], at(b, 1, 1))
                            pe.wait_ge(s["t_drained"], at(b, NC, c))
                            pe.wait_ge(s["yT_copied"], at(b, NC, c + 1))
                            t.matmul(bank[7][:, 0:P], x_st[:, c * P:(c + 1) * P], ident[:, :], start=True, stop=False)
                            t.matmul(bank[7][:, 0:P], yT[:, c % 2, 0, :], outT[:, 0, :], start=False, stop=False)
                            t.matmul(bank[7][:, 0:P], yT[:, c % 2, 1, :], outT[:, 1, :], start=False,
                                     stop=True).then_inc(s["t_ready"], 1)

                        def chunk_xnT(c):
                            pe.wait_ge(s["lnx_ready"], at(b, NC, c + 1))
                            pe.wait_ge(s["yT_copied"], at(b, NC, min(c + 4, NC)))
                            pe.wait_ge(s["xnT_copied"], at(b, NC, c))
                            t.transpose(bank[6][:, 256:384], xnt[:, c % 2, :], ident[:, :]).then_inc(s["xnT_ready"], 1)

                        for step in range(NC + 6):
                            for f, lag in ((chunk_in, 0), (chunk_y, 1), (chunk_yT, 3), (chunk_out, 4), (chunk_xnT, 6)):
                                if 0 <= step - lag < NC:
                                    f(step - lag)
                    pe.wait_ge(s["xnT_copied"], B * NC + 1)

                @block.scalar
                def _(act):
                    a = nc.scalar
                    act.wait_ge(consts_in, 16 * N_CONST)
                    a.activation(aexp[:, :], alog[:, :], ACT.Exp).then_inc(a_exp, 1)
                    act.wait_ge(s["pad_zero"], 1)
                    with act.Fori(0, B) as b:
                        for hf in range(2):
                            act.wait_ge(s["xc_ready"], at(b, 2, hf + 1))
                            a.activation(sq[:, hf * HALF:(hf + 1) * HALF], xc[:, hf * HALF:(hf + 1) * HALF],
                                         ACT.Square).then_inc(s["sq_ready"], 1)
                        act.wait_ge(s["conv_done"], at(b, 3, 0))
                        for u in range(6):
                            hf, m = u // 3, u % 3
                            n = P if m < 2 else CB
                            act.wait_ge(s["proj_ready"], at(b, 6, u + 1))
                            a.activation(pad[0:n, m, 1 + hf * RH:1 + (hf + 1) * RH, 1:1 + WW],
                                         bank[2 + u % 2][0:n, :].rearrange("p (h w) -> p h w", w=WW),
                                         ACT.Copy).then_inc(s["pad_copied"], 1)
                        act.wait_ge(s["t_ready"], at(b, NC, 0))
                        a.activation(x_st[:, :], x_in_sb[:, :], ACT.Copy).then_inc(s["xst_ready"], 1)
                        act.wait_ge(s["yg_ready"], at(b, NC, 0))
                        for c in range(NC):
                            act.wait_ge(s["zproj_ready"], at(b, NC, c + 1))
                            a.activation(zs[:, c, :], bank[4 + c % 2][:, 0:DI], ACT.Silu).then_inc(s["z_ready"], 1)
                        act.wait_ge(s["dtabs_ready"], at(b, 1, 1))
                        a.activation(dte[:, :], dta[:, :], ACT.Exp, scale=-1.0).then_inc(s["dte_ready"], 1)
                        act.wait_ge(s["dte_ready"], at(b, 1, 1))
                        a.activation(dtl[:, :], dte[:, :], ACT.Ln, bias=1.0).then_inc(s["dtln_ready"], 1)
                        act.wait_ge(s["tok_ready"], at(b, NC, 0))
                        act.wait_ge(s["y_ready"], at(b, NC, 0))
                        for m in range(2):
                            act.wait_ge(s["conv_done"], at(b, 3, m + 1))
                            a.activation(xsC[:, m, :], acc[:, m, :], ACT.Silu, bias=cb[:, m:m + 1]).then_inc(s["xs_ready"], 1)
                        act.wait_ge(s["conv_done"], at(b, 3, 3))
                        for j in range(2):
                            a.activation(BC[:, j, :], acc[j * NS:(j + 1) * NS, 2, :], ACT.Silu,
                                         bias=cb[j * NS:(j + 1) * NS, 2:3]).then_inc(s["xs_ready"], 1)
                        act.wait_ge(s["nacs_ready"], at(b, 1, 1))
                        a.activation(eAcs[:, :], nAcs[:, :], ACT.Exp, scale=-1.0).then_inc(s["eacs_ready"], 1)

                        def chunk_in(c):
                            if c == 0:
                                act.wait_ge(s["st_ready"], at(b, NC, 0))
                                act.wait_ge(s["dx_ready"], at(b, NC, 0))
                            act.wait_ge(s["tok_ready"], at(b, NC, c + 1))
                            a.activation(tok[:, c, :], bank[c % 2][:, 0:DI + NS], ACT.Copy).then_inc(s["tok_copied"], 1)
                            act.wait_ge(s["seg_ready"], at(b, NC, c + 1))
                            act.wait_ge(s["xd_ready"], at(b, NC, max(c - 1, 0)))
                            act.wait_ge(s["gl_ready"], at(b, NC, max(c - 1, 0)))
                            for h in range(NH):
                                a.activation(Ldec[:, c % 2, h, :], bank[2 + h // 4][:, (h % 4) * P:(h % 4 + 1) * P], ACT.Exp,
                                             bias=nAcs[:, c * NH + h:c * NH + h + 1])
                            if c == 0:
                                act.wait_ge(s["state_ready"], at(b, NC, 0))
                            for j in range(2):
                                last = a.activation(edec[:, c, 4 * j:4 * j + 4],
                                                    bank[2 + j][0:NS, :].rearrange("p (h q) -> p h q", q=P)[:, :, P - 1],
                                                    ACT.Exp)
                            last.then_inc(s["decay_ready"], 1)

                        def chunk_sq(c):
                            act.wait_ge(s["yg_ready"], at(b, NC, c + 1))
                            if c == 0:
                                act.wait_ge(s["yn_ready"], at(b, NC, 0))
                            act.wait_ge(s["ssq_ready"], at(b, NC, c))
                            a.activation(ysq[:, :], y1[:, c % 2, :], ACT.Square, scale=DI ** -0.5,
                                         accum_out=ssq[:, c:c + 1]).then_inc(s["ssq_ready"], 1)

                        def chunk_yT(c):
                            act.wait_ge(s["yT_ready"], at(b, NC, c + 1))
                            act.wait_ge(s["t_ready"], at(b, NC, max(c - 1, 0)))
                            a.activation(yT[:, c % 2, :, :], bank[6][:, 0:256].rearrange("p (j q) -> p j q", q=P),
                                         ACT.Copy).then_inc(s["yT_copied"], 1)

                        def chunk_xnT(c):
                            act.wait_ge(s["xnT_ready"], at(b, NC, c + 1))
                            a.activation(xT_all[:, bass.ds(b * NC + c, 1), :].rearrange("p a q -> p (a q)"),
                                         bank[6][:, 256:384], ACT.Copy).then_inc(s["xnT_copied"], 1)

                        for step in range(NC + 6):
                            for f, lag in ((chunk_in, 0), (chunk_sq, 2), (chunk_yT, 3), (chunk_xnT, 6)):
                                if 0 <= step - lag < NC:
                                    f(step - lag)

                @block.vector
                def _(dve):
                    v = nc.vector
                    for j in range(5):
                        n = P if j < 4 else 72
                        dve.wait_ge(setup_T, j + 1)
                        v.tensor_copy(inT[:, j * P:j * P + n], bank[j % 2][:, 0:n]).then_inc(setup_copied, 1)
                    for j in range(2):
                        dve.wait_ge(setup_T, 6 + j)
                        v.tensor_scalar(outT[:, j, :], bank[(5 + j) % 2][:, 0:P], rmsw[:, j:j + 1], None,
                                        ALU.mult).then_inc(setup_copied, 1)
                    dve.wait_ge(a_exp, 1)
                    v.tensor_scalar(aneg[:, :], aexp[:, :], -1.0, None, ALU.mult).then_inc(a_neg, 1)
                    dve.wait_ge(a_neg, 1)
                    dve.wait_ge(s["x_in"], 16)
                    PER = DVE_STEPS
                    with dve.Fori(0, B) as b:
                        k = [0]

                        def link(ins):
                            k[0] += 1
                            ins.then_inc(s["dve_step"], 1)
                            dve.wait_ge(s["dve_step"], b * PER + k[0])

                        for hf in range(2):
                            sl = slice(hf * HALF, (hf + 1) * HALF)
                            dve.wait_ge(s["mean_ready"], at(b, 2, hf + 1))
                            v.tensor_tensor(xc[:, sl], x_in_sb[:, sl],
                                            bank[hf][:, :], ALU.subtract).then_inc(s["xc_ready"], 1)
                        dve.wait_ge(s["zproj_ready"], at(b, NC, 0))
                        dve.wait_ge(s["xc_ready"], at(b, 2, 2))
                        dve.wait_ge(s["var_ready"], at(b, 1, 1))
                        v.tensor_scalar(rstd[:, :], bank[0][:, 0:NC], EPS, None, ALU.add).then_inc(s["var_drained"], 1)
                        for hf in range(2):
                            sl = slice(hf * HALF, (hf + 1) * HALF)
                            dve.wait_ge(s["rstd_rows"], at(b, 2, hf + 1))
                            link(v.tensor_tensor(xn[:, sl], xc[:, sl], bank[hf][:, :], ALU.mult))
                            v.tensor_scalar(xn[:, sl], xn[:, sl], lnw[:, :], lnb[:, :], ALU.mult, ALU.add
                                            ).then_inc(s["xn_ready"], 1)
                        dve.wait_ge(s["dtproj_ready"], at(b, 1, 1))
                        link(v.tensor_tensor(dtr[:, :].rearrange("p (c h) -> p c h", h=NH),
                                             bank[6][:, 0:NC * NH].rearrange("p (c h) -> p c h", h=NH),
                                             dtb[:, :].unsqueeze(1).to_broadcast([P, NC, NH]), ALU.add))
                        v.scalar_tensor_tensor(dta[:, :], dtr[:, :], -1.0, dtr[:, :], ALU.mult, ALU.max
                                               ).then_inc(s["dtabs_ready"], 1)

                        def conv(m):
                            n = P if m < 2 else CB
                            dst = acc[0:n, m, :].rearrange("p (h w) -> p h w", w=WW)
                            for tap in range(TAPS * TAPS):
                                r, c0 = tap // TAPS, tap % TAPS
                                win = pad[0:n, m, r:r + HH, c0:c0 + WW]
                                if tap == 0:
                                    ins = v.tensor_scalar(dst, win, cw[0:n, m, 0:1], None, ALU.mult)
                                else:
                                    ins = v.scalar_tensor_tensor(dst, win, cw[0:n, m, tap:tap + 1], dst, ALU.mult, ALU.add)
                                if tap < TAPS * TAPS - 1:
                                    link(ins)
                            ins.then_inc(s["conv_done"], 1)

                        dve.wait_ge(s["pad_copied"], at(b, 6, 6))
                        dve.wait_ge(s["xs_ready"], at(b, 4, 0))
                        conv(0)
                        dve.wait_ge(s["dtln_ready"], at(b, 1, 1))
                        dve.wait_ge(s["xdt_ready"], at(b, NC, 0))
                        link(v.scalar_tensor_tensor(dt[:, :], dtr[:, :], 0.0, dtl[:, :], ALU.max, ALU.add))
                        dve.wait_ge(s["seg_ready"], at(b, NC, 0))
                        v.tensor_tensor(dA[:, :].rearrange("p (c h) -> p c h", h=NH),
                                        dt[:, :].rearrange("p (c h) -> p c h", h=NH),
                                        aneg[:, :].unsqueeze(1).to_broadcast([P, NC, NH]), ALU.mult).then_inc(s["dA_ready"], 1)
                        conv(1)
                        conv(2)
                        dve.wait_ge(s["acs_ready"], at(b, 1, 1))
                        dve.wait_ge(s["decay_ready"], at(b, NC, 0))
                        v.tensor_scalar(nAcs[:, :], bank[6][:, 64:128], -1.0, None, ALU.mult).then_inc(s["nacs_ready"], 1)

                        def chunk_norm(c):
                            dve.wait_ge(s["rs_ready"], at(b, NC, c + 1))
                            dve.wait_ge(s["yT_ready"], at(b, NC, max(c - 1, 0)))
                            v.tensor_scalar(yn[:, c % 2, :], y1[:, c % 2, :], rs[:, c:c + 1], None, ALU.mult
                                            ).then_inc(s["yn_ready"], 1)

                        def chunk_in(c):
                            dve.wait_ge(s["decay_ready"], at(b, NC, c + 1))
                            dve.wait_ge(s["tok_copied"], at(b, NC, c + 1))
                            dve.wait_ge(s["y_ready"], at(b, NC, max(c - 1, 0)))
                            v.tensor_tensor(GL[:, c % 2, :, :], Ldec[:, c % 2, :, :],
                                            bank[c % 2][:, 384:512].unsqueeze(1).to_broadcast([P, NH, P]), ALU.mult
                                            ).then_inc(s["gl_ready"], 1)
                            dve.wait_ge(s["xdt_ready"], at(b, NC, c + 1))
                            dve.wait_ge(s["st_ready"], at(b, NC, max(c - 1, 0)))
                            v.tensor_tensor(Xd[:, c % 2, :].rearrange("p (h d) -> p h d", d=HD),
                                            xdt[:, c % 2, :].rearrange("p (h d) -> p h d", d=HD),
                                            Ldec[:, c % 2, :, P - 1:P].to_broadcast([P, NH, HD]), ALU.mult
                                            ).then_inc(s["xd_ready"], 1)

                        def chunk_y(c):
                            dve.wait_ge(s["st_ready"], at(b, NC, c + 1))
                            dve.wait_ge(s["y_ready"], at(b, NC, c + 1))
                            if c == 0:
                                v.tensor_copy(S[:, :], bank[5][0:NS, 0:DI]).then_inc(s["state_ready"], 1)
                                dve.wait_ge(s["dx_ready"], at(b, NC, c + 1))
                                ins = v.tensor_tensor(y1[:, c % 2, :], bank[4][:, DI:2 * DI], dx[:, c % 2, :], ALU.add)
                                ins.then_inc(s["y_drained"], 1)
                                dve.wait_ge(s["y_drained"], at(b, NC, c + 1))
                            else:
                                link(v.tensor_tensor(S[:, :].rearrange("p (h d) -> p h d", d=HD),
                                                     S[:, :].rearrange("p (h d) -> p h d", d=HD),
                                                     edec[:, c, :].unsqueeze(2).to_broadcast([NS, NH, HD]), ALU.mult))
                                v.tensor_tensor(S[:, :], S[:, :], bank[5][0:NS, 0:DI], ALU.add).then_inc(s["state_ready"], 1)
                                if c == 1:
                                    dve.wait_ge(s["eacs_ready"], at(b, 1, 1))
                                link(v.tensor_tensor(y1[:, c % 2, :].rearrange("p (h d) -> p h d", d=HD),
                                                     bank[4][:, 0:DI].rearrange("p (h d) -> p h d", d=HD),
                                                     eAcs[:, c * NH:(c + 1) * NH].unsqueeze(2).to_broadcast([P, NH, HD]), ALU.mult))
                                ins = v.tensor_tensor(y1[:, c % 2, :], y1[:, c % 2, :], bank[4][:, DI:2 * DI], ALU.add)
                                ins.then_inc(s["y_drained"], 1)
                                dve.wait_ge(s["y_drained"], at(b, NC, c + 1))
                                dve.wait_ge(s["dx_ready"], at(b, NC, c + 1))
                                link(v.tensor_tensor(y1[:, c % 2, :], y1[:, c % 2, :], dx[:, c % 2, :], ALU.add))
                            if c == 0:
                                dve.wait_ge(s["z_ready"], at(b, NC, NC))
                            v.tensor_tensor(y1[:, c % 2, :], y1[:, c % 2, :], zs[:, c, :], ALU.mult).then_inc(s["yg_ready"], 1)

                        def chunk_ln(c):
                            tile = t_all[:, bass.ds(b * NC + c, 1), :].rearrange("p a q -> p (a q)")
                            dve.wait_ge(s["ve_ready"], at(b, NC, max(c - 1, 0)))
                            dve.wait_ge(s["t_ready"], at(b, NC, c + 1))
                            v.tensor_copy(tile, bank[7][:, 0:P]).then_inc(s["t_drained"], 1)
                            dve.drain()
                            v.bn_stats(st6[:, :], tile)
                            dve.drain()
                            v.bn_aggr(mv[:, c % 2, :], st6[:, :]).then_inc(s["mv_ready"], 1)

                        def chunk_lnx(c):
                            tile = t_all[:, bass.ds(b * NC + c, 1), :].rearrange("p a q -> p (a q)")
                            dve.wait_ge(s["rs2_ready"], at(b, NC, c + 1))
                            dve.wait_ge(s["xnT_ready"], at(b, NC, max(c - 1, 0)))
                            v.tensor_scalar(xnt[:, c % 2, :], tile, mv[:, c % 2, 0:1], rs2[:, c % 2:c % 2 + 1], ALU.subtract, ALU.mult
                                            ).then_inc(s["lnx_ready"], 1)

                        for step in range(NC + 5):
                            for f, lag in ((chunk_norm, 3), (chunk_in, 0), (chunk_y, 1), (chunk_ln, 4), (chunk_lnx, 5)):
                                if 0 <= step - lag < NC:
                                    f(step - lag)
                        assert k[0] == PER, k[0]


        with ExitStack() as attn:
            def sb2(name, shape, dt=F32):
                return attn.enter_context(nc.sbuf_tensor(name, shape, dt))

            wuT = sb2("wuT", [P, NH, P])
            w_raw = sb2("w_raw", [P, 2, P])
            qk_w = sb2("qk_w", [P, NH, 2, P], F32R)
            vu_w = sb2("vu_w", [P, NH, P])
            qk_st = sb2("qk_st", [P, 2, P], F32R)
            vu_st = sb2("vu_st", [P, P])
            bu_col = sb2("bu_col", [P, 1])
            x_at = wq[:, :, :].rearrange("p h d -> p (h d)")
            xT = sb2("xT", [P, 2, L], F32R)
            x_tok = sb2("x_tok", [P, NC, P])
            qT = sb2("qT", [P, 2, L], F32R)
            prob = sb2("prob", [P, 4, L])
            probT = [sb2("probT0", [P, NC // 2, HALF]), sb2("probT1", [P, NC, HALF])]
            att = sb2("att", [P, 2, HALF])
            oT = sb2("oT", [P, L])
            nmax = sb2("nmax", [P, NC])
            rsum = sb2("rsum", [P, NC])
            rinv = sb2("rinv", [P, NC])

            a = {n: sem(n) for n in """w_filled w_copied w_high bu_in x_at_ready xT_ready qk_st_ready vu_st_ready
                bank4_filled bank5_filled bank4_drained bank5_drained u_filled u_drained
                q_filled q_high q_drained o_filled o_drained scores_ready nmax_ready prob_ready rinv_ready
                scaled""".split()}
            start_at_one(a, ("w_filled", "w_copied", "w_high", "bu_in"))
            t_filled = [a["bank4_filled"], a["bank5_filled"]]
            t_drained = [a["bank4_drained"], a["bank5_drained"]]

            GROUPS = [(i, g) for i in range(NC) for g in range(0, i + 1, 4)]
            PER_HEAD = len(GROUPS)
            assert PER_HEAD % 2 == 0
            PER_IMAGE = PER_HEAD // 2 * NH + 2

            def turned(b, h, i, k):
                n = sum(1 for x in GROUPS if x[0] <= i)
                return at(b, PER_IMAGE, 1 + h * (PER_HEAD // 2) + (n + 1 - k) // 2)

            STEPS = [
                [("T", "last", 5), ("U", "last", 0, 2, 4)],
                [("T", "last", 6), ("O", "last", 0)],
                [("T", "last", 7)],
                [("T", "this", 0), ("U", "last", 1, 0, 2)],
                [("T", "this", 1), ("U", "last", 1, 2, 4)],
                [("T", "this", 2), ("U", "last", 1, 4, 6)],
                [("T", "this", 3), ("U", "last", 1, 6, 8), ("Q", "next", 0)],
                [("T", "this", 4), ("U", "this", 0, 0, 2), ("O", "last", 1), ("Q", "next", 1)],
            ]

            def items(step, h, skipped):
                for kind, whose, *rest in STEPS[step]:
                    if whose not in skipped:
                        yield kind, {"last": h - 1, "this": h, "next": h + 1}[whose], rest

            def heads(engine, b, head):
                head(b, 0, ("last",))
                head(b, 1, ())
                with engine.Fori(2, NH - 1) as h:
                    head(b, h, ())
                head(b, NH - 1, ("next",))
                head(b, NH, ("this", "next"))

            with nc.Block() as block:
                @block.sync
                def _(sp):
                    sp.dma_start(bu_col[:, :], bu.rearrange("(n a) -> n a", a=1)).then_inc(a["bu_in"], 16)

                @block.gpsimd
                def _(pool):
                    g_ = nc.gpsimd

                    def scale(hh, i):
                        w = (i + 1) * P
                        pool.wait_ge(a["rinv_ready"], at(hh, NC, i + 1))
                        g_.tensor_tensor(prob[:, i % 4, 0:w], prob[:, i % 4, 0:w], rinv[:, i:i + 1].to_broadcast([P, w]),
                                         ALU.mult).then_inc(a["scaled"], 1)

                    with pool.Fori(0, B * NH) as hh:
                        for i in range(NC):
                            scale(hh, i)

                @block.tensor
                def _(pe):
                    t = nc.tensor

                    def mm3(out_, left, right, start, stop):
                        t.matmul(out_, left[1], right[0], start=start, stop=False)
                        t.matmul(out_, left[0], right[1], start=False, stop=False)
                        return t.matmul(out_, left[0], right[0], start=False, stop=stop)

                    def parts(x, *where):
                        return x[(slice(None), 0) + where], x[(slice(None), 1) + where]

                    pe.wait_ge(attn_in, 16 * 4)
                    for h in range(NH):
                        if h >= 2:
                            pe.wait_ge(a["w_copied"], h - 1)
                        t.transpose(bank[h % 2][:, 0:P], wu[:, h * P:(h + 1) * P], ident[:, :]).then_inc(a["w_filled"], 1)
                    for h in range(NH):
                        pe.wait_ge(a["w_copied"], NH + max(h - 1, 0))
                        t.matmul(bank[h % 2][:, 0:P], wq[:, h, :], wk[:, h, :], start=True, stop=True)
                        t.matmul(bank[h % 2][:, P:2 * P], wv[:, h, :], wuT[:, h, :], start=True,
                                 stop=True).then_inc(a["w_filled"], 1)

                    def scores(b, h, i):
                        if i in (0, 4):
                            pe.wait_ge(a["q_drained"], at(b, 2 * NH, 2 * h + i // 4 + 1))
                        before = max(i - 1, 0) if isinstance(h, int) and h == 0 else i - 1
                        pe.wait_ge(a["prob_ready"], at(b * NH + h, NC, before))
                        w = (i + 1) * P
                        for j in range((w + HALF - 1) // HALF):
                            n = min(HALF, w - j * HALF)
                            diag = i * P - j * HALF
                            last_j = w <= (j + 1) * HALF
                            last = mm3(bank[2 * (i % 2) + j][:, 0:n], parts(qT, slice(i * P, (i + 1) * P)),
                                       parts(xT, slice(j * HALF, j * HALF + n)), True, not last_j)
                            if last_j:
                                last = t.matmul(bank[2 * (i % 2) + j][:, diag:diag + P], ident_bf[:, :],
                                                mask_ahead[:, :], start=False, stop=True)
                        last.then_inc(a["scores_ready"], 1)

                    def turn(b, h, i):
                        pe.wait_ge(a["scaled"], at(b * NH + h, NC, i + 1))
                        for n, (i_, g) in enumerate(GROUPS):
                            if i_ == i:
                                k = n % 2
                                pe.wait_ge(t_drained[k], at(b, PER_IMAGE, 1 + h * (PER_HEAD // 2) + n // 2))
                                for kt in range(g, min(g + 4, i + 1)):
                                    last = t.transpose(bank[4 + k][:, (kt - g) * P:(kt - g + 1) * P],
                                                       prob[:, i % 4, kt * P:(kt + 1) * P], ident[:, :])
                                last.then_inc(t_filled[k], 1)

                    def attend(b, h, half, kt0, kt1):
                        if kt0 == 0:
                            pe.wait_ge(a["u_drained"], at(b, 2 * NH, 2 * h + half))
                            for k in range(2):
                                pe.wait_ge(t_drained[k], turned(b, h, 4 * half + 3, k))
                        for kt in range(kt0, kt1):
                            q0 = max(0, kt - 4 * half) * P
                            last = t.matmul(bank[6][:, q0:HALF], x_tok[:, kt, :], probT[half][:, kt, q0:HALF],
                                            start=kt == 0, stop=kt == 4 * half + 3)
                        if kt1 == 4 * half + 4:
                            last.then_inc(a["u_filled"], 1)

                    def output(b, h, half, next_q):
                        pe.wait_ge(a["q_drained"], at(b, 2 * NH, next_q))
                        pe.wait_ge(a["o_drained"], at(b, 2 * NH, 2 * h + half))
                        pe.wait_ge(a["vu_st_ready"], at(b, NH, h + 1))
                        pe.wait_ge(a["u_drained"], at(b, 2 * NH, 2 * h + half + 1))
                        t.matmul(bank[7][:, :], vu_st[:, :], att[:, half, :], start=True, stop=True).then_inc(a["o_filled"], 1)

                    def queries(b, h, half, outputs):
                        pe.wait_ge(a["o_drained"], at(b, 2 * NH, outputs))
                        pe.wait_ge(a["q_drained"], at(b, 2 * NH, 2 * h + half))
                        pe.wait_ge(a["qk_st_ready"], at(b, NH, h + 1))
                        mm3(bank[7][:, :], parts(qk_st, slice(None)), parts(xT, slice(half * HALF, (half + 1) * HALF)),
                            True, True).then_inc(a["q_filled"], 1)

                    def head(b, h, skipped):
                        for step in range(NC):
                            if "this" not in skipped:
                                scores(b, h, step)
                            for kind, h_, rest in items(step, h, skipped):
                                if kind == "T":
                                    turn(b, h_, *rest)
                                elif kind == "U":
                                    attend(b, h_, *rest)
                                elif kind == "O":
                                    half, = rest
                                    if "next" in skipped:
                                        q = 2 * NH
                                    else:
                                        q = 2 * h + 2 + half
                                    output(b, h_, half, q)
                                else:
                                    half, = rest
                                    queries(b, h_, half, 0 if "last" in skipped else 2 * h - 1 + half)

                    with pe.Fori(0, B) as b:
                        pe.wait_ge(a["x_at_ready"], at(b, 1, 1))
                        for k in range(2):
                            pe.wait_ge(t_drained[k], at(b, PER_IMAGE, 0))
                            for j in range(4):
                                last = t.transpose(bank[4 + k][:, j * P:(j + 1) * P], x_at[:, (4 * k + j) * P:(4 * k + j + 1) * P],
                                                   ident[:, :])
                            last.then_inc(t_filled[k], 1)
                        pe.wait_ge(a["xT_ready"], at(b, 1, 1))
                        for half in range(2):
                            queries(b, 0, half, 0)
                        heads(pe, b, head)
                        pe.wait_ge(a["o_drained"], at(b, 2 * NH, 2 * NH))
                        for k in range(2):
                            pe.wait_ge(t_drained[k], at(b, PER_IMAGE, PER_IMAGE - 1))
                            for j in range(4):
                                last = t.transpose(bank[4 + k][:, j * P:(j + 1) * P], oT[:, (4 * k + j) * P:(4 * k + j + 1) * P],
                                                   ident[:, :])
                            last.then_inc(t_filled[k], 1)

                def turned_groups(i):
                    for n, (i_, g) in enumerate(GROUPS):
                        if i_ == i:
                            m_ = min(4, i + 1 - g)
                            yield (n, n % 2, probT[i // 4][:, g:g + m_, (i % 4) * P:(i % 4 + 1) * P],
                                   bank[4 + n % 2][:, 0:m_ * P].rearrange("p (k q) -> p k q", q=P))

                @block.scalar
                def _(act):
                    s_ = nc.scalar

                    def head(b, h, skipped):
                        for step in range(NC):
                            work = list(items(step, h, skipped))
                            for kind, h_, rest in work:
                                if kind == "T":
                                    i, = rest
                                    for n, k, where, source in turned_groups(i):
                                        if k == 0:
                                            act.wait_ge(t_filled[0], at(b, PER_IMAGE, 1 + h_ * (PER_HEAD // 2) + n // 2 + 1))
                                            s_.activation(where, source, ACT.Copy).then_inc(t_drained[0], 1)
                            if "this" not in skipped:
                                i, hh = step, b * NH + h
                                act.wait_ge(a["nmax_ready"], at(hh, NC, i + 1))
                                if i >= 4 or "last" not in skipped:
                                    for k in range(2):
                                        act.wait_ge(t_filled[k], turned(b, h if i >= 4 else h - 1, (i + 4) % NC, k))
                                w = (i + 1) * P
                                s_.activation(prob[:, i % 4, 0:w], psum_pair(2 * (i % 2), w), ACT.Exp, bias=nmax[:, i:i + 1],
                                              accum_out=rsum[:, i:i + 1]).then_inc(a["prob_ready"], 1)
                            for kind, h_, rest in work:
                                if kind == "U" and rest[2] == 4 * rest[0] + 4:
                                    half = rest[0]
                                    act.wait_ge(a["u_filled"], at(b, 2 * NH, 2 * h_ + half + 1))
                                    if not isinstance(h_, int) or h_ > 0:
                                        act.wait_ge(a["o_filled"], at(b, 2 * NH, 2 * h_ - 1 + half))
                                    s_.activation(att[:, half, :], bank[6][:, :], ACT.Copy).then_inc(a["u_drained"], 1)
                                elif kind == "Q":
                                    query(b, h_, rest[0])

                    def query(b, h, half):
                        act.wait_ge(a["q_filled"], at(b, 2 * NH, 2 * h + half + 1))
                        s_.activation(qT[:, 0, half * HALF:(half + 1) * HALF], bank[7][:, :], ACT.Copy).then_inc(a["q_high"], 1)

                    with act.Fori(0, B) as b:
                        act.wait_ge(t_filled[0], at(b, PER_IMAGE, 1))
                        s_.activation(x_tok[:, 0:4, :], bank[4][:, :].rearrange("p (k q) -> p k q", q=P), ACT.Copy
                                      ).then_inc(t_drained[0], 1)
                        for half in range(2):
                            query(b, 0, half)
                        heads(act, b, head)

                @block.vector
                def _(dve):
                    v = nc.vector
                    for h in range(NH):
                        dve.wait_ge(a["w_filled"], h + 1)
                        v.tensor_copy(wuT[:, h, :], bank[h % 2][:, 0:P]).then_inc(a["w_copied"], 1)
                    for h in range(NH):
                        dve.wait_ge(a["w_filled"], NH + h + 1)
                        v.tensor_scalar(w_raw[:, h % 2, :], bank[h % 2][:, 0:P], P ** -0.5, None, ALU.mult)
                        v.tensor_copy(vu_w[:, h, :], bank[h % 2][:, P:2 * P]).then_inc(a["w_copied"], 1)
                        dve.wait_ge(a["w_copied"], NH + h + 1)
                        v.tensor_copy(qk_w[:, h, 0, :], w_raw[:, h % 2, :]).then_inc(a["w_high"], 1)
                        dve.wait_ge(a["w_high"], 2 * h + 1)
                        v.tensor_tensor(qk_w[:, h, 1, :], w_raw[:, h % 2, :], qk_w[:, h, 0, :].bitcast(F32), ALU.subtract
                                        ).then_inc(a["w_high"], 1)
                    dve.wait_ge(a["w_high"], 2 * NH)
                    dve.wait_ge(a["bu_in"], 16)

                    def low_query(b, h, half):
                        cols = slice(half * HALF, (half + 1) * HALF)
                        dve.wait_ge(a["q_high"], at(b, 2 * NH, 2 * h + half + 1))
                        v.tensor_tensor(qT[:, 1, cols], bank[7][:, :], qT[:, 0, cols].bitcast(F32), ALU.subtract
                                        ).then_inc(a["q_drained"], 1)

                    def add(b, h, half):
                        to_bias = isinstance(h, int) and h == 0
                        where_ = oT[:, half * HALF:(half + 1) * HALF]
                        dve.wait_ge(a["o_filled"], at(b, 2 * NH, 2 * h + half + 1))
                        if to_bias:
                            v.tensor_scalar(where_, bank[7][:, :], bu_col[:, 0:1], None, ALU.add).then_inc(a["o_drained"], 1)
                        else:
                            dve.wait_ge(a["o_drained"], at(b, 2 * NH, 2 * h + half - 1))
                            v.tensor_tensor(where_, bank[7][:, :], where_, ALU.add).then_inc(a["o_drained"], 1)

                    def norm(hh, i):
                        dve.wait_ge(a["prob_ready"], at(hh, NC, i + 1))
                        v.reciprocal(rinv[:, i:i + 1], rsum[:, i:i + 1]).then_inc(a["rinv_ready"], 1)

                    def stage(weights, h):
                        letters = "s q" if len(weights.shape) == 4 else "q"
                        mine = weights[:, h:h + 1] if isinstance(h, int) else weights[:, bass.ds(h, 1)]
                        return mine.rearrange(f"p a {letters} -> p (a {letters})")

                    def head(b, h, skipped):
                        for step in range(NC):
                            if "this" not in skipped:
                                i, hh = step, b * NH + h
                                dve.wait_ge(a["scores_ready"], at(hh, NC, i + 1))
                                v.reduce_max(nmax[:, i:i + 1], psum_pair(2 * (i % 2), (i + 1) * P), AX, negate=True
                                             ).then_inc(a["nmax_ready"], 1)
                                if i:
                                    norm(hh, i - 1)
                                elif "last" not in skipped:
                                    norm(hh - 1, NC - 1)
                                if i == 2 and "next" not in skipped:
                                    v.tensor_copy(qk_st[:, :, :].rearrange("p s q -> p (s q)"), stage(qk_w, h + 1).bitcast(F32)).then_inc(a["qk_st_ready"], 1)
                            elif step == 0:
                                norm(b * NH + NH - 1, NC - 1)
                            for kind, h_, rest in items(step, h, skipped):
                                if kind == "T":
                                    if rest[0] in (1, 4) and not (isinstance(h_, int) and h_ == 0):
                                        dve.wait_ge(a["u_filled"], at(b, 2 * NH, 2 * h_ - 1 + rest[0] // 4))
                                    for n, k, where, source in turned_groups(rest[0]):
                                        if k == 1:
                                            dve.wait_ge(t_filled[1], at(b, PER_IMAGE, 1 + h_ * (PER_HEAD // 2) + n // 2 + 1))
                                            v.tensor_copy(where, source).then_inc(t_drained[1], 1)
                                elif kind == "Q":
                                    low_query(b, h_, rest[0])
                                elif kind == "O":
                                    add(b, h_, rest[0])
                            if "this" not in skipped and step == NC - 1:
                                dve.wait_ge(a["o_filled"], at(b, 2 * NH, 2 * h))
                                v.tensor_copy(vu_st[:, :], stage(vu_w, h)).then_inc(a["vu_st_ready"], 1)

                    with dve.Fori(0, B) as b:
                        dve.wait_ge(a["o_filled"], at(b, 2 * NH, 0))
                        v.tensor_copy(x_at[:, :].rearrange("p (i q) -> p i q", q=P), xT_all[:, bass.ds(b * NC, NC), :]
                                      ).then_inc(a["x_at_ready"], 1)
                        v.tensor_copy(qk_st[:, :, :], qk_w[:, 0, :, :].bitcast(F32)).then_inc(a["qk_st_ready"], 1)
                        dve.wait_ge(a["x_at_ready"], at(b, 1, 1))
                        v.tensor_copy(xT[:, 0, :], x_at[:, :])
                        dve.drain()
                        v.tensor_tensor(xT[:, 1, :], x_at[:, :], xT[:, 0, :].bitcast(F32), ALU.subtract).then_inc(a["xT_ready"], 1)
                        dve.wait_ge(t_filled[1], at(b, PER_IMAGE, 1))
                        v.tensor_copy(x_tok[:, 4:8, :], bank[5][:, :].rearrange("p (k q) -> p k q", q=P)).then_inc(t_drained[1], 1)
                        for half in range(2):
                            low_query(b, 0, half)
                        heads(dve, b, head)
                        for k in range(2):
                            dve.wait_ge(t_filled[k], at(b, PER_IMAGE, PER_IMAGE))
                            tiles = t_all[:, bass.ds(b * NC + 4 * k, 4), :]
                            v.tensor_tensor(tiles, bank[4 + k][:, :].rearrange("p (k q) -> p k q", q=P), tiles, ALU.add
                                            ).then_inc(t_drained[k], 1)

        until_experts.close()
        gates = sb("gates", [P, NT, E])
        x_high = sb("x_high", [P, NT, P], F32R)
        x_low = sb("x_low", [P, NT, P], F32R)
        with ExitStack() as rout:
            def sb3(name, shape, dt=F32):
                return rout.enter_context(nc.sbuf_tensor(name, shape, dt))

            router_nat = sb3("router_nat", [E, P])
            routerT = sb3("routerT", [P, E])
            st6b = sb3("st6b", [P, 6])
            mvb = sb3("mvb", [P, 2, 2])
            rsb = sb3("rsb", [P, 2])
            x2t = sb3("x2t", [P, 2, P])
            x2s = sb3("x2s", [P, 2, P])
            logits = sb3("logits", [P, NT, E])
            expo = sb3("expo", [P, NT, E])
            probs = sb3("probs", [P, NT, E])
            first = sb3("first", [P, NT, E])
            second = sb3("second", [P, NT, E])
            cand = sb3("cand", [P, NT, E])
            number = sb3("number", [P, E])
            best = sb3("best", [P, NT])
            best2 = sb3("best2", [P, NT])
            pick = sb3("pick", [P, NT])
            den = sb3("den", [P, NT])
            mhalf2 = sb3("mhalf2", [P, 1])
            epst2 = sb3("epst2", [P, 1])
            r = {n: sem(n) for n in """mvb_ready veb_ready rsb_ready x2_ready x2T_ready x2s_ready x2_high x2T_copied logits_ready
                logits_drained router_in routerT_ready routerT_copied consts2_made peak_off expo_ready gate_step""".split()}
            start_at_one(r, ("router_in", "routerT_ready", "routerT_copied", "consts2_made", "peak_off", "expo_ready", "gate_step"))
            with nc.Block() as block:
                @block.sync
                def _(sp):
                    sp.dma_start(router_nat[:, :], router_w).then_inc(r["router_in"], 16)

                @block.gpsimd
                def _(pool):
                    g = nc.gpsimd
                    g.memset(mhalf2[:, :], -0.5).then_inc(r["consts2_made"], 1)
                    g.memset(epst2[:, :], EPS).then_inc(r["consts2_made"], 1)
                    for e in range(E):
                        g.memset(number[:, e:e + 1], float(e)).then_inc(r["consts2_made"], 1)
                    pool.wait_ge(r["consts2_made"], 2 + E)
                    with pool.Fori(0, B) as b:
                        for c in range(NC):
                            pool.wait_ge(r["mvb_ready"], at(b, NC, c + 1))
                            pool.wait_ge(r["x2_ready"], at(b, NC, max(c - 1, 0)))
                            g.tensor_tensor(rsb[:, c % 2:c % 2 + 1], mvb[:, c % 2, 1:2], epst2[:, :], ALU.add
                                            ).then_inc(r["veb_ready"], 1)
                            pool.wait_ge(r["veb_ready"], at(b, NC, c + 1))
                            g.tensor_tensor(rsb[:, c % 2:c % 2 + 1], rsb[:, c % 2:c % 2 + 1], mhalf2[:, :], ALU.pow
                                            ).then_inc(r["rsb_ready"], 1)

                @block.vector
                def _(dve):
                    v = nc.vector
                    dve.wait_ge(r["routerT_ready"], 1)
                    v.tensor_copy(routerT[:, :], bank[0][:, 0:E]).then_inc(r["routerT_copied"], 1)
                    with dve.Fori(0, B) as b:
                        def stats(c):
                            tile = t_all[:, bass.ds(b * NC + c, 1), :].rearrange("p a q -> p (a q)")
                            dve.drain()
                            v.bn_stats(st6b[:, :], tile)
                            dve.drain()
                            v.bn_aggr(mvb[:, c % 2, :], st6b[:, :]).then_inc(r["mvb_ready"], 1)

                        def norm(c):
                            tile = t_all[:, bass.ds(b * NC + c, 1), :].rearrange("p a q -> p (a q)")
                            dve.wait_ge(r["rsb_ready"], at(b, NC, c + 1))
                            dve.wait_ge(r["x2T_ready"], at(b, NC, max(c - 1, 0)))
                            v.tensor_scalar(x2t[:, c % 2, :], tile, mvb[:, c % 2, 0:1], rsb[:, c % 2:c % 2 + 1],
                                            ALU.subtract, ALU.mult).then_inc(r["x2_ready"], 1)

                        def low(c):
                            tile = bass.ds(b * NC + c, 1)
                            dve.wait_ge(r["x2_high"], at(b, NC, c + 1))
                            v.tensor_tensor(x_low[:, tile, :].rearrange("p a q -> p (a q)"), bank[c % 2][:, 0:P],
                                            x_high[:, tile, :].rearrange("p a q -> p (a q)").bitcast(F32), ALU.subtract
                                            ).then_inc(r["x2T_copied"], 1)

                        for c in range(NC + 2):
                            if c < NC:
                                stats(c)
                            if 0 < c <= NC:
                                norm(c - 1)
                            if c > 1:
                                low(c - 2)
                        dve.wait_ge(r["logits_ready"], at(b, 1, 1))
                        v.tensor_copy(logits[:, bass.ds(b * NC, NC), :],
                                      bank[2][:, 0:NC * E].rearrange("p (c e) -> p c e", e=E)).then_inc(r["logits_drained"], 1)

                    k = [0]

                    def step(ins):
                        k[0] += 1
                        ins.then_inc(r["gate_step"], 1)
                        dve.wait_ge(r["gate_step"], k[0])

                    def wide(t):
                        return t[:, :].unsqueeze(2).to_broadcast([P, NT, E])

                    numbers = number[:, :].unsqueeze(1).to_broadcast([P, NT, E])
                    dve.wait_ge(r["logits_drained"], B + 1)
                    step(v.reduce_max(best[:, :], logits[:, :, :], AX))
                    v.tensor_tensor(logits[:, :, :], logits[:, :, :], wide(best), ALU.subtract).then_inc(r["peak_off"], 1)
                    dve.wait_ge(r["expo_ready"], 1)
                    step(v.tensor_reduce(den[:, :], expo[:, :, :], AX, ALU.add))
                    step(v.reciprocal(den[:, :], den[:, :]))
                    step(v.tensor_tensor(probs[:, :, :], expo[:, :, :], wide(den), ALU.mult))

                    def top(hot, value):
                        step(v.reduce_max(value[:, :], probs[:, :, :], AX))
                        step(v.tensor_tensor(cand[:, :, :], probs[:, :, :], wide(value), ALU.is_lt))
                        step(v.tensor_scalar(cand[:, :, :], cand[:, :, :], float(E), None, ALU.mult))
                        step(v.tensor_tensor(cand[:, :, :], cand[:, :, :], numbers, ALU.add))
                        step(v.tensor_reduce(pick[:, :], cand[:, :, :], AX, ALU.min))
                        step(v.tensor_tensor(hot[:, :, :], wide(pick), numbers, ALU.is_equal))

                    dve.wait_ge(r["consts2_made"], 2 + E)
                    top(first, best)
                    step(v.scalar_tensor_tensor(probs[:, :, :].rearrange("p t e -> p (t e)"), first[:, :, :].rearrange("p t e -> p (t e)"),
                                                -2.0, probs[:, :, :].rearrange("p t e -> p (t e)"), ALU.mult, ALU.add))
                    top(second, best2)
                    step(v.tensor_tensor(den[:, :], best[:, :], best2[:, :], ALU.add))
                    step(v.tensor_scalar(den[:, :], den[:, :], 1e-9, None, ALU.add))
                    step(v.reciprocal(den[:, :], den[:, :]))
                    step(v.tensor_tensor(best[:, :], best[:, :], den[:, :], ALU.mult))
                    step(v.tensor_tensor(best2[:, :], best2[:, :], den[:, :], ALU.mult))
                    step(v.tensor_tensor(first[:, :, :], first[:, :, :], wide(best), ALU.mult))
                    step(v.tensor_tensor(second[:, :, :], second[:, :, :], wide(best2), ALU.mult))
                    step(v.tensor_tensor(gates[:, :, :], first[:, :, :], second[:, :, :], ALU.add))

                @block.tensor
                def _(pe):
                    t = nc.tensor
                    pe.wait_ge(r["router_in"], 16)
                    t.transpose(bank[0][:, 0:E], router_nat[:, :], ident[0:E, 0:E]).then_inc(r["routerT_ready"], 1)
                    pe.wait_ge(r["routerT_copied"], 1)
                    with pe.Fori(0, B) as b:
                        def turn(c):
                            pe.wait_ge(r["x2_ready"], at(b, NC, c + 1))
                            pe.wait_ge(r["x2T_copied"], at(b, NC, max(c - 1, 0)))
                            t.transpose(bank[c % 2][:, 0:P], x2t[:, c % 2, :], ident[:, :]).then_inc(r["x2T_ready"], 1)

                        def route(c):
                            if c == 0:
                                pe.wait_ge(r["logits_drained"], at(b, 1, 0))
                            pe.wait_ge(r["x2s_ready"], at(b, NC, c + 1))
                            return t.matmul(bank[2][:, c * E:(c + 1) * E], x2s[:, c % 2, :], routerT[:, :], start=True, stop=True)

                        for c in range(NC + 1):
                            if c < NC:
                                turn(c)
                            if c:
                                last = route(c - 1)
                                if c == NC:
                                    last.then_inc(r["logits_ready"], 1)

                @block.scalar
                def _(act):
                    a_ = nc.scalar
                    with act.Fori(0, B) as b:
                        for c in range(NC):
                            act.wait_ge(r["x2T_ready"], at(b, NC, c + 1))
                            a_.activation(x2s[:, c % 2, :], bank[c % 2][:, 0:P], ACT.Copy).then_inc(r["x2s_ready"], 1)
                            a_.activation(x_high[:, bass.ds(b * NC + c, 1), :].rearrange("p a q -> p (a q)"),
                                          bank[c % 2][:, 0:P], ACT.Copy).then_inc(r["x2_high"], 1)
                    act.wait_ge(r["peak_off"], 1)
                    a_.activation(expo[:, :, :], logits[:, :, :], ACT.Exp).then_inc(r["expo_ready"], 1)

        with ExitStack() as moe:
            def sb4(name, shape, dt=F32):
                return moe.enter_context(nc.sbuf_tensor(name, shape, dt))

            SUP = NT // 4
            w1n = sb4("w1n", [P, NF, P])
            w3n = sb4("w3n", [P, NF, P])
            w2n = sb4("w2n", [P, HF])
            w1T = sb4("w1T", [P, 2, HF], F32R)
            w3T = sb4("w3T", [P, 2, HF], F32R)
            w2T = sb4("w2T", [P, NF * P])
            act1 = sb4("act1", [P, 2, HALF])
            hT = sb4("hT", [P, 2, NF, HALF])
            m = {n: sem(n) for n in """w_in wT_made wT_high wT_split up_ready silu_ready hid_ready
                down_ready down_drained""".split()}
            start_at_one(m, ("w_in",))
            LASTF = FCH[-1][1]
            with nc.Block() as block:
                @block.sync
                def _(sp):
                    with sp.Fori(0, E) as e:
                        sp.wait_ge(m["wT_made"], at(e, 1, 0))
                        for w, src in ((w1n, w1), (w3n, w3)):
                            sp.dma_start(w[:, 0:NF - 1, :], src[bass.ds(e, 1), 0:(NF - 1) * P, :].rearrange("a (j p) c -> p (a j) c", p=P)
                                         ).then_inc(m["w_in"], 16)
                            sp.dma_start(w[0:LASTF, NF - 1, :], src[bass.ds(e, 1), (NF - 1) * P:HF, :].rearrange("a p c -> p (a c)")
                                         ).then_inc(m["w_in"], 16)
                        sp.dma_start(w2n[:, :], w2[bass.ds(e, 1), :, :].rearrange("a p c -> p (a c)")).then_inc(m["w_in"], 16)

                @block.tensor
                def _(pe):
                    t = nc.tensor

                    def mm3(out_, left, right, start, stop):
                        t.matmul(out_, left[1], right[0], start=start, stop=False)
                        t.matmul(out_, left[0], right[1], start=False, stop=False)
                        return t.matmul(out_, left[0], right[0], start=False, stop=stop)

                    with pe.Fori(0, E) as e:
                        pe.wait_ge(m["w_in"], e * 80 + 80)
                        pe.wait_ge(m["down_drained"], at(e, SUP, 0))
                        pe.wait_ge(m["wT_split"], at(e, 1, 0))
                        for f, n in enumerate(x[1] for x in FCH):
                            t.transpose(bank[6][:, f * P:f * P + n], w1n[0:n, f, :], ident[0:n, 0:n])
                            t.transpose(bank[7][:, f * P:f * P + n], w3n[0:n, f, :], ident[0:n, 0:n])
                            last = t.transpose(bank[4][0:n, f * P:(f + 1) * P], w2n[:, f * P:f * P + n], ident[:, :])
                        last.then_inc(m["wT_made"], 1)
                        with pe.Fori(0, SUP // 2) as s2:
                            es = e * SUP + s2 * 2

                            def up(s):
                                group = bass.ds(s2 * 8 + 4 * s, 4)
                                x_ = (x_high[:, group, :].rearrange("p j q -> p (j q)"),
                                      x_low[:, group, :].rearrange("p j q -> p (j q)"))
                                for f, (f0, n) in enumerate(FCH):
                                    u = 3 * s + f
                                    pe.wait_ge(m["hid_ready"], at(es, NF, max(u - 1, 0)))
                                    mm3(bank[u % 2][0:n, :], [w1T[:, part, f0:f0 + n] for part in range(2)], x_, True, True)
                                    mm3(bank[2 + u % 2][0:n, :], [w3T[:, part, f0:f0 + n] for part in range(2)], x_, True, True
                                        ).then_inc(m["up_ready"], 1)

                            def down(s):
                                pe.wait_ge(m["hid_ready"], at(es, NF, NF * (s + 1)))
                                pe.wait_ge(m["down_drained"], at(es, 1, max(s - 1, 0)))
                                for j in range(4):
                                    for f, (f0, n) in enumerate(FCH):
                                        last = t.matmul(bank[4 + s][:, j * P:(j + 1) * P], hT[0:n, s, f, j * P:(j + 1) * P],
                                                        w2T[0:n, f * P:(f + 1) * P], start=(f == 0), stop=(f == NF - 1))
                                last.then_inc(m["down_ready"], 1)

                            pe.wait_ge(m["wT_split"], at(e, 1, 1))
                            up(0)
                            up(1)
                            down(0)
                            down(1)

                @block.scalar
                def _(act):
                    a_ = nc.scalar
                    with act.Fori(0, E) as e:
                        act.wait_ge(m["wT_made"], at(e, 1, 1))
                        act.wait_ge(m["down_ready"], at(e, SUP, 0))
                        a_.activation(w1T[:, 0, :], bank[6][:, 0:HF], ACT.Copy)
                        a_.activation(w3T[:, 0, :], bank[7][:, 0:HF], ACT.Copy)
                        a_.activation(w2T[:, 0:(NF - 1) * P], bank[4][:, 0:(NF - 1) * P], ACT.Copy)
                        a_.activation(w2T[0:LASTF, (NF - 1) * P:NF * P], bank[4][0:LASTF, (NF - 1) * P:NF * P], ACT.Copy
                                      ).then_inc(m["wT_high"], 1)
                        with act.Fori(0, SUP // 2) as s2:
                            es = e * SUP + s2 * 2
                            def silu(u):
                                n = FCH[u % NF][1]
                                act.wait_ge(m["up_ready"], at(es, NF, u + 1))
                                act.wait_ge(m["hid_ready"], at(es, NF, max(u - 1, 0)))
                                a_.activation(act1[0:n, u % 2, :], bank[u % 2][0:n, :], ACT.Silu).then_inc(m["silu_ready"], 1)

                            for u in range(2 * NF):
                                silu(u)

                @block.vector
                def _(dve):
                    v = nc.vector
                    with dve.Fori(0, E) as e:
                        dve.wait_ge(m["wT_made"], at(e, 1, 1))
                        dve.wait_ge(m["down_ready"], at(e, SUP, 0))
                        dve.wait_ge(m["wT_high"], at(e, 1, 1))
                        v.tensor_tensor(w1T[:, 1, :], bank[6][:, 0:HF], w1T[:, 0, :].bitcast(F32), ALU.subtract)
                        v.tensor_tensor(w3T[:, 1, :], bank[7][:, 0:HF], w3T[:, 0, :].bitcast(F32), ALU.subtract
                                        ).then_inc(m["wT_split"], 1)
                        with dve.Fori(0, SUP // 2) as s2:
                            es = e * SUP + s2 * 2

                            def hidden(s):
                                for f, (f0, n) in enumerate(FCH):
                                    u = 3 * s + f
                                    dve.wait_ge(m["silu_ready"], at(es, NF, u + 1))
                                    dve.wait_ge(m["down_ready"], at(es, 1, 0))
                                    v.tensor_tensor(hT[0:n, s, f, :], act1[0:n, u % 2, :], bank[2 + u % 2][0:n, :], ALU.mult
                                                    ).then_inc(m["hid_ready"], 1)

                            def weigh(s):
                                dve.wait_ge(m["down_ready"], at(es, 1, s + 1))
                                for j in range(4):
                                    tile = t_all[:, bass.ds(s2 * 8 + 4 * s + j, 1), :].rearrange("p a q -> p (a q)")
                                    gate = gates[:, bass.ds(s2 * 8 + 4 * s + j, 1), bass.ds(e, 1)].rearrange("p a q -> p (a q)")
                                    last = v.scalar_tensor_tensor(tile, bank[4 + s][:, j * P:(j + 1) * P], gate, tile,
                                                                  ALU.mult, ALU.add)
                                last.then_inc(m["down_drained"], 1)

                            hidden(0)
                            hidden(1)
                            weigh(0)
                            weigh(1)

        with ExitStack() as fin:
            t_st = fin.enter_context(nc.sbuf_tensor("t_st", [P, NC, P], F32))
            f = {n: sem(n) for n in ("staged", "turned", "drained_scalar", "drained_vector")}
            start_at_one(f, ())
            staged, turned = f["staged"], f["turned"]
            drained = [f["drained_scalar"], f["drained_vector"]]
            stored = sem("stored")
            with nc.Block() as block:
                @block.gpsimd
                def _(pool):
                    with pool.Fori(0, B) as b:
                        pool.wait_ge(turned, at(b, 2, 0))
                        nc.gpsimd.tensor_copy(t_st[:, :, :], t_all[:, bass.ds(b * NC, NC), :]).then_inc(staged, 1)

                @block.tensor
                def _(pe):
                    with pe.Fori(0, B) as b:
                        pe.wait_ge(staged, at(b, 1, 1))
                        for hf in range(2):
                            pe.wait_ge(drained[hf], at(b, 1, 0))
                            for j in range(4):
                                last = nc.tensor.transpose(bank[hf][:, j * P:(j + 1) * P], t_st[:, 4 * hf + j, :], ident[:, :])
                            last.then_inc(turned, 1)

                @block.scalar
                def _(act):
                    with act.Fori(0, B) as b:
                        act.wait_ge(turned, at(b, 2, 1))
                        nc.scalar.activation(xT_all[:, bass.ds(b * NC, 4), :],
                                             bank[0][:, :].rearrange("p (j q) -> p j q", q=P), ACT.Copy).then_inc(drained[0], 1)

                @block.vector
                def _(dve):
                    with dve.Fori(0, B) as b:
                        dve.wait_ge(turned, at(b, 2, 2))
                        nc.vector.tensor_copy(xT_all[:, bass.ds(b * NC + 4, 4), :],
                                              bank[1][:, :].rearrange("p (j q) -> p j q", q=P)).then_inc(drained[1], 1)

                @block.sync
                def _(sp):
                    with sp.Fori(0, B) as b:
                        sp.wait_ge(drained[0], at(b, 1, 1))
                        sp.wait_ge(drained[1], at(b, 1, 1))
                        sp.dma_start(out[bass.ds(b, 1)].rearrange("b c h w -> c b (h w)"),
                                     xT_all[:, bass.ds(b * NC, NC), :].rearrange("p (a j) q -> p a (j q)", a=1)).then_inc(stored, 16)
                    sp.wait_ge(stored, B * 16)


_INS = ["x", "L0_conv_ln_w", "L0_conv_ln_b", "L0_conv_in_proj_w", "L0_conv_conv_w", "L0_conv_conv_b", "L0_conv_A_log",
        "L0_conv_D", "L0_conv_dt_bias", "L0_conv_rms_w", "L0_conv_out_proj_w", "L1_attn_Wk", "L1_attn_Wq", "L1_attn_Wv",
        "L1_attn_Wu", "L1_attn_bu", "L1_ffn_router_w", "L1_ffn_w1", "L1_ffn_w2", "L1_ffn_w3"]


def kernel(**inputs):
    import numpy as _np
    import concourse.bacc as _bacc
    from concourse import mybir as _mybir
    from concourse.bass_utils import run_bass_kernel_spmd as _run

    nc = _bacc.Bacc("TRN2", target_bir_lowering=False, num_devices=1)
    arrays, args = {}, []
    for name in _INS:
        a = _np.ascontiguousarray(inputs[name])
        arrays[f"in_{name}"] = a
        args.append(nc.dram_tensor(f"in_{name}", a.shape, _mybir.dt.from_np(a.dtype), kind="ExternalInput").ap())
    shape = inputs["x"].shape
    args.append(nc.dram_tensor("out_0", shape, _mybir.dt.float32, kind="ExternalOutput").ap())
    hybrid_kernel(nc, *args)
    r = _run(nc, [arrays], core_ids=[0])
    return r.results[0]["out_0"]
```

```python
from contextlib import ExitStack

import concourse.bass as bass
from concourse import mybir

P = 128
HALF = 512
NH = 8
HD = 32
DI = NH * HD
NS = 32
TAPS = 3
NEG = -1.0e30
EPS = 1e-5

ALU = mybir.AluOpType
ACT = mybir.ActivationFunctionType
F32 = mybir.dt.float32
F32R = mybir.dt.float32r
BF16 = mybir.dt.bfloat16
AX = mybir.AxisListType.X
DVE_STEPS = 41


def hybrid_kernel(nc, x, ln_w, ln_b, in_w, conv_w, conv_b, A_log, D, dt_bias, rms_w, out_w,
                  Wk, Wq, Wv, Wu, bu, router_w, w1, w2, w3, out):
    B, C, HH, WW = x.shape
    L = HH * WW
    NC = L // P
    NT = B * NC
    E, HF, _ = w1.shape
    RH = HH // 2
    CB = 2 * NS
    assert C == P and L == 2 * HALF and Wq.shape[0] == NH * P
    FCH = [(f, min(P, HF - f)) for f in range(0, HF, P)]
    NF = len(FCH)

    ctx = ExitStack()
    with ctx:
        def sb(name, shape, dt=F32):
            return ctx.enter_context(nc.sbuf_tensor(name, shape, dt))

        def sem(name):
            return ctx.enter_context(nc.semaphore(name))

        psum = ctx.enter_context(nc.psum_tensor("psum", [P, 8 * HALF], F32))
        bank = [psum[:, i * HALF:(i + 1) * HALF] for i in range(8)]

        def psum_pair(i, width):
            return psum[:, i * HALF:i * HALF + width]

        def at(n, per, k):
            return n * per + k + 1

        ident = sb("ident", [P, P])
        ident_bf = sb("ident_bf", [P, P], BF16)
        upto = sb("upto", [P, P])
        mask_after = sb("mask_after", [P, P], BF16)
        mask_ahead = sb("mask_ahead", [P, P], BF16)

        until_experts = ExitStack()

        def sb0(name, shape, dt=F32):
            return until_experts.enter_context(nc.sbuf_tensor(name, shape, dt))

        t_all = sb("t_all", [P, NT, P])
        xT_all = sb0("xT_all", [P, NT, P])

        wq = sb0("wq", [P, NH, P])
        wk = sb0("wk", [P, NH, P])
        wv = sb0("wv", [P, NH, P])
        wu = sb0("wu", [P, NH * P])

        consts_in = sem("consts_in")
        attn_in = sem("attn_in")
        pool_made = sem("pool_made")
        setup_T = sem("setup_T")
        setup_copied = sem("setup_copied")
        a_exp = sem("a_exp")
        a_neg = sem("a_neg")

        N_CONST = 13

        def start_at_one(sems, but):
            with nc.Block() as block:
                @block.sync
                def _(sp):
                    for name in sems:
                        if name not in but:
                            sp.sem_inc(sems[name], 1)

        scan = ExitStack()
        with scan:
            def sb1(name, shape, dt=F32):
                return scan.enter_context(nc.sbuf_tensor(name, shape, dt))

            mean_w = sb1("mean_w", [P, P])
            in_nat = sb1("in_nat", [P, 5, P])
            inT = sb1("inT", [P, 584])
            cw = sb1("cw", [P, 3, TAPS * TAPS])
            cb = sb1("cb", [P, 3])
            lnw = sb1("lnw", [P, 1])
            lnb = sb1("lnb", [P, 1])
            rmsw = sb1("rmsw", [P, 2])
            out_nat = sb1("out_nat", [P, DI])
            outT = sb1("outT", [P, 2, P])
            dtb = sb1("dtb", [P, NH])
            alog = sb1("alog", [P, NH])
            aexp = sb1("aexp", [P, NH])
            aneg = sb1("aneg", [P, NH])
            dvec = sb1("dvec", [P, NH])
            x_in_sb = sb1("x_in_sb", [P, L])
            x_st = sb1("x_st", [P, L])
            xc = sb1("xc", [P, L])
            sq = sb1("sq", [P, L])
            rstd = sb1("rstd", [P, NC])
            xn = sb1("xn", [P, L])
            pad = sb1("pad", [P, 3, HH + 2, WW + 2])
            acc = sb1("acc", [P, 3, L])
            weighed = [sq[0:CB, :], xc[0:CB, :], sb1("weighed_tap", [CB, L])[:, :]]
            assert NC + 1 == TAPS * TAPS
            xsC = sb1("xsC", [P, 2, L])
            BC = sb1("BC", [NS, 2, L])
            zs = sb1("zs", [P, NC, DI])
            dtr = sb1("dtr", [P, NC * NH])
            dta = sb1("dta", [P, NC * NH])
            dte = sb1("dte", [P, NC * NH])
            dtl = sb1("dtl", [P, NC * NH])
            dt = sb1("dt", [P, NC * NH])
            dA = sb1("dA", [P, NC * NH])
            nAcs = sb1("nAcs", [P, NC * NH])
            eAcs = sb1("eAcs", [P, NC * NH])
            tok = sb1("tok", [P, NC, DI + NS])
            Ldec = sb1("Ldec", [P, 2, NH, P])
            edec = sb1("edec", [NS, NC, NH])
            GL = sb1("GL", [P, 2, NH, P])
            xdt = sb1("xdt", [P, 2, DI])
            dx = sb1("dx", [P, 2, DI])
            Xd = sb1("Xd", [P, 2, DI])
            S = sb1("S", [NS, DI])
            y1 = sb1("y1", [P, 2, DI])
            ysq = sb1("ysq", [P, DI])
            ssq = sb1("ssq", [P, NC])
            rs = sb1("rs", [P, NC])
            yn = sb1("yn", [P, 2, DI])
            yT = sb1("yT", [P, 2, 2, P])
            st6 = sb1("st6", [P, 6])
            mv = sb1("mv", [P, 2, 2])
            rs2 = sb1("rs2", [P, 2])
            xnt = sb1("xnt", [P, 2, P])
            mhalf = sb1("mhalf", [P, 1])
            epst = sb1("epst", [P, 1])

            names = """x_in mean_ready xc_ready sq_ready var_ready xn_ready proj_ready pad_copied zproj_ready z_ready
                dtproj_ready dtabs_ready dte_ready dtln_ready dA_ready acs_ready nacs_ready eacs_ready conv_done tap_scaled tap_added
                xs_ready tok_ready tok_copied seg_ready decay_ready gl_ready xd_ready xdt_ready dx_ready st_ready
                state_ready y_ready y_drained yg_ready ssq_ready yn_ready yT_ready yT_copied t_ready t_drained
                lnx_ready xnT_ready xnT_copied xst_ready dve_step pool_step pad_zero var_drained rstd_ready rstd_rows ms_ready rs_ready mv_ready ve_ready rs2_ready""".split()
            s = {n: sem(n) for n in names}

            start_at_one(s, ("x_in", "dve_step", "pool_step", "pad_zero"))

            def tile_at(n):
                return slice(n, n + 1) if isinstance(n, int) else bass.ds(n, 1)

            def images(engine, ahead, image):
                for piece in ahead(0):
                    piece()
                with engine.Fori(0, B - 1) as b:
                    image(b, ahead(b + 1))
                image(B - 1, [])

            AHEAD_AT = {NC + n: n for n in range(6)}

            def piece_of(pieces, step):
                if step in AHEAD_AT and AHEAD_AT[step] < len(pieces):
                    pieces[AHEAD_AT[step]]()
            with nc.Block() as block:
                @block.sync
                def _(sp):
                    sp.dma_start(in_nat[:, 0:4, :], in_w[0:512, :].rearrange("(j p) c -> p j c", p=P)).then_inc(consts_in, 16)
                    sp.dma_start(in_nat[0:72, 4, :], in_w[512:584, :]).then_inc(consts_in, 16)
                    sp.dma_start(cw[:, 0:2, :], conv_w[0:256].rearrange("(j p) a h w -> p j (a h w)", p=P)).then_inc(consts_in, 16)
                    sp.dma_start(cw[0:CB, 2, :], conv_w[256:320].rearrange("p a h w -> p (a h w)")).then_inc(consts_in, 16)
                    with nc.allow_non_contiguous_dma("small vectors, one element a partition"):
                        sp.dma_start(cb[:, 0:2], conv_b[0:256].rearrange("(j p) -> p j", p=P)).then_inc(consts_in, 16)
                        sp.dma_start(cb[0:CB, 2:3], conv_b[256:320].rearrange("(p a) -> p a", a=1)).then_inc(consts_in, 16)
                        sp.dma_start(lnw[:, :], ln_w.rearrange("(p a) -> p a", a=1)).then_inc(consts_in, 16)
                        sp.dma_start(lnb[:, :], ln_b.rearrange("(p a) -> p a", a=1)).then_inc(consts_in, 16)
                        sp.dma_start(rmsw[:, :], rms_w.rearrange("(j p) -> p j", p=P)).then_inc(consts_in, 16)
                    sp.dma_start(out_nat[:, :], out_w).then_inc(consts_in, 16)
                    sp.dma_start(dtb[:, :], dt_bias.partition_broadcast(P)).then_inc(consts_in, 16)
                    sp.dma_start(alog[:, :], A_log.partition_broadcast(P)).then_inc(consts_in, 16)
                    sp.dma_start(dvec[:, :], D.partition_broadcast(P)).then_inc(consts_in, 16)
                    sp.dma_start(x_in_sb[:, :], x[0].rearrange("c h w -> c (h w)")).then_inc(s["x_in"], 16)
                    for w, src in ((wq, Wq), (wk, Wk), (wv, Wv)):
                        sp.dma_start(w[:, :, :], src.rearrange("(h o) d -> o h d", o=P)).then_inc(attn_in, 16)
                    sp.dma_start(wu[:, :], Wu).then_inc(attn_in, 16)
                    with sp.Fori(1, B) as b:
                        sp.wait_ge(s["xst_ready"], at(b, 1, 0))
                        sp.wait_ge(s["xc_ready"], at(b, 2, 0))
                        sp.dma_start(x_in_sb[:, :], x[bass.ds(b, 1)].rearrange("b c h w -> c (b h w)")).then_inc(s["x_in"], 16)

                @block.gpsimd
                def _(pool):
                    g = nc.gpsimd
                    g.memset(ident[:, :], 1.0).then_inc(s["pool_step"], 1)
                    g.memset(ident_bf[:, :], 1.0).then_inc(s["pool_step"], 1)
                    g.memset(upto[:, :], 1.0).then_inc(s["pool_step"], 1)
                    g.memset(mask_after[:, :], 0.0).then_inc(s["pool_step"], 1)
                    g.memset(mask_ahead[:, :], 0.0).then_inc(s["pool_step"], 1)
                    g.memset(mean_w[:, :], 1.0 / C).then_inc(s["pool_step"], 1)
                    g.memset(mhalf[:, :], -0.5).then_inc(s["pool_step"], 1)
                    g.memset(epst[:, :], EPS).then_inc(s["pool_step"], 1)
                    g.memset(pad[:, :, :, :], 0.0).then_inc(s["pad_zero"], 1)
                    pool.wait_ge(s["pool_step"], 8)
                    for m in (ident, ident_bf):
                        g.affine_select(out=m[:, :], in_=m[:, :], compare_op=ALU.is_equal, fill=0.0, base=0,
                                        pattern=[[-1, P]], channel_multiplier=1).then_inc(pool_made, 1)
                    g.affine_select(out=upto[:, :], in_=upto[:, :], compare_op=ALU.is_ge, fill=0.0, base=0,
                                    pattern=[[1, P]], channel_multiplier=-1).then_inc(pool_made, 1)
                    g.affine_select(out=mask_after[:, :], in_=mask_after[:, :], compare_op=ALU.is_ge, fill=NEG, base=0,
                                    pattern=[[1, P]], channel_multiplier=-1).then_inc(pool_made, 1)
                    g.affine_select(out=mask_ahead[:, :], in_=mask_ahead[:, :], compare_op=ALU.is_ge, fill=NEG, base=0,
                                    pattern=[[-1, P]], channel_multiplier=1).then_inc(pool_made, 1)
                    pool.wait_ge(consts_in, 16 * N_CONST)
                    def power(t, ready):
                        return g.tensor_tensor(t, t, mhalf[:, 0:1].to_broadcast([P, t.shape[1]]), ALU.pow).then_inc(ready, 1)

                    def ahead(b):
                        def deviation():
                            pool.wait_ge(s["var_drained"], at(b, 1, 1))
                            power(rstd[:, :], s["rstd_ready"])

                        return [deviation]

                    def image(b, pieces):
                        for tap in range(TAPS * TAPS):
                            pool.wait_ge(s["tap_scaled"], at(b, TAPS * TAPS, tap + 1))
                            if tap == 0:
                                pool.wait_ge(s["xs_ready"], at(b, 4, 0))
                                continue
                            if tap > 1:
                                pool.wait_ge(s["tap_added"], at(b, TAPS * TAPS, tap))
                            so_far = weighed[0] if tap == 1 else acc[0:CB, 2, :]
                            g.tensor_tensor(acc[0:CB, 2, :], so_far, weighed[tap % 3], ALU.add
                                            ).then_inc(s["tap_added"], 2 if tap == 1 else 1)

                        def chunk_in(c):
                            pool.wait_ge(s["tok_copied"], at(b, NC, c + 1))
                            pool.wait_ge(s["y_ready"], at(b, NC, max(c - 1, 0)))
                            pool.wait_ge(s["xd_ready"], at(b, NC, max(c - 1, 0)))
                            xs3 = tok[:, c, 0:DI].rearrange("p (h d) -> p h d", d=HD)
                            g.tensor_tensor(xdt[:, c % 2, :].rearrange("p (h d) -> p h d", d=HD), xs3,
                                            dt[:, c * NH:(c + 1) * NH].unsqueeze(2).to_broadcast([P, NH, HD]), ALU.mult
                                            ).then_inc(s["xdt_ready"], 1)
                            pool.wait_ge(s["yg_ready"], at(b, NC, max(c - 1, 0)))
                            g.tensor_tensor(dx[:, c % 2, :].rearrange("p (h d) -> p h d", d=HD), xs3,
                                            dvec[:, :].unsqueeze(2).to_broadcast([P, NH, HD]), ALU.mult
                                            ).then_inc(s["dx_ready"], 1)

                        def chunk_rs(c):
                            pool.wait_ge(s["ssq_ready"], at(b, NC, c + 1))
                            if c == 0:
                                pool.wait_ge(s["yn_ready"], at(b, NC, 0))
                            g.tensor_tensor(rs[:, c:c + 1], ssq[:, c:c + 1], epst[:, :], ALU.add
                                            ).then_inc(s["ms_ready"], 1)
                            pool.wait_ge(s["ms_ready"], at(b, NC, c + 1))
                            power(rs[:, c:c + 1], s["rs_ready"])

                        def chunk_rs2(c):
                            pool.wait_ge(s["mv_ready"], at(b, NC, c + 1))
                            pool.wait_ge(s["lnx_ready"], at(b, NC, max(c - 1, 0)))
                            g.tensor_tensor(rs2[:, c % 2:c % 2 + 1], mv[:, c % 2, 1:2], epst[:, :], ALU.add
                                            ).then_inc(s["ve_ready"], 1)
                            pool.wait_ge(s["ve_ready"], at(b, NC, c + 1))
                            power(rs2[:, c % 2:c % 2 + 1], s["rs2_ready"])

                        for step in range(NC + 4):
                            for f, lag in ((chunk_in, 0), (chunk_rs, 2), (chunk_rs2, 4)):
                                if 0 <= step - lag < NC:
                                    f(step - lag)
                            if step == NC + 1:
                                for piece in pieces:
                                    piece()

                    images(pool, ahead, image)

                @block.tensor
                def _(pe):
                    t = nc.tensor
                    pe.wait_ge(pool_made, 5)
                    pe.wait_ge(consts_in, 16 * N_CONST)
                    for j in range(5):
                        n = P if j < 4 else 72
                        if j >= 2:
                            pe.wait_ge(setup_copied, j - 1)
                        t.transpose(bank[j % 2][:, 0:n], in_nat[0:n, j, :], ident[0:n, 0:n]).then_inc(setup_T, 1)
                    for j in range(2):
                        pe.wait_ge(setup_copied, 4 + j)
                        t.transpose(bank[(5 + j) % 2][:, 0:P], out_nat[:, j * P:(j + 1) * P], ident[:, :]).then_inc(setup_T, 1)
                    pe.wait_ge(setup_copied, 7)
                    def ahead(b):
                        def mean():
                            pe.wait_ge(s["x_in"], b * 16 + 16)
                            pe.wait_ge(s["gl_ready"], at(b, NC, 0))
                            for hf in range(2):
                                t.matmul(bank[hf][:, :], mean_w[:, :],
                                         x_in_sb[:, hf * HALF:(hf + 1) * HALF],
                                         start=True, stop=True).then_inc(s["mean_ready"], 1)

                        def variance():
                            pe.wait_ge(s["sq_ready"], at(b, 2, 2))
                            for c in range(NC):
                                last = t.matmul(bank[0][:, c:c + 1], sq[:, c * P:(c + 1) * P], mean_w[:, 0:1], start=True, stop=True)
                            last.then_inc(s["var_ready"], 1)

                        def rows():
                            pe.wait_ge(s["rstd_ready"], at(b, 1, 1))
                            for c in range(NC):
                                last = t.matmul(bank[c // 4][:, (c % 4) * P:(c % 4 + 1) * P], rstd[:, c:c + 1].to_broadcast([P, P]),
                                                ident[:, :], start=True, stop=True)
                                if c % 4 == 3:
                                    last.then_inc(s["rstd_rows"], 1)

                        def project(n_):
                            if n_ == 0:
                                pe.wait_ge(s["decay_ready"], at(b, NC, 0))
                            for u in range(2 * n_, 2 * n_ + 2):
                                hf, m = u // 3, u % 3
                                n = P if m < 2 else CB
                                pe.wait_ge(s["xn_ready"], at(b, 2, hf + 1))
                                if u >= 2:
                                    pe.wait_ge(s["pad_copied"], at(b, 6, u - 1))
                                t.matmul(bank[2 + u % 2][0:n, :], inT[:, DI + m * P:DI + m * P + n],
                                         xn[:, hf * HALF:(hf + 1) * HALF], start=True, stop=True).then_inc(s["proj_ready"], 1)

                        return [mean, variance, rows] + [lambda n_=n_: project(n_) for n_ in range(3)]

                    def image(b, pieces):
                        pe.wait_ge(s["yT_copied"], at(b, NC, 0))
                        pe.wait_ge(s["xnT_copied"], at(b, NC, 0))
                        for c in range(NC):
                            last = t.matmul(bank[6][:, c * NH:(c + 1) * NH], xn[:, c * P:(c + 1) * P], inT[:, 576:584],
                                            start=True, stop=True)
                        last.then_inc(s["dtproj_ready"], 1)
                        pe.wait_ge(s["y_drained"], at(b, NC, 0))
                        pe.wait_ge(s["state_ready"], at(b, NC, 0))
                        for c in range(NC):
                            if c >= 2:
                                pe.wait_ge(s["z_ready"], at(b, NC, c - 1))
                            t.matmul(bank[4 + c % 2][:, 0:DI], xn[:, c * P:(c + 1) * P], inT[:, 0:DI],
                                     start=True, stop=True).then_inc(s["zproj_ready"], 1)
                        pe.wait_ge(s["dA_ready"], at(b, 1, 1))
                        t.matmul(bank[6][:, 64:128], upto[:, :], dA[:, :], start=True, stop=True).then_inc(s["acs_ready"], 1)

                        def chunk_in(c):
                            sl = slice(c * P, (c + 1) * P)
                            pb = bank[c % 2]
                            if c == 0:
                                pe.wait_ge(s["xs_ready"], at(b, 4, 4))
                            if c >= 2:
                                pe.wait_ge(s["gl_ready"], at(b, NC, c - 1))
                            for m in range(2):
                                t.transpose(pb[:, m * P:(m + 1) * P], xsC[:, m, sl], ident[:, :])
                            t.transpose(pb[:, DI:DI + NS], BC[:, 0, sl], ident[0:NS, 0:NS])
                            t.matmul(pb[:, 384:512], BC[:, 0, sl], BC[:, 1, sl], start=True, stop=True).then_inc(s["tok_ready"], 1)
                            if c == 0:
                                pe.wait_ge(s["pad_copied"], at(b, 6, 6))
                            else:
                                pe.wait_ge(s["decay_ready"], at(b, NC, c))
                            for j in range(2):
                                seg = bank[2 + j]
                                t.matmul(seg[:, :].rearrange("p (h q) -> p h q", q=P), ident_bf[:, :],
                                         mask_after[:, :].unsqueeze(1).to_broadcast([P, 4, P]), start=True, stop=False)
                                for h in range(4):
                                    col = c * NH + 4 * j + h
                                    last = t.matmul(seg[:, h * P:(h + 1) * P], dA[:, col:col + 1].to_broadcast([P, P]),
                                                    upto[:, :], start=False, stop=(h == 3))
                            last.then_inc(s["seg_ready"], 1)

                        def chunk_y(c):
                            sl = slice(c * P, (c + 1) * P)
                            pe.wait_ge(s["xd_ready"], at(b, NC, c + 1))
                            if c == 0:
                                pe.wait_ge(s["z_ready"], at(b, NC, NC))
                            else:
                                pe.wait_ge(s["state_ready"], at(b, NC, c))
                            t.matmul(bank[5][0:NS, 0:DI], tok[:, c, DI:DI + NS], Xd[:, c % 2, :], start=True,
                                     stop=True).then_inc(s["st_ready"], 1)
                            pe.wait_ge(s["y_drained"], at(b, NC, c))
                            pe.wait_ge(s["gl_ready"], at(b, NC, c + 1))
                            pe.wait_ge(s["xdt_ready"], at(b, NC, c + 1))
                            for h in range(NH):
                                last = t.matmul(bank[4][:, DI + h * HD:DI + (h + 1) * HD], GL[:, c % 2, h, :],
                                                xdt[:, c % 2, h * HD:(h + 1) * HD], start=True, stop=True)
                            if c:
                                last = t.matmul(bank[4][:, 0:DI], BC[:, 1, sl], S[:, :], start=True, stop=True)
                            last.then_inc(s["y_ready"], 1)

                        def chunk_yT(c):
                            pe.wait_ge(s["yn_ready"], at(b, NC, c + 1))
                            if c == 0:
                                pe.wait_ge(s["nacs_ready"], at(b, 1, 1))
                            if c >= 4:
                                pe.wait_ge(s["xnT_copied"], at(b, NC, c - 3))
                            pe.wait_ge(s["yT_copied"], at(b, NC, c))
                            for j in range(2):
                                last = t.transpose(bank[6][:, j * P:(j + 1) * P], yn[:, c % 2, j * P:(j + 1) * P], ident[:, :])
                            last.then_inc(s["yT_ready"], 1)

                        def chunk_out(c):
                            if c == 0:
                                pe.wait_ge(s["xst_ready"], at(b, 1, 1))
                            pe.wait_ge(s["t_drained"], at(b, NC, c))
                            pe.wait_ge(s["yT_copied"], at(b, NC, c + 1))
                            t.matmul(bank[7][:, 0:P], x_st[:, c * P:(c + 1) * P], ident[:, :], start=True, stop=False)
                            t.matmul(bank[7][:, 0:P], yT[:, c % 2, 0, :], outT[:, 0, :], start=False, stop=False)
                            t.matmul(bank[7][:, 0:P], yT[:, c % 2, 1, :], outT[:, 1, :], start=False,
                                     stop=True).then_inc(s["t_ready"], 1)

                        def chunk_xnT(c):
                            pe.wait_ge(s["lnx_ready"], at(b, NC, c + 1))
                            pe.wait_ge(s["yT_copied"], at(b, NC, min(c + 4, NC)))
                            pe.wait_ge(s["xnT_copied"], at(b, NC, c))
                            t.transpose(bank[6][:, 256:384], xnt[:, c % 2, :], ident[:, :]).then_inc(s["xnT_ready"], 1)

                        for step in range(NC + 6):
                            for f, lag in ((chunk_in, 0), (chunk_y, 1), (chunk_yT, 3), (chunk_out, 4), (chunk_xnT, 6)):
                                if 0 <= step - lag < NC:
                                    f(step - lag)
                            piece_of(pieces, step)

                    images(pe, ahead, image)
                    pe.wait_ge(s["xnT_copied"], B * NC + 1)

                @block.scalar
                def _(act):
                    a = nc.scalar
                    act.wait_ge(consts_in, 16 * N_CONST)
                    a.activation(aexp[:, :], alog[:, :], ACT.Exp).then_inc(a_exp, 1)
                    act.wait_ge(s["pad_zero"], 1)
                    def ahead(b):
                        def square():
                            for hf in range(2):
                                act.wait_ge(s["xc_ready"], at(b, 2, hf + 1))
                                a.activation(sq[:, hf * HALF:(hf + 1) * HALF], xc[:, hf * HALF:(hf + 1) * HALF],
                                             ACT.Square).then_inc(s["sq_ready"], 1)

                        def nothing():
                            pass

                        def pad_copy(n_):
                            if n_ == 0:
                                act.wait_ge(s["conv_done"], at(b, 2, 0))
                                act.wait_ge(s["tap_scaled"], at(b, TAPS * TAPS, 0))
                            for u in range(2 * n_, 2 * n_ + 2):
                                hf, m = u // 3, u % 3
                                n = P if m < 2 else CB
                                act.wait_ge(s["proj_ready"], at(b, 6, u + 1))
                                a.activation(pad[0:n, m, 1 + hf * RH:1 + (hf + 1) * RH, 1:1 + WW],
                                             bank[2 + u % 2][0:n, :].rearrange("p (h w) -> p h w", w=WW),
                                             ACT.Copy).then_inc(s["pad_copied"], 1)

                        return [square, nothing, nothing] + [lambda n_=n_: pad_copy(n_) for n_ in range(3)]

                    def image(b, pieces):
                        act.wait_ge(s["dtabs_ready"], at(b, 1, 1))
                        a.activation(dte[:, :], dta[:, :], ACT.Exp, scale=-1.0).then_inc(s["dte_ready"], 1)
                        act.wait_ge(s["dte_ready"], at(b, 1, 1))
                        a.activation(dtl[:, :], dte[:, :], ACT.Ln, bias=1.0).then_inc(s["dtln_ready"], 1)
                        act.wait_ge(s["t_ready"], at(b, NC, 0))
                        a.activation(x_st[:, :], x_in_sb[:, :], ACT.Copy).then_inc(s["xst_ready"], 1)
                        act.wait_ge(s["yg_ready"], at(b, NC, 0))
                        def weigh(tap):
                            r, c0 = tap // TAPS, tap % TAPS
                            act.wait_ge(s["tap_added"], at(b, TAPS * TAPS, max(tap - 2, 0)))
                            a.activation(weighed[tap % 3].rearrange("p (h w) -> p h w", w=WW),
                                         pad[0:CB, 2, r:r + HH, c0:c0 + WW], ACT.Copy, scale=cw[0:CB, 2, tap:tap + 1]
                                         ).then_inc(s["tap_scaled"], 1)

                        for c in range(NC + 1):
                            if c < NC:
                                act.wait_ge(s["zproj_ready"], at(b, NC, c + 1))
                                a.activation(zs[:, c, :], bank[4 + c % 2][:, 0:DI], ACT.Silu).then_inc(s["z_ready"], 1)
                            if c == 0:
                                act.wait_ge(s["pad_copied"], at(b, 6, 6))
                            weigh(c)
                        act.wait_ge(s["tok_ready"], at(b, NC, 0))
                        act.wait_ge(s["y_ready"], at(b, NC, 0))
                        for m in range(2):
                            act.wait_ge(s["conv_done"], at(b, 2, m + 1))
                            a.activation(xsC[:, m, :], acc[:, m, :], ACT.Silu, bias=cb[:, m:m + 1]).then_inc(s["xs_ready"], 1)
                        act.wait_ge(s["tap_added"], at(b, TAPS * TAPS, TAPS * TAPS))
                        for j in range(2):
                            a.activation(BC[:, j, :], acc[j * NS:(j + 1) * NS, 2, :], ACT.Silu,
                                         bias=cb[j * NS:(j + 1) * NS, 2:3]).then_inc(s["xs_ready"], 1)
                        act.wait_ge(s["nacs_ready"], at(b, 1, 1))
                        a.activation(eAcs[:, :], nAcs[:, :], ACT.Exp, scale=-1.0).then_inc(s["eacs_ready"], 1)

                        def chunk_in(c):
                            if c == 0:
                                act.wait_ge(s["st_ready"], at(b, NC, 0))
                                act.wait_ge(s["dx_ready"], at(b, NC, 0))
                            act.wait_ge(s["tok_ready"], at(b, NC, c + 1))
                            a.activation(tok[:, c, :], bank[c % 2][:, 0:DI + NS], ACT.Copy).then_inc(s["tok_copied"], 1)
                            act.wait_ge(s["seg_ready"], at(b, NC, c + 1))
                            act.wait_ge(s["xd_ready"], at(b, NC, max(c - 1, 0)))
                            act.wait_ge(s["gl_ready"], at(b, NC, max(c - 1, 0)))
                            for h in range(NH):
                                a.activation(Ldec[:, c % 2, h, :], bank[2 + h // 4][:, (h % 4) * P:(h % 4 + 1) * P], ACT.Exp,
                                             bias=nAcs[:, c * NH + h:c * NH + h + 1])
                            if c == 0:
                                act.wait_ge(s["state_ready"], at(b, NC, 0))
                            for j in range(2):
                                last = a.activation(edec[:, c, 4 * j:4 * j + 4],
                                                    bank[2 + j][0:NS, :].rearrange("p (h q) -> p h q", q=P)[:, :, P - 1],
                                                    ACT.Exp)
                            last.then_inc(s["decay_ready"], 1)

                        def chunk_sq(c):
                            act.wait_ge(s["yg_ready"], at(b, NC, c + 1))
                            if c == 0:
                                act.wait_ge(s["yn_ready"], at(b, NC, 0))
                            act.wait_ge(s["ssq_ready"], at(b, NC, c))
                            a.activation(ysq[:, :], y1[:, c % 2, :], ACT.Square, scale=DI ** -0.5,
                                         accum_out=ssq[:, c:c + 1]).then_inc(s["ssq_ready"], 1)

                        def chunk_yT(c):
                            act.wait_ge(s["yT_ready"], at(b, NC, c + 1))
                            act.wait_ge(s["t_ready"], at(b, NC, max(c - 1, 0)))
                            a.activation(yT[:, c % 2, :, :], bank[6][:, 0:256].rearrange("p (j q) -> p j q", q=P),
                                         ACT.Copy).then_inc(s["yT_copied"], 1)

                        def chunk_xnT(c):
                            act.wait_ge(s["xnT_ready"], at(b, NC, c + 1))
                            a.activation(xT_all[:, tile_at(b * NC + c), :].rearrange("p a q -> p (a q)"),
                                         bank[6][:, 256:384], ACT.Copy).then_inc(s["xnT_copied"], 1)

                        for step in range(NC + 6):
                            for f, lag in ((chunk_in, 0), (chunk_sq, 2), (chunk_yT, 3), (chunk_xnT, 6)):
                                if 0 <= step - lag < NC:
                                    f(step - lag)
                            piece_of(pieces, step)

                    images(act, ahead, image)

                @block.vector
                def _(dve):
                    v = nc.vector
                    for j in range(5):
                        n = P if j < 4 else 72
                        dve.wait_ge(setup_T, j + 1)
                        v.tensor_copy(inT[:, j * P:j * P + n], bank[j % 2][:, 0:n]).then_inc(setup_copied, 1)
                    for j in range(2):
                        dve.wait_ge(setup_T, 6 + j)
                        v.tensor_scalar(outT[:, j, :], bank[(5 + j) % 2][:, 0:P], rmsw[:, j:j + 1], None,
                                        ALU.mult).then_inc(setup_copied, 1)
                    dve.wait_ge(a_exp, 1)
                    v.tensor_scalar(aneg[:, :], aexp[:, :], -1.0, None, ALU.mult).then_inc(a_neg, 1)
                    dve.wait_ge(a_neg, 1)
                    dve.wait_ge(s["x_in"], 16)
                    made = [0]

                    def link(ins, b):
                        made[0] += 1
                        ins.then_inc(s["dve_step"], 1)
                        dve.wait_ge(s["dve_step"], b * DVE_STEPS + made[0])

                    def ahead(b):
                        before = b - 1 if not isinstance(b, int) or b else 0

                        def centre():
                            for hf in range(2):
                                sl = slice(hf * HALF, (hf + 1) * HALF)
                                dve.wait_ge(s["mean_ready"], at(b, 2, hf + 1))
                                v.tensor_tensor(xc[:, sl], x_in_sb[:, sl],
                                                bank[hf][:, :], ALU.subtract).then_inc(s["xc_ready"], 1)

                        def variance():
                            dve.wait_ge(s["zproj_ready"], at(b, NC, 0))
                            dve.wait_ge(s["xc_ready"], at(b, 2, 2))
                            dve.wait_ge(s["var_ready"], at(b, 1, 1))
                            v.tensor_scalar(rstd[:, :], bank[0][:, 0:NC], EPS, None, ALU.add).then_inc(s["var_drained"], 1)

                        def normalise():
                            for hf in range(2):
                                sl = slice(hf * HALF, (hf + 1) * HALF)
                                dve.wait_ge(s["rstd_rows"], at(b, 2, hf + 1))
                                link(v.tensor_tensor(xn[:, sl], xc[:, sl], bank[hf][:, :], ALU.mult), before)
                                v.tensor_scalar(xn[:, sl], xn[:, sl], lnw[:, :], lnb[:, :], ALU.mult, ALU.add
                                                ).then_inc(s["xn_ready"], 1)

                        return [centre, variance, normalise]

                    def image(b, pieces):
                        made[0] = 2

                        dve.wait_ge(s["dtproj_ready"], at(b, 1, 1))
                        link(v.tensor_tensor(dtr[:, :].rearrange("p (c h) -> p c h", h=NH),
                                             bank[6][:, 0:NC * NH].rearrange("p (c h) -> p c h", h=NH),
                                             dtb[:, :].unsqueeze(1).to_broadcast([P, NC, NH]), ALU.add), b)
                        v.scalar_tensor_tensor(dta[:, :], dtr[:, :], -1.0, dtr[:, :], ALU.mult, ALU.max
                                               ).then_inc(s["dtabs_ready"], 1)

                        def conv(m):
                            dst = acc[:, m, :].rearrange("p (h w) -> p h w", w=WW)
                            for tap in range(TAPS * TAPS):
                                r, c0 = tap // TAPS, tap % TAPS
                                win = pad[:, m, r:r + HH, c0:c0 + WW]
                                if tap == 0:
                                    ins = v.tensor_scalar(dst, win, cw[:, m, 0:1], None, ALU.mult)
                                else:
                                    ins = v.scalar_tensor_tensor(dst, win, cw[:, m, tap:tap + 1], dst, ALU.mult, ALU.add)
                                if tap < TAPS * TAPS - 1:
                                    link(ins, b)
                            ins.then_inc(s["conv_done"], 1)

                        dve.wait_ge(s["pad_copied"], at(b, 6, 6))
                        dve.wait_ge(s["xs_ready"], at(b, 4, 0))
                        conv(0)
                        dve.wait_ge(s["dtln_ready"], at(b, 1, 1))
                        dve.wait_ge(s["xdt_ready"], at(b, NC, 0))
                        link(v.scalar_tensor_tensor(dt[:, :], dtr[:, :], 0.0, dtl[:, :], ALU.max, ALU.add), b)
                        dve.wait_ge(s["seg_ready"], at(b, NC, 0))
                        v.tensor_tensor(dA[:, :].rearrange("p (c h) -> p c h", h=NH),
                                        dt[:, :].rearrange("p (c h) -> p c h", h=NH),
                                        aneg[:, :].unsqueeze(1).to_broadcast([P, NC, NH]), ALU.mult).then_inc(s["dA_ready"], 1)
                        conv(1)
                        dve.wait_ge(s["acs_ready"], at(b, 1, 1))
                        dve.wait_ge(s["decay_ready"], at(b, NC, 0))
                        v.tensor_scalar(nAcs[:, :], bank[6][:, 64:128], -1.0, None, ALU.mult).then_inc(s["nacs_ready"], 1)

                        def chunk_norm(c):
                            dve.wait_ge(s["rs_ready"], at(b, NC, c + 1))
                            dve.wait_ge(s["yT_ready"], at(b, NC, max(c - 1, 0)))
                            v.tensor_scalar(yn[:, c % 2, :], y1[:, c % 2, :], rs[:, c:c + 1], None, ALU.mult
                                            ).then_inc(s["yn_ready"], 1)

                        def chunk_in(c):
                            dve.wait_ge(s["decay_ready"], at(b, NC, c + 1))
                            dve.wait_ge(s["tok_copied"], at(b, NC, c + 1))
                            dve.wait_ge(s["y_ready"], at(b, NC, max(c - 1, 0)))
                            v.tensor_tensor(GL[:, c % 2, :, :], Ldec[:, c % 2, :, :],
                                            bank[c % 2][:, 384:512].unsqueeze(1).to_broadcast([P, NH, P]), ALU.mult
                                            ).then_inc(s["gl_ready"], 1)
                            dve.wait_ge(s["xdt_ready"], at(b, NC, c + 1))
                            dve.wait_ge(s["st_ready"], at(b, NC, max(c - 1, 0)))
                            v.tensor_tensor(Xd[:, c % 2, :].rearrange("p (h d) -> p h d", d=HD),
                                            xdt[:, c % 2, :].rearrange("p (h d) -> p h d", d=HD),
                                            Ldec[:, c % 2, :, P - 1:P].to_broadcast([P, NH, HD]), ALU.mult
                                            ).then_inc(s["xd_ready"], 1)

                        def chunk_y(c):
                            dve.wait_ge(s["st_ready"], at(b, NC, c + 1))
                            dve.wait_ge(s["y_ready"], at(b, NC, c + 1))
                            if c == 0:
                                v.tensor_copy(S[:, :], bank[5][0:NS, 0:DI]).then_inc(s["state_ready"], 1)
                                dve.wait_ge(s["dx_ready"], at(b, NC, c + 1))
                                ins = v.tensor_tensor(y1[:, c % 2, :], bank[4][:, DI:2 * DI], dx[:, c % 2, :], ALU.add)
                                ins.then_inc(s["y_drained"], 1)
                                dve.wait_ge(s["y_drained"], at(b, NC, c + 1))
                            else:
                                link(v.tensor_tensor(S[:, :].rearrange("p (h d) -> p h d", d=HD),
                                                     S[:, :].rearrange("p (h d) -> p h d", d=HD),
                                                     edec[:, c, :].unsqueeze(2).to_broadcast([NS, NH, HD]), ALU.mult), b)
                                v.tensor_tensor(S[:, :], S[:, :], bank[5][0:NS, 0:DI], ALU.add).then_inc(s["state_ready"], 1)
                                if c == 1:
                                    dve.wait_ge(s["eacs_ready"], at(b, 1, 1))
                                link(v.tensor_tensor(y1[:, c % 2, :].rearrange("p (h d) -> p h d", d=HD),
                                                     bank[4][:, 0:DI].rearrange("p (h d) -> p h d", d=HD),
                                                     eAcs[:, c * NH:(c + 1) * NH].unsqueeze(2).to_broadcast([P, NH, HD]), ALU.mult), b)
                                ins = v.tensor_tensor(y1[:, c % 2, :], y1[:, c % 2, :], bank[4][:, DI:2 * DI], ALU.add)
                                ins.then_inc(s["y_drained"], 1)
                                dve.wait_ge(s["y_drained"], at(b, NC, c + 1))
                                dve.wait_ge(s["dx_ready"], at(b, NC, c + 1))
                                link(v.tensor_tensor(y1[:, c % 2, :], y1[:, c % 2, :], dx[:, c % 2, :], ALU.add), b)
                            if c == 0:
                                dve.wait_ge(s["z_ready"], at(b, NC, NC))
                            v.tensor_tensor(y1[:, c % 2, :], y1[:, c % 2, :], zs[:, c, :], ALU.mult).then_inc(s["yg_ready"], 1)

                        def chunk_ln(c):
                            tile = t_all[:, tile_at(b * NC + c), :].rearrange("p a q -> p (a q)")
                            dve.wait_ge(s["ve_ready"], at(b, NC, max(c - 1, 0)))
                            dve.wait_ge(s["t_ready"], at(b, NC, c + 1))
                            v.tensor_copy(tile, bank[7][:, 0:P]).then_inc(s["t_drained"], 1)
                            dve.drain()
                            v.bn_stats(st6[:, :], tile)
                            dve.drain()
                            v.bn_aggr(mv[:, c % 2, :], st6[:, :]).then_inc(s["mv_ready"], 1)

                        def chunk_lnx(c):
                            tile = t_all[:, tile_at(b * NC + c), :].rearrange("p a q -> p (a q)")
                            dve.wait_ge(s["rs2_ready"], at(b, NC, c + 1))
                            dve.wait_ge(s["xnT_ready"], at(b, NC, max(c - 1, 0)))
                            v.tensor_scalar(xnt[:, c % 2, :], tile, mv[:, c % 2, 0:1], rs2[:, c % 2:c % 2 + 1], ALU.subtract, ALU.mult
                                            ).then_inc(s["lnx_ready"], 1)

                        for step in range(NC + 5):
                            for f, lag in ((chunk_norm, 3), (chunk_in, 0), (chunk_y, 1), (chunk_ln, 4), (chunk_lnx, 5)):
                                if 0 <= step - lag < NC:
                                    f(step - lag)
                            piece_of(pieces, step)
                        assert not pieces or made[0] == DVE_STEPS + 2, made[0]

                    images(dve, ahead, image)


        with ExitStack() as attn:
            def sb2(name, shape, dt=F32):
                return attn.enter_context(nc.sbuf_tensor(name, shape, dt))

            wuT = sb2("wuT", [P, NH, P])
            w_raw = sb2("w_raw", [P, 2, P])
            qk_w = sb2("qk_w", [P, NH, 2, P], F32R)
            vu_w = sb2("vu_w", [P, NH, P])
            qk_st = sb2("qk_st", [P, 2, P], F32R)
            vu_st = sb2("vu_st", [P, P])
            bu_col = sb2("bu_col", [P, 1])
            x_at = wq[:, :, :].rearrange("p h d -> p (h d)")
            xT = sb2("xT", [P, 2, L], F32R)
            x_tok = sb2("x_tok", [P, NC, P])
            qT = sb2("qT", [P, 2, L], F32R)
            prob = sb2("prob", [P, 4, L])
            probT = [sb2("probT0", [P, NC // 2, HALF]), sb2("probT1", [P, NC, HALF])]
            att = sb2("att", [P, 2, HALF])
            oT = sb2("oT", [P, L])
            nmax = sb2("nmax", [P, NC])
            rsum = sb2("rsum", [P, NC])
            rinv = sb2("rinv", [P, NC])

            a = {n: sem(n) for n in """w_filled w_copied w_high bu_in x_at_ready xT_ready qk_st_ready vu_st_ready
                bank4_filled bank5_filled bank4_drained bank5_drained u_filled u_drained q_filled q_high q_drained
                o_filled o_drained x6_filled x7_filled x6_drained x7_drained sum1_filled sum3_filled sum1_drained
                sum3_drained scores_ready nmax_ready prob_ready rinv_ready scaled""".split()}
            start_at_one(a, ("w_filled", "w_copied", "w_high", "bu_in"))
            t_filled = [a["bank4_filled"], a["bank5_filled"]]
            t_drained = [a["bank4_drained"], a["bank5_drained"]]
            x_filled, x_drained = [a["x6_filled"], a["x7_filled"]], [a["x6_drained"], a["x7_drained"]]
            sum_filled, sum_drained = [a["sum1_filled"], a["sum3_filled"]], [a["sum1_drained"], a["sum3_drained"]]

            GROUPS = [(i, g) for i in range(NC) for g in range(0, i + 1, 4)]
            assert len(GROUPS) % 2 == 0
            TURNS = len(GROUPS) // 2

            def at_least_one(n, per, k):
                count = at(n, per, k)
                return max(count, 1) if isinstance(count, int) else count

            def turned(g, i, k):
                n = sum(1 for x in GROUPS if x[0] <= i)
                return at_least_one(g, TURNS, (n + 1 - k) // 2)

            STEPS = [
                [("T", "last", 5), ("U", "last", 0, 1, 4)],
                [("T", "last", 6), ("O", "last", 0)],
                [("T", "last", 7)],
                [("T", "this", 0), ("U", "last", 1, 0, 2)],
                [("T", "this", 1), ("U", "last", 1, 2, 4)],
                [("T", "this", 2), ("U", "last", 1, 4, 6), ("Q", "next", 0)],
                [("T", "this", 3), ("U", "last", 1, 6, 8)],
                [("T", "this", 4), ("O", "last", 1), ("U", "this", 0, 0, 1), ("Q", "next", 1)],
            ]
            EXTRA = {0: {0: [("Q", "this", 0)], 2: [("Q", "this", 1)], 6: [("X", "this")]},
                     1: {0: [("S", "sum", 0)], 1: [("S", "sum", 1)]}}

            def first_of(h):
                return isinstance(h, int) and h == 0

            def second_of(h):
                return isinstance(h, int) and h == 1

            def items(step, g, h, skipped):
                extra = EXTRA.get(h, {}).get(step, []) if isinstance(h, int) else []
                where_extra = 1 if second_of(h) else len(STEPS[step])
                for kind, whose, *rest in STEPS[step][:where_extra] + extra + STEPS[step][where_extra:]:
                    if whose not in skipped:
                        yield kind, {"last": g - 1, "this": g, "next": g + 1, "sum": None}[whose], rest

            def images(engine, image_start, head):
                def image(b, first):
                    if image_start:
                        image_start(b)
                    g = b * NH
                    head(b, 0, g, ("last",) if first else ())
                    head(b, 1, g + 1, ("sum",) if first else ())
                    with engine.Fori(2, NH - 1) as h:
                        head(b, h, g + h, ())
                    head(b, NH - 1, g + NH - 1, ("next",))

                image(0, True)
                with engine.Fori(1, B) as b:
                    image(b, False)
                head(B, NH, B * NH, ("this", "next"))

            with nc.Block() as block:
                @block.sync
                def _(sp):
                    sp.dma_start(bu_col[:, :], bu.rearrange("(n a) -> n a", a=1)).then_inc(a["bu_in"], 16)

                @block.gpsimd
                def _(pool):
                    g_ = nc.gpsimd

                    def scale(hh, i):
                        w = (i + 1) * P
                        pool.wait_ge(a["rinv_ready"], at(hh, NC, i + 1))
                        g_.tensor_tensor(prob[:, i % 4, 0:w], prob[:, i % 4, 0:w], rinv[:, i:i + 1].to_broadcast([P, w]),
                                         ALU.mult).then_inc(a["scaled"], 1)

                    with pool.Fori(0, B * NH) as hh:
                        for i in range(NC):
                            scale(hh, i)

                @block.tensor
                def _(pe):
                    t = nc.tensor

                    def mm3(out_, left, right, start, stop):
                        t.matmul(out_, left[1], right[0], start=start, stop=False)
                        t.matmul(out_, left[0], right[1], start=False, stop=False)
                        return t.matmul(out_, left[0], right[0], start=False, stop=stop)

                    def parts(x, *where):
                        return x[(slice(None), 0) + where], x[(slice(None), 1) + where]

                    pe.wait_ge(attn_in, 16 * 4)
                    for h in range(NH):
                        if h >= 2:
                            pe.wait_ge(a["w_copied"], h - 1)
                        t.transpose(bank[h % 2][:, 0:P], wu[:, h * P:(h + 1) * P], ident[:, :]).then_inc(a["w_filled"], 1)
                    for h in range(NH):
                        pe.wait_ge(a["w_copied"], NH + max(h - 1, 0))
                        t.matmul(bank[h % 2][:, 0:P], wq[:, h, :], wk[:, h, :], start=True, stop=True)
                        t.matmul(bank[h % 2][:, P:2 * P], wv[:, h, :], wuT[:, h, :], start=True,
                                 stop=True).then_inc(a["w_filled"], 1)

                    def scores(b, h, g, i):
                        if i in (0, 4):
                            pe.wait_ge(a["q_drained"], at_least_one(g, 2, i // 4 + 1))
                        if second_of(h) and i in (4, 5):
                            pe.wait_ge(sum_drained[i - 4], at_least_one(b, 1, 0))
                        pe.wait_ge(a["prob_ready"], at_least_one(g, NC, i - 1))
                        w = (i + 1) * P
                        for j in range((w + HALF - 1) // HALF):
                            n = min(HALF, w - j * HALF)
                            diag = i * P - j * HALF
                            last_j = w <= (j + 1) * HALF
                            last = mm3(bank[2 * (i % 2) + j][:, 0:n], parts(qT, slice(i * P, (i + 1) * P)),
                                       parts(xT, slice(j * HALF, j * HALF + n)), True, not last_j)
                            if last_j:
                                last = t.matmul(bank[2 * (i % 2) + j][:, diag:diag + P], ident_bf[:, :],
                                                mask_ahead[:, :], start=False, stop=True)
                        last.then_inc(a["scores_ready"], 1)

                    def turn(g, i):
                        pe.wait_ge(a["scaled"], at_least_one(g, NC, i + 1))
                        for n, (i_, first_kt) in enumerate(GROUPS):
                            if i_ == i:
                                k = n % 2
                                pe.wait_ge(t_drained[k], at_least_one(g, TURNS, n // 2))
                                for kt in range(first_kt, min(first_kt + 4, i + 1)):
                                    last = t.transpose(bank[4 + k][:, (kt - first_kt) * P:(kt - first_kt + 1) * P],
                                                       prob[:, i % 4, kt * P:(kt + 1) * P], ident[:, :])
                                last.then_inc(t_filled[k], 1)

                    def turn_four(to, source, half):
                        for j in range(4):
                            last = t.transpose(to[:, j * P:(j + 1) * P], source[:, (4 * half + j) * P:(4 * half + j + 1) * P],
                                               ident[:, :])
                        return last

                    def attend(g, half, kt0, kt1):
                        if kt0 == 0:
                            pe.wait_ge(a["u_drained"], at_least_one(g, 2, half))
                            for k in range(2):
                                pe.wait_ge(t_drained[k], turned(g, 4 * half + 3, k))
                        for kt in range(kt0, kt1):
                            q0 = max(0, kt - 4 * half) * P
                            last = t.matmul(bank[6][:, q0:HALF], x_tok[:, kt, :], probT[half][:, kt, q0:HALF],
                                            start=kt == 0, stop=kt == 4 * half + 3)
                        if kt1 == 4 * half + 4:
                            last.then_inc(a["u_filled"], 1)

                    def bank7_free(queries, outputs):
                        pe.wait_ge(a["q_drained"], at_least_one(queries, 1, 0))
                        pe.wait_ge(a["o_drained"], at_least_one(outputs, 1, 0))

                    def output(g, half):
                        pe.wait_ge(a["vu_st_ready"], at_least_one(g, 1, 1))
                        pe.wait_ge(a["u_drained"], at_least_one(g, 2, half + 1))
                        t.matmul(bank[7][:, :], vu_st[:, :], att[:, half, :], start=True, stop=True).then_inc(a["o_filled"], 1)

                    def queries(g, half):
                        pe.wait_ge(a["qk_st_ready"], at_least_one(g, 1, 1))
                        mm3(bank[7][:, :], parts(qk_st, slice(None)), parts(xT, slice(half * HALF, (half + 1) * HALF)),
                            True, True).then_inc(a["q_filled"], 1)

                    def turn_sum(b, k):
                        pe.wait_ge(a["o_drained"], at_least_one(b, 2 * NH, 0))
                        turn_four(bank[1 + 2 * k], oT, k).then_inc(sum_filled[k], 1)

                    def head(b, h, g, skipped):
                        for step in range(NC):
                            first = first_of(h) and step == 0
                            if "this" not in skipped and not first:
                                scores(b, h, g, step)
                            for kind, g_, rest in items(step, g, h, skipped):
                                if kind == "T":
                                    turn(g_, *rest)
                                elif kind == "U":
                                    if first_of(h) and step == 7:
                                        for k in range(2):
                                            pe.wait_ge(x_drained[k], at_least_one(b, 1, 1))
                                    attend(g_, *rest)
                                elif kind == "O":
                                    made = 2 * g + (1 if first_of(h) else 2) if step == 1 else 2 * g + (2 if "next" in skipped else 3)
                                    if "this" in skipped:
                                        made = 2 * g
                                    if first_of(h) and step == 7:
                                        pe.wait_ge(x_drained[1], at_least_one(b, 1, 1))
                                    bank7_free(made, 2 * g_ + rest[0])
                                    output(g_, *rest)
                                elif kind == "Q":
                                    if first:
                                        pe.wait_ge(a["xT_ready"], at_least_one(b, 1, 1))
                                    bank7_free(2 * g_ + rest[0], 2 * g - {0: 2, 2: 1, 5: 1, 7: 0}[step])
                                    queries(g_, *rest)
                                elif kind == "X":
                                    pe.wait_ge(a["x_at_ready"], at_least_one(b, 1, 1))
                                    pe.wait_ge(a["u_drained"], at_least_one(g, 2, 0))
                                    turn_four(bank[6], x_at, 0).then_inc(x_filled[0], 1)
                                    bank7_free(2 * g + 3, 2 * g - 1)
                                    turn_four(bank[7], x_at, 1).then_inc(x_filled[1], 1)
                                else:
                                    pe.wait_ge(a["prob_ready"], at_least_one(g - 1, NC, NC - 1 + rest[0]))
                                    turn_sum(b, *rest)
                            if "this" not in skipped and first:
                                scores(b, h, g, step)

                    images(pe, None, head)
                    for k in range(2):
                        turn_sum(B, k)

                def turned_groups(i):
                    for n, (i_, first_kt) in enumerate(GROUPS):
                        if i_ == i:
                            m_ = min(4, i + 1 - first_kt)
                            yield (n, n % 2, probT[i // 4][:, first_kt:first_kt + m_, (i % 4) * P:(i % 4 + 1) * P],
                                   bank[4 + n % 2][:, 0:m_ * P].rearrange("p (k q) -> p k q", q=P))

                def four_tiles(source):
                    return source[:, :].rearrange("p (k q) -> p k q", q=P)

                def tiles_of(b, first_tile, n):
                    t0 = b * NC + first_tile
                    return slice(t0, t0 + n) if isinstance(b, int) else bass.ds(t0, n)

                @block.scalar
                def _(act):
                    s_ = nc.scalar

                    def exponentials(g, i, skipped):
                        act.wait_ge(a["nmax_ready"], at_least_one(g, NC, i + 1))
                        if i >= 4 or "last" not in skipped:
                            for k in range(2):
                                act.wait_ge(t_filled[k], turned(g if i >= 4 else g - 1, (i + 4) % NC, k))
                        w = (i + 1) * P
                        s_.activation(prob[:, i % 4, 0:w], psum_pair(2 * (i % 2), w), ACT.Exp, bias=nmax[:, i:i + 1],
                                      accum_out=rsum[:, i:i + 1]).then_inc(a["prob_ready"], 1)

                    def head(b, h, g, skipped):
                        for step in range(NC):
                            first = first_of(h) and step == 0
                            work = list(items(step, g, h, skipped))
                            for kind, g_, rest in work:
                                if kind == "T":
                                    for n, k, where, source in turned_groups(rest[0]):
                                        if k == 0:
                                            act.wait_ge(t_filled[0], at_least_one(g_, TURNS, n // 2 + 1))
                                            s_.activation(where, source, ACT.Copy).then_inc(t_drained[0], 1)
                            if "this" not in skipped and not first:
                                exponentials(g, step, skipped)
                            if first_of(h) and step == 1:
                                for k in range(2):
                                    act.wait_ge(x_filled[k], at_least_one(b, 1, 0))
                                s_.activation(four_tiles(x_at), xT_all[:, tiles_of(b, 0, NC), :], ACT.Copy
                                              ).then_inc(a["x_at_ready"], 1)
                            for kind, g_, rest in work:
                                if kind == "U" and rest[2] == 4 * rest[0] + 4:
                                    half = rest[0]
                                    act.wait_ge(a["u_filled"], at_least_one(g_, 2, half + 1))
                                    act.wait_ge(a["o_filled"], at_least_one(g_, 2, half - 1))
                                    s_.activation(att[:, half, :], bank[6][:, :], ACT.Copy).then_inc(a["u_drained"], 1)
                                elif kind == "Q":
                                    half = rest[0]
                                    act.wait_ge(a["q_filled"], at_least_one(g_, 2, half + 1))
                                    s_.activation(qT[:, 0, half * HALF:(half + 1) * HALF], bank[7][:, :], ACT.Copy
                                                  ).then_inc(a["q_high"], 1)
                                elif kind == "X":
                                    act.wait_ge(x_filled[0], at_least_one(b, 1, 1))
                                    s_.activation(x_tok[:, 0:4, :], four_tiles(bank[6]), ACT.Copy).then_inc(x_drained[0], 1)
                            if "this" not in skipped and first:
                                exponentials(g, step, skipped)

                    images(act, None, head)

                @block.vector
                def _(dve):
                    v = nc.vector
                    for h in range(NH):
                        dve.wait_ge(a["w_filled"], h + 1)
                        v.tensor_copy(wuT[:, h, :], bank[h % 2][:, 0:P]).then_inc(a["w_copied"], 1)
                    for h in range(NH):
                        dve.wait_ge(a["w_filled"], NH + h + 1)
                        v.tensor_scalar(w_raw[:, h % 2, :], bank[h % 2][:, 0:P], P ** -0.5, None, ALU.mult)
                        v.tensor_copy(vu_w[:, h, :], bank[h % 2][:, P:2 * P]).then_inc(a["w_copied"], 1)
                        dve.wait_ge(a["w_copied"], NH + h + 1)
                        v.tensor_copy(qk_w[:, h, 0, :], w_raw[:, h % 2, :]).then_inc(a["w_high"], 1)
                        dve.wait_ge(a["w_high"], 2 * h + 1)
                        v.tensor_tensor(qk_w[:, h, 1, :], w_raw[:, h % 2, :], qk_w[:, h, 0, :].bitcast(F32), ALU.subtract
                                        ).then_inc(a["w_high"], 1)
                    dve.wait_ge(a["w_high"], 2 * NH)
                    dve.wait_ge(a["bu_in"], 16)

                    def low_query(g, half):
                        cols = slice(half * HALF, (half + 1) * HALF)
                        dve.wait_ge(a["q_high"], at_least_one(g, 2, half + 1))
                        v.tensor_tensor(qT[:, 1, cols], bank[7][:, :], qT[:, 0, cols].bitcast(F32), ALU.subtract
                                        ).then_inc(a["q_drained"], 1)

                    def add(g, half, to_bias):
                        where_ = oT[:, half * HALF:(half + 1) * HALF]
                        dve.wait_ge(a["o_filled"], at_least_one(g, 2, half + 1))
                        if to_bias:
                            v.tensor_scalar(where_, bank[7][:, :], bu_col[:, 0:1], None, ALU.add).then_inc(a["o_drained"], 1)
                        else:
                            dve.wait_ge(a["o_drained"], at_least_one(g, 2, half - 1))
                            v.tensor_tensor(where_, bank[7][:, :], where_, ALU.add).then_inc(a["o_drained"], 1)

                    def add_sum(b, k):
                        dve.wait_ge(sum_filled[k], at_least_one(b, 1, 0))
                        tiles = t_all[:, tiles_of(b - 1, 4 * k, 4), :]
                        v.tensor_tensor(tiles, four_tiles(bank[1 + 2 * k]), tiles, ALU.add).then_inc(sum_drained[k], 1)

                    def norm(g, i):
                        dve.wait_ge(a["prob_ready"], at_least_one(g, NC, i + 1))
                        v.reciprocal(rinv[:, i:i + 1], rsum[:, i:i + 1]).then_inc(a["rinv_ready"], 1)

                    def maximum(g, i):
                        dve.wait_ge(a["scores_ready"], at_least_one(g, NC, i + 1))
                        v.reduce_max(nmax[:, i:i + 1], psum_pair(2 * (i % 2), (i + 1) * P), AX, negate=True
                                     ).then_inc(a["nmax_ready"], 1)

                    def stage(weights, h):
                        letters = "s q" if len(weights.shape) == 4 else "q"
                        mine = weights[:, h:h + 1] if isinstance(h, int) else weights[:, bass.ds(h, 1)]
                        return mine.rearrange(f"p a {letters} -> p (a {letters})")

                    def stage_queries(h):
                        v.tensor_copy(qk_st[:, :, :].rearrange("p s q -> p (s q)"), stage(qk_w, h).bitcast(F32)
                                      ).then_inc(a["qk_st_ready"], 1)

                    def image_start(b):
                        dve.wait_ge(a["scores_ready"], at_least_one(b, NH * NC, 0))
                        tokens = xT_all[:, tiles_of(b, 0, NC), :]
                        v.tensor_copy(four_tiles(xT[:, 0, :]), tokens)
                        dve.drain()
                        v.tensor_tensor(four_tiles(xT[:, 1, :]), tokens, four_tiles(xT[:, 0, :]).bitcast(F32), ALU.subtract
                                        ).then_inc(a["xT_ready"], 1)

                    def head(b, h, g, skipped):
                        for step in range(NC):
                            first = first_of(h) and step == 0
                            if "this" not in skipped and not first:
                                maximum(g, step)
                            if step == 0:
                                if "last" not in skipped:
                                    norm(g - 1, NC - 1)
                            elif "this" not in skipped:
                                norm(g, step - 1)
                            if step == 2 and "this" not in skipped:
                                if not first_of(h):
                                    stage_queries(0 if isinstance(h, int) and h == NH - 1 else h + 1)
                            for kind, g_, rest in items(step, g, h, skipped):
                                if kind == "T":
                                    if rest[0] in (1, 4):
                                        dve.wait_ge(a["u_filled"], at_least_one(g_, 2, rest[0] // 4 - 1))
                                    for n, k, where, source in turned_groups(rest[0]):
                                        if k == 1:
                                            dve.wait_ge(t_filled[1], at_least_one(g_, TURNS, n // 2 + 1))
                                            v.tensor_copy(where, source).then_inc(t_drained[1], 1)
                                elif kind == "Q":
                                    low_query(g_, rest[0])
                                elif kind == "O":
                                    add(g_, rest[0], second_of(h))
                                elif kind == "X":
                                    dve.wait_ge(x_filled[1], at_least_one(b, 1, 1))
                                    v.tensor_copy(x_tok[:, 4:8, :], four_tiles(bank[7])).then_inc(x_drained[1], 1)
                                elif kind == "S":
                                    add_sum(b, rest[0])
                            if first_of(h) and step == 3:
                                stage_queries(1)
                            if "this" not in skipped and step == NC - 1:
                                dve.wait_ge(a["o_filled"], at_least_one(g, 2, 0))
                                v.tensor_copy(vu_st[:, :], stage(vu_w, h)).then_inc(a["vu_st_ready"], 1)
                            if "this" not in skipped and first:
                                maximum(g, step)

                    stage_queries(0)
                    images(dve, image_start, head)
                    for k in range(2):
                        add_sum(B, k)

        until_experts.close()
        gates = sb("gates", [P, NT, E])
        x_high = sb("x_high", [P, NT, P], F32R)
        x_low = sb("x_low", [P, NT, P], F32R)
        with ExitStack() as rout:
            def sb3(name, shape, dt=F32):
                return rout.enter_context(nc.sbuf_tensor(name, shape, dt))

            router_nat = sb3("router_nat", [E, P])
            routerT = sb3("routerT", [P, E])
            st6b = sb3("st6b", [P, NC, 6])
            mvb = sb3("mvb", [P, NC, 2])
            rsb = sb3("rsb", [P, NC])
            x2t = sb3("x2t", [P, 4, P])
            x2s = sb3("x2s", [P, 4, P])
            logits = sb3("logits", [P, NT, E])
            expo = sb3("expo", [P, NT, E])
            probs = sb3("probs", [P, NT, E])
            first = sb3("first", [P, NT, E])
            second = sb3("second", [P, NT, E])
            cand = sb3("cand", [P, NT, E])
            number = sb3("number", [P, E])
            best = sb3("best", [P, NT])
            best2 = sb3("best2", [P, NT])
            pick = sb3("pick", [P, NT])
            den = sb3("den", [P, NT])
            mhalf2 = sb3("mhalf2", [P, 1])
            epst2 = sb3("epst2", [P, 1])
            r = {n: sem(n) for n in """mvb_ready veb_ready rsb_ready x2_ready x2T_ready x2s_ready x2_high x2T_copied logits_ready
                logits_drained router_in routerT_ready routerT_copied consts2_made peak_off expo_ready gate_step""".split()}
            turn_bank = [bank[0], bank[1], bank[3], bank[4]]
            start_at_one(r, ("router_in", "routerT_ready", "routerT_copied", "consts2_made", "peak_off", "expo_ready", "gate_step"))
            with nc.Block() as block:
                @block.sync
                def _(sp):
                    sp.dma_start(router_nat[:, :], router_w).then_inc(r["router_in"], 16)

                @block.gpsimd
                def _(pool):
                    g = nc.gpsimd
                    g.memset(mhalf2[:, :], -0.5).then_inc(r["consts2_made"], 1)
                    g.memset(epst2[:, :], EPS).then_inc(r["consts2_made"], 1)
                    for e in range(E):
                        g.memset(number[:, e:e + 1], float(e)).then_inc(r["consts2_made"], 1)
                    pool.wait_ge(r["consts2_made"], 2 + E)
                    with pool.Fori(0, B) as b:
                        for half in range(2):
                            cols = slice(half * NC // 2, (half + 1) * NC // 2)
                            pool.wait_ge(r["mvb_ready"], at(b, NC, (half + 1) * NC // 2))
                            pool.wait_ge(r["x2_ready"], at(b, NC, 0))
                            g.tensor_tensor(rsb[:, cols], mvb[:, cols, 1], epst2[:, 0:1].to_broadcast([P, NC // 2]), ALU.add
                                            ).then_inc(r["veb_ready"], 1)
                            pool.wait_ge(r["veb_ready"], at(b, 2, half + 1))
                            g.tensor_tensor(rsb[:, cols], rsb[:, cols], mhalf2[:, 0:1].to_broadcast([P, NC // 2]), ALU.pow
                                            ).then_inc(r["rsb_ready"], 1)

                @block.vector
                def _(dve):
                    v = nc.vector
                    dve.wait_ge(r["routerT_ready"], 1)
                    v.tensor_copy(routerT[:, :], bank[0][:, 0:E]).then_inc(r["routerT_copied"], 1)
                    with dve.Fori(0, B) as b:
                        def stats(c):
                            tile = t_all[:, bass.ds(b * NC + c, 1), :].rearrange("p a q -> p (a q)")
                            v.bn_stats(st6b[:, c, :], tile)

                        def aggregate(c):
                            v.bn_aggr(mvb[:, c, :], st6b[:, c, :]).then_inc(r["mvb_ready"], 1)

                        def norm(c):
                            tile = t_all[:, bass.ds(b * NC + c, 1), :].rearrange("p a q -> p (a q)")
                            dve.wait_ge(r["rsb_ready"], at(b, 2, c // (NC // 2) + 1))
                            dve.wait_ge(r["x2T_ready"], at(b, NC, max(c - 3, 0)))
                            v.tensor_scalar(x2t[:, c % 4, :], tile, mvb[:, c, 0:1], rsb[:, c:c + 1],
                                            ALU.subtract, ALU.mult).then_inc(r["x2_ready"], 1)

                        def low(c):
                            tile = bass.ds(b * NC + c, 1)
                            dve.wait_ge(r["x2_high"], at(b, NC, c + 1))
                            v.tensor_tensor(x_low[:, tile, :].rearrange("p a q -> p (a q)"), turn_bank[c % 4][:, 0:P],
                                            x_high[:, tile, :].rearrange("p a q -> p (a q)").bitcast(F32), ALU.subtract
                                            ).then_inc(r["x2T_copied"], 1)

                        for half in range(2):
                            chunks = range(half * NC // 2, (half + 1) * NC // 2)
                            dve.drain()
                            for c in chunks:
                                stats(c)
                            dve.drain()
                            for c in chunks:
                                aggregate(c)
                        for c in range(NC + 3):
                            if c < NC:
                                norm(c)
                            if c > 2:
                                low(c - 3)
                        dve.wait_ge(r["logits_ready"], at(b, 1, 1))
                        v.tensor_copy(logits[:, bass.ds(b * NC, NC), :],
                                      bank[2][:, 0:NC * E].rearrange("p (c e) -> p c e", e=E)).then_inc(r["logits_drained"], 1)

                    k = [0]

                    def step(ins):
                        k[0] += 1
                        ins.then_inc(r["gate_step"], 1)
                        dve.wait_ge(r["gate_step"], k[0])

                    def wide(t):
                        return t[:, :].unsqueeze(2).to_broadcast([P, NT, E])

                    numbers = number[:, :].unsqueeze(1).to_broadcast([P, NT, E])
                    dve.wait_ge(r["logits_drained"], B + 1)
                    step(v.reduce_max(best[:, :], logits[:, :, :], AX))
                    v.tensor_tensor(logits[:, :, :], logits[:, :, :], wide(best), ALU.subtract).then_inc(r["peak_off"], 1)
                    dve.wait_ge(r["expo_ready"], 1)
                    step(v.tensor_reduce(den[:, :], expo[:, :, :], AX, ALU.add))
                    step(v.reciprocal(den[:, :], den[:, :]))
                    step(v.tensor_tensor(probs[:, :, :], expo[:, :, :], wide(den), ALU.mult))

                    def top(hot, value):
                        step(v.reduce_max(value[:, :], probs[:, :, :], AX))
                        step(v.tensor_tensor(cand[:, :, :], probs[:, :, :], wide(value), ALU.is_lt))
                        step(v.tensor_scalar(cand[:, :, :], cand[:, :, :], float(E), None, ALU.mult))
                        step(v.tensor_tensor(cand[:, :, :], cand[:, :, :], numbers, ALU.add))
                        step(v.tensor_reduce(pick[:, :], cand[:, :, :], AX, ALU.min))
                        step(v.tensor_tensor(hot[:, :, :], wide(pick), numbers, ALU.is_equal))

                    dve.wait_ge(r["consts2_made"], 2 + E)
                    top(first, best)
                    step(v.scalar_tensor_tensor(probs[:, :, :].rearrange("p t e -> p (t e)"), first[:, :, :].rearrange("p t e -> p (t e)"),
                                                -2.0, probs[:, :, :].rearrange("p t e -> p (t e)"), ALU.mult, ALU.add))
                    top(second, best2)
                    step(v.tensor_tensor(den[:, :], best[:, :], best2[:, :], ALU.add))
                    step(v.tensor_scalar(den[:, :], den[:, :], 1e-9, None, ALU.add))
                    step(v.reciprocal(den[:, :], den[:, :]))
                    step(v.tensor_tensor(best[:, :], best[:, :], den[:, :], ALU.mult))
                    step(v.tensor_tensor(best2[:, :], best2[:, :], den[:, :], ALU.mult))
                    step(v.tensor_tensor(first[:, :, :], first[:, :, :], wide(best), ALU.mult))
                    step(v.tensor_tensor(second[:, :, :], second[:, :, :], wide(best2), ALU.mult))
                    step(v.tensor_tensor(gates[:, :, :], first[:, :, :], second[:, :, :], ALU.add))

                @block.tensor
                def _(pe):
                    t = nc.tensor
                    pe.wait_ge(r["router_in"], 16)
                    t.transpose(bank[0][:, 0:E], router_nat[:, :], ident[0:E, 0:E]).then_inc(r["routerT_ready"], 1)
                    pe.wait_ge(r["routerT_copied"], 1)
                    with pe.Fori(0, B) as b:
                        def turn(c):
                            pe.wait_ge(r["x2_ready"], at(b, NC, c + 1))
                            pe.wait_ge(r["x2T_copied"], at(b, NC, max(c - 3, 0)))
                            t.transpose(turn_bank[c % 4][:, 0:P], x2t[:, c % 4, :], ident[:, :]).then_inc(r["x2T_ready"], 1)

                        def route(c):
                            if c == 0:
                                pe.wait_ge(r["logits_drained"], at(b, 1, 0))
                            pe.wait_ge(r["x2s_ready"], at(b, NC, c + 1))
                            return t.matmul(bank[2][:, c * E:(c + 1) * E], x2s[:, c % 4, :], routerT[:, :], start=True, stop=True)

                        for c in range(NC + 1):
                            if c < NC:
                                turn(c)
                            if c:
                                last = route(c - 1)
                                if c == NC:
                                    last.then_inc(r["logits_ready"], 1)

                @block.scalar
                def _(act):
                    a_ = nc.scalar
                    with act.Fori(0, B) as b:
                        for c in range(NC):
                            act.wait_ge(r["x2T_ready"], at(b, NC, c + 1))
                            a_.activation(x2s[:, c % 4, :], turn_bank[c % 4][:, 0:P], ACT.Copy).then_inc(r["x2s_ready"], 1)
                            a_.activation(x_high[:, bass.ds(b * NC + c, 1), :].rearrange("p a q -> p (a q)"),
                                          turn_bank[c % 4][:, 0:P], ACT.Copy).then_inc(r["x2_high"], 1)
                    act.wait_ge(r["peak_off"], 1)
                    a_.activation(expo[:, :, :], logits[:, :, :], ACT.Exp).then_inc(r["expo_ready"], 1)

        with ExitStack() as moe:
            def sb4(name, shape, dt=F32):
                return moe.enter_context(nc.sbuf_tensor(name, shape, dt))

            SUP = NT // 4
            BODY = 4
            assert SUP % BODY == 0
            ORDER = [("up", 0)] + [x for n in range(1, BODY) for x in (("up", n), ("down", n - 1))] + [("down", BODY - 1)]
            w1n = sb4("w1n", [P, NF, P])
            w3n = sb4("w3n", [P, NF, P])
            w2n = sb4("w2n", [P, HF])
            w1T = sb4("w1T", [P, 2, HF], F32R)
            w3T = sb4("w3T", [P, 2, HF], F32R)
            w2T = sb4("w2T", [P, NF * P])
            act1 = sb4("act1", [P, 2, HALF])
            hT = sb4("hT", [P, 2, NF, HALF])
            m = {n: sem(n) for n in """w_in wT_made wT_high wT_split up_ready silu_ready hid_ready
                down_ready down_drained""".split()}
            start_at_one(m, ("w_in",))
            LASTF = FCH[-1][1]
            with nc.Block() as block:
                @block.sync
                def _(sp):
                    with sp.Fori(0, E) as e:
                        sp.wait_ge(m["wT_made"], at(e, 1, 0))
                        for w, src in ((w1n, w1), (w3n, w3)):
                            sp.dma_start(w[:, 0:NF - 1, :], src[bass.ds(e, 1), 0:(NF - 1) * P, :].rearrange("a (j p) c -> p (a j) c", p=P)
                                         ).then_inc(m["w_in"], 16)
                            sp.dma_start(w[0:LASTF, NF - 1, :], src[bass.ds(e, 1), (NF - 1) * P:HF, :].rearrange("a p c -> p (a c)")
                                         ).then_inc(m["w_in"], 16)
                        sp.dma_start(w2n[:, :], w2[bass.ds(e, 1), :, :].rearrange("a p c -> p (a c)")).then_inc(m["w_in"], 16)

                @block.tensor
                def _(pe):
                    t = nc.tensor

                    def mm3(out_, left, right, start, stop):
                        t.matmul(out_, left[1], right[0], start=start, stop=False)
                        t.matmul(out_, left[0], right[1], start=False, stop=False)
                        return t.matmul(out_, left[0], right[0], start=False, stop=stop)

                    with pe.Fori(0, E) as e:
                        pe.wait_ge(m["w_in"], e * 80 + 80)
                        pe.wait_ge(m["down_drained"], at(e, SUP, 0))
                        pe.wait_ge(m["wT_split"], at(e, 1, 0))
                        for f, n in enumerate(x[1] for x in FCH):
                            t.transpose(bank[6][:, f * P:f * P + n], w1n[0:n, f, :], ident[0:n, 0:n])
                            t.transpose(bank[7][:, f * P:f * P + n], w3n[0:n, f, :], ident[0:n, 0:n])
                            last = t.transpose(bank[4][0:n, f * P:(f + 1) * P], w2n[:, f * P:f * P + n], ident[:, :])
                        last.then_inc(m["wT_made"], 1)
                        with pe.Fori(0, SUP // BODY) as sb_:
                            es = e * SUP + sb_ * BODY

                            def up(s):
                                group = bass.ds(sb_ * (4 * BODY) + 4 * s, 4)
                                x_ = (x_high[:, group, :].rearrange("p j q -> p (j q)"),
                                      x_low[:, group, :].rearrange("p j q -> p (j q)"))
                                for f, (f0, n) in enumerate(FCH):
                                    u = NF * s + f
                                    pe.wait_ge(m["hid_ready"], at(es, NF, max(u - 1, 0)))
                                    mm3(bank[u % 2][0:n, :], [w1T[:, part, f0:f0 + n] for part in range(2)], x_, True, True)
                                    mm3(bank[2 + u % 2][0:n, :], [w3T[:, part, f0:f0 + n] for part in range(2)], x_, True, True
                                        ).then_inc(m["up_ready"], 1)

                            def down(s):
                                pe.wait_ge(m["hid_ready"], at(es, NF, NF * (s + 1)))
                                pe.wait_ge(m["down_drained"], at(es, 1, max(s - 1, 0)))
                                for j in range(4):
                                    for f, (f0, n) in enumerate(FCH):
                                        last = t.matmul(bank[4 + s % 2][:, j * P:(j + 1) * P], hT[0:n, s % 2, f, j * P:(j + 1) * P],
                                                        w2T[0:n, f * P:(f + 1) * P], start=(f == 0), stop=(f == NF - 1))
                                last.then_inc(m["down_ready"], 1)

                            pe.wait_ge(m["wT_split"], at(e, 1, 1))
                            for what, s in ORDER:
                                (up if what == "up" else down)(s)

                @block.scalar
                def _(act):
                    a_ = nc.scalar
                    with act.Fori(0, E) as e:
                        act.wait_ge(m["wT_made"], at(e, 1, 1))
                        act.wait_ge(m["down_ready"], at(e, SUP, 0))
                        a_.activation(w1T[:, 0, :], bank[6][:, 0:HF], ACT.Copy)
                        a_.activation(w3T[:, 0, :], bank[7][:, 0:HF], ACT.Copy)
                        a_.activation(w2T[:, 0:(NF - 1) * P], bank[4][:, 0:(NF - 1) * P], ACT.Copy)
                        a_.activation(w2T[0:LASTF, (NF - 1) * P:NF * P], bank[4][0:LASTF, (NF - 1) * P:NF * P], ACT.Copy
                                      ).then_inc(m["wT_high"], 1)
                        with act.Fori(0, SUP // BODY) as sb_:
                            es = e * SUP + sb_ * BODY
                            def silu(u):
                                n = FCH[u % NF][1]
                                act.wait_ge(m["up_ready"], at(es, NF, u + 1))
                                act.wait_ge(m["hid_ready"], at(es, NF, max(u - 1, 0)))
                                a_.activation(act1[0:n, u % 2, :], bank[u % 2][0:n, :], ACT.Silu).then_inc(m["silu_ready"], 1)

                            for u in range(BODY * NF):
                                silu(u)

                @block.vector
                def _(dve):
                    v = nc.vector
                    with dve.Fori(0, E) as e:
                        dve.wait_ge(m["wT_made"], at(e, 1, 1))
                        dve.wait_ge(m["down_ready"], at(e, SUP, 0))
                        dve.wait_ge(m["wT_high"], at(e, 1, 1))
                        v.tensor_tensor(w1T[:, 1, :], bank[6][:, 0:HF], w1T[:, 0, :].bitcast(F32), ALU.subtract)
                        v.tensor_tensor(w3T[:, 1, :], bank[7][:, 0:HF], w3T[:, 0, :].bitcast(F32), ALU.subtract
                                        ).then_inc(m["wT_split"], 1)
                        with dve.Fori(0, SUP // BODY) as sb_:
                            es = e * SUP + sb_ * BODY

                            def hidden(s):
                                for f, (f0, n) in enumerate(FCH):
                                    u = NF * s + f
                                    dve.wait_ge(m["silu_ready"], at(es, NF, u + 1))
                                    dve.wait_ge(m["down_ready"], at(es, 1, max(s - 1, 0)))
                                    v.tensor_tensor(hT[0:n, s % 2, f, :], act1[0:n, u % 2, :], bank[2 + u % 2][0:n, :], ALU.mult
                                                    ).then_inc(m["hid_ready"], 1)

                            def weigh(s):
                                dve.wait_ge(m["down_ready"], at(es, 1, s + 1))
                                for j in range(4):
                                    tile = t_all[:, bass.ds(sb_ * (4 * BODY) + 4 * s + j, 1), :].rearrange("p a q -> p (a q)")
                                    gate = gates[:, bass.ds(sb_ * (4 * BODY) + 4 * s + j, 1), bass.ds(e, 1)].rearrange("p a q -> p (a q)")
                                    last = v.scalar_tensor_tensor(tile, bank[4 + s % 2][:, j * P:(j + 1) * P], gate, tile,
                                                                  ALU.mult, ALU.add)
                                last.then_inc(m["down_drained"], 1)

                            for what, s in ORDER:
                                (hidden if what == "up" else weigh)(s)

        with ExitStack() as fin:
            t_st = fin.enter_context(nc.sbuf_tensor("t_st", [P, NC, P], F32))
            f = {n: sem(n) for n in ("staged", "turned", "drained_scalar", "drained_vector")}
            start_at_one(f, ())
            staged, turned = f["staged"], f["turned"]
            drained = [f["drained_scalar"], f["drained_vector"]]
            stored = sem("stored")
            with nc.Block() as block:
                @block.gpsimd
                def _(pool):
                    with pool.Fori(0, B) as b:
                        pool.wait_ge(turned, at(b, 2, 0))
                        nc.gpsimd.tensor_copy(t_st[:, :, :], t_all[:, bass.ds(b * NC, NC), :]).then_inc(staged, 1)

                @block.tensor
                def _(pe):
                    with pe.Fori(0, B) as b:
                        pe.wait_ge(staged, at(b, 1, 1))
                        for hf in range(2):
                            pe.wait_ge(drained[hf], at(b, 1, 0))
                            for j in range(4):
                                last = nc.tensor.transpose(bank[hf][:, j * P:(j + 1) * P], t_st[:, 4 * hf + j, :], ident[:, :])
                            last.then_inc(turned, 1)

                @block.scalar
                def _(act):
                    with act.Fori(0, B) as b:
                        act.wait_ge(turned, at(b, 2, 1))
                        nc.scalar.activation(xT_all[:, bass.ds(b * NC, 4), :],
                                             bank[0][:, :].rearrange("p (j q) -> p j q", q=P), ACT.Copy).then_inc(drained[0], 1)

                @block.vector
                def _(dve):
                    with dve.Fori(0, B) as b:
                        dve.wait_ge(turned, at(b, 2, 2))
                        nc.vector.tensor_copy(xT_all[:, bass.ds(b * NC + 4, 4), :],
                                              bank[1][:, :].rearrange("p (j q) -> p j q", q=P)).then_inc(drained[1], 1)

                @block.sync
                def _(sp):
                    with sp.Fori(0, B) as b:
                        sp.wait_ge(drained[0], at(b, 1, 1))
                        sp.wait_ge(drained[1], at(b, 1, 1))
                        sp.dma_start(out[bass.ds(b, 1)].rearrange("b c h w -> c b (h w)"),
                                     xT_all[:, bass.ds(b * NC, NC), :].rearrange("p (a j) q -> p a (j q)", a=1)).then_inc(stored, 16)
                    sp.wait_ge(stored, B * 16)


_INS = ["x", "L0_conv_ln_w", "L0_conv_ln_b", "L0_conv_in_proj_w", "L0_conv_conv_w", "L0_conv_conv_b", "L0_conv_A_log",
        "L0_conv_D", "L0_conv_dt_bias", "L0_conv_rms_w", "L0_conv_out_proj_w", "L1_attn_Wk", "L1_attn_Wq", "L1_attn_Wv",
        "L1_attn_Wu", "L1_attn_bu", "L1_ffn_router_w", "L1_ffn_w1", "L1_ffn_w2", "L1_ffn_w3"]


def kernel(**inputs):
    import numpy as _np
    import concourse.bacc as _bacc
    from concourse import mybir as _mybir
    from concourse.bass_utils import run_bass_kernel_spmd as _run

    nc = _bacc.Bacc("TRN2", target_bir_lowering=False, num_devices=1)
    arrays, args = {}, []
    for name in _INS:
        a = _np.ascontiguousarray(inputs[name])
        arrays[f"in_{name}"] = a
        args.append(nc.dram_tensor(f"in_{name}", a.shape, _mybir.dt.from_np(a.dtype), kind="ExternalInput").ap())
    shape = inputs["x"].shape
    args.append(nc.dram_tensor("out_0", shape, _mybir.dt.float32, kind="ExternalOutput").ap())
    hybrid_kernel(nc, *args)
    r = _run(nc, [arrays], core_ids=[0])
    return r.results[0]["out_0"]
```
